# Optimizing a Trainium2 kernel written in Bass

```python
import numpy as np
import jax
import jax.numpy as jnp

def _softmax(x, axis=-1):
    return jax.nn.softmax(x, axis=axis)

def _gelu(x):
    return jax.nn.gelu(x, approximate=True)

def _silu(x):
    return jax.nn.silu(x)

def _sigmoid(x):
    return jax.nn.sigmoid(x)

def _layernorm(x, axis=-1, eps=1e-05):
    m = jnp.mean(x, axis=axis, keepdims=True)
    v = jnp.var(x, axis=axis, keepdims=True)
    return (x - m) / jnp.sqrt(v + eps)

def _scatter_add(tgt, idx, src, axis=0):
    return tgt.at[idx].add(src)

def _segment_sum(src, seg, n):
    return jax.ops.segment_sum(src, seg, n)
kernel_name = 'mk_gnn_ffn_d2_gnn_r8_8d4dd6'

def setup_inputs(seed: int=0):
    np.random.seed(seed)
    _w = jnp.asarray

    def _rec_inputs():
        import jax
        import jax.numpy as jnp
        _gk = jax.random.key(seed)
        x = -0.0003713 + 1 * jax.random.normal(jax.random.fold_in(_gk, 1), (6250, 256), jnp.float32)
        _s = jax.random.randint(jax.random.fold_in(_gk, 2), (100000,), 0, 6250, jnp.int32)
        _d = jax.random.randint(jax.random.fold_in(_gk, 3), (100000,), 0, 6250, jnp.int32)
        _loop = jnp.arange(6250, dtype=jnp.int32)
        src = jnp.concatenate([_s, _d, _loop])
        dst = jnp.concatenate([_d, _s, _loop])
        _o = jnp.argsort(dst, stable=True)
        src = src[_o]
        dst = dst[_o]
        edge_attr_3 = -1.09012e-05 + 0.99985 * jax.random.normal(jax.random.fold_in(_gk, 11), (206250, 3), jnp.float32)
        return (x, src, dst, edge_attr_3)
    x, src, dst, edge_attr_3 = _rec_inputs()

    def _L0_gnn_setup():
        import jax, jax.numpy as jnp
        import numpy as np
        N = 6250
        E = 50000
        IN = 256
        H = 8
        D = 32
        EF = 3
        key = jax.random.key(seed)
        ks = jax.random.split(key, 8)
        x = jax.random.normal(ks[0], (N, IN), dtype=jnp.float32)
        edge_index = jax.random.randint(ks[1], (2, E), 0, N, dtype=jnp.int64)
        edge_attr = jax.random.normal(ks[2], (E, EF), dtype=jnp.float32)
        W = jax.random.normal(ks[3], (H * D, IN), dtype=jnp.float32) * np.float32(np.sqrt(2.0 / (IN + H * D)))
        a_src = jax.random.normal(ks[4], (H, D), dtype=jnp.float32) * np.float32(np.sqrt(2.0 / (H + D)))
        a_dst = jax.random.normal(ks[5], (H, D), dtype=jnp.float32) * np.float32(np.sqrt(2.0 / (H + D)))
        edge_W = jax.random.normal(ks[6], (H * D, EF), dtype=jnp.float32) * np.float32(np.sqrt(2.0 / (EF + H * D)))
        edge_b = jnp.zeros((H * D,), dtype=jnp.float32)
        bias = jnp.zeros((H * D,), dtype=jnp.float32)
        return {'x': x, 'W': W, 'a_src': a_src, 'a_dst': a_dst, 'edge_W': edge_W, 'edge_b': edge_b, 'bias': bias, 'edge_attr': edge_attr, 'edge_index': edge_index}
    _L0_gnn_all = _L0_gnn_setup()
    _L0_gnn_in = {k: v for k, v in _L0_gnn_all.items() if k in ('W', 'a_src', 'a_dst', 'edge_W', 'edge_b', 'bias')}
    del _L0_gnn_all

    def _L0_ffn_setup():
        import jax, jax.numpy as jnp
        import numpy as np
        TOP_K = 2
        LN_EPS = 1e-05
        key = jax.random.key(seed)
        ks = jax.random.split(key, 8)
        B, S, D, E, H = (16, 1024, 256, 8, 1024)
        x = jax.random.normal(ks[0], (B, S, D), dtype=jnp.float32)
        Wr = jax.random.normal(ks[1], (D, E), dtype=jnp.float32) * 0.1
        br = jnp.zeros((E,), dtype=jnp.float32)
        ln_g = jnp.ones((E, D), dtype=jnp.float32)
        ln_b = jnp.zeros((E, D), dtype=jnp.float32)
        W1 = jax.random.normal(ks[2], (E, D, H), dtype=jnp.float32) * (1.0 / np.sqrt(D))
        b1 = jnp.zeros((E, H), dtype=jnp.float32)
        W2 = jax.random.normal(ks[3], (E, H, D), dtype=jnp.float32) * (1.0 / np.sqrt(H))
        b2 = jnp.zeros((E, D), dtype=jnp.float32)
        return {'x': x, 'Wr': Wr, 'br': br, 'ln_g': ln_g, 'ln_b': ln_b, 'W1': W1, 'b1': b1, 'W2': W2, 'b2': b2}
    _L0_ffn_all = _L0_ffn_setup()
    _L0_ffn_in = {k: v for k, v in _L0_ffn_all.items() if k in ('Wr', 'br', 'ln_g', 'ln_b', 'W1', 'b1', 'W2', 'b2')}
    del _L0_ffn_all

    def _L1_gnn_setup():
        import jax, jax.numpy as jnp
        import numpy as np
        N = 6250
        E = 100000
        IN_C = 256
        HEADS = 8
        OUT_C = 32
        NEG_SLOPE = 0.2
        key = jax.random.key(seed)
        k1, k2, k3, k4, k5 = jax.random.split(key, 5)
        x = jax.random.normal(k1, (N, IN_C), dtype=jnp.float32)
        edge_index = jax.random.randint(k2, (2, E), 0, N, dtype=jnp.int64)
        W = jax.random.normal(k3, (IN_C, HEADS * OUT_C), dtype=jnp.float32) * (1.0 / np.sqrt(IN_C))
        attn_l = jax.random.normal(k4, (1, HEADS, OUT_C), dtype=jnp.float32) * 0.1
        attn_r = jax.random.normal(k5, (1, HEADS, OUT_C), dtype=jnp.float32) * 0.1
        bias = jnp.zeros((HEADS * OUT_C,), dtype=jnp.float32)
        return {'x': x, 'edge_index': edge_index, 'W': W, 'attn_l': attn_l, 'attn_r': attn_r, 'bias': bias}
    _L1_gnn_all = _L1_gnn_setup()
    _L1_gnn_in = {k: v for k, v in _L1_gnn_all.items() if k in ('W', 'attn_l', 'attn_r', 'bias')}
    del _L1_gnn_all

    def _L1_ffn_setup():
        import math
        import jax, jax.numpy as jnp
        import numpy as np
        CAPACITY_FACTOR = 1.25
        key = jax.random.key(seed)
        ks = jax.random.split(key, 5)
        B, L, D, F, E = (8, 1024, 256, 1024, 8)
        h = jax.random.normal(ks[0], (B, L, D), dtype=jnp.float32)
        gate_w = jax.random.normal(ks[1], (D, E), dtype=jnp.float32) * 0.02
        gate_b = jnp.zeros((E,), dtype=jnp.float32)
        w1 = jax.random.normal(ks[2], (E, D, F), dtype=jnp.float32) * (1.0 / math.sqrt(D))
        b1 = jnp.zeros((E, F), dtype=jnp.float32)
        w2 = jax.random.normal(ks[3], (E, F, D), dtype=jnp.float32) * (1.0 / math.sqrt(F))
        b2 = jnp.zeros((E, D), dtype=jnp.float32)
        return {'h': h, 'gate_w': gate_w, 'gate_b': gate_b, 'w1': w1, 'b1': b1, 'w2': w2, 'b2': b2}
    _L1_ffn_all = _L1_ffn_setup()
    _L1_ffn_in = {k: v for k, v in _L1_ffn_all.items() if k in ('gate_w', 'gate_b', 'w1', 'b1', 'w2', 'b2')}
    del _L1_ffn_all
    return {'x': x, 'src': src, 'dst': dst, 'edge_attr_3': edge_attr_3, 'L0_gnn_W': _L0_gnn_in['W'], 'L0_gnn_a_src': _L0_gnn_in['a_src'], 'L0_gnn_a_dst': _L0_gnn_in['a_dst'], 'L0_gnn_edge_W': _L0_gnn_in['edge_W'], 'L0_gnn_edge_b': _L0_gnn_in['edge_b'], 'L0_gnn_bias': _L0_gnn_in['bias'], 'L0_ffn_Wr': _L0_ffn_in['Wr'], 'L0_ffn_br': _L0_ffn_in['br'], 'L0_ffn_ln_g': _L0_ffn_in['ln_g'], 'L0_ffn_ln_b': _L0_ffn_in['ln_b'], 'L0_ffn_W1': _L0_ffn_in['W1'], 'L0_ffn_b1': _L0_ffn_in['b1'], 'L0_ffn_W2': _L0_ffn_in['W2'], 'L0_ffn_b2': _L0_ffn_in['b2'], 'L1_gnn_W': _L1_gnn_in['W'], 'L1_gnn_attn_l': _L1_gnn_in['attn_l'], 'L1_gnn_attn_r': _L1_gnn_in['attn_r'], 'L1_gnn_bias': _L1_gnn_in['bias'], 'L1_ffn_gate_w': _L1_ffn_in['gate_w'], 'L1_ffn_gate_b': _L1_ffn_in['gate_b'], 'L1_ffn_w1': _L1_ffn_in['w1'], 'L1_ffn_b1': _L1_ffn_in['b1'], 'L1_ffn_w2': _L1_ffn_in['w2'], 'L1_ffn_b2': _L1_ffn_in['b2']}

def reference(x, src, dst, edge_attr_3, L0_gnn_W, L0_gnn_a_src, L0_gnn_a_dst, L0_gnn_edge_W, L0_gnn_edge_b, L0_gnn_bias, L0_ffn_Wr, L0_ffn_br, L0_ffn_ln_g, L0_ffn_ln_b, L0_ffn_W1, L0_ffn_b1, L0_ffn_W2, L0_ffn_b2, L1_gnn_W, L1_gnn_attn_l, L1_gnn_attn_r, L1_gnn_bias, L1_ffn_gate_w, L1_ffn_gate_b, L1_ffn_w1, L1_ffn_b1, L1_ffn_w2, L1_ffn_b2):
    import jax
    import jax.numpy as jnp

    def _L0_gnn_ref(x, W, a_src, a_dst, edge_W, edge_b, bias, edge_attr, edge_index):
        import jax, jax.numpy as jnp
        import numpy as np
        N = 6250
        E = 50000
        IN = 256
        H = 8
        D = 32
        EF = 3
        n = x.shape[0]
        h = (x @ W.T).reshape(n, H, D)
        src, dst = (edge_index[0], edge_index[1])
        h_src = h[src]
        h_dst = h[dst]
        alpha = jnp.einsum('ehd,hd->eh', h_src, a_src) + jnp.einsum('ehd,hd->eh', h_dst, a_dst)
        enc = jax.nn.relu(edge_attr @ edge_W.T + edge_b).reshape(-1, H, D)
        alpha = alpha + jnp.sum(enc * h_dst, axis=-1)
        alpha = jnp.where(alpha >= 0, alpha, 0.2 * alpha)
        amax = jax.ops.segment_max(alpha, dst, num_segments=n)
        ex = jnp.exp(alpha - amax[dst])
        denom = jax.ops.segment_sum(ex, dst, num_segments=n)
        attn = ex / jnp.maximum(denom[dst], 1e-10)
        out = jax.ops.segment_sum(h_src * attn[..., None], dst, num_segments=n)
        return out.reshape(n, H * D) + bias

    def _L0_ffn_ref(x, Wr, br, ln_g, ln_b, W1, b1, W2, b2):
        import jax, jax.numpy as jnp
        import numpy as np
        TOP_K = 2
        LN_EPS = 1e-05
        B, S, D = x.shape
        N = B * S
        xt = x.reshape(N, D)
        logits = xt @ Wr + br
        probs = jax.nn.softmax(logits, axis=-1)
        top_p, top_idx = jax.lax.top_k(probs, TOP_K)
        weights = top_p / top_p.sum(axis=-1, keepdims=True)
        mu = xt.mean(axis=-1, keepdims=True)
        var = ((xt - mu) ** 2).mean(axis=-1, keepdims=True)
        xn = (xt - mu) * jax.lax.rsqrt(var + LN_EPS)
        xe = xn[None, :, :] * ln_g[:, None, :] + ln_b[:, None, :]
        h = jax.nn.gelu(jnp.einsum('end,edh->enh', xe, W1) + b1[:, None, :], approximate=False)
        y = jnp.einsum('enh,ehd->end', h, W2) + b2[:, None, :]
        y_tok = jnp.transpose(y, (1, 0, 2))
        sel = jnp.take_along_axis(y_tok, top_idx[:, :, None], axis=1)
        out = (weights[:, :, None] * sel).sum(axis=1)
        return out.reshape(B, S, D)

    def _L1_gnn_ref(x, edge_index, W, attn_l, attn_r, bias):
        import jax, jax.numpy as jnp
        import numpy as np
        N = 6250
        E = 100000
        IN_C = 256
        HEADS = 8
        OUT_C = 32
        NEG_SLOPE = 0.2
        n = x.shape[0]
        h = (x @ W).reshape(n, HEADS, OUT_C)
        a1 = jnp.sum(h * attn_l, axis=-1)
        a2 = jnp.sum(h * attn_r, axis=-1)
        src, dst = (edge_index[0], edge_index[1])
        e = a1[src] + a2[dst]
        e = jax.nn.leaky_relu(e, negative_slope=NEG_SLOPE)
        seg_max = jax.ops.segment_max(e, dst, num_segments=n)
        seg_max = jnp.where(jnp.isfinite(seg_max), seg_max, 0.0)
        ex = jnp.exp(e - seg_max[dst])
        denom = jax.ops.segment_sum(ex, dst, num_segments=n)
        alpha = ex / denom[dst]
        message = h[src] * alpha[:, :, None]
        out = jax.ops.segment_sum(message, dst, num_segments=n)
        out = out.reshape(n, HEADS * OUT_C)
        return out + bias

    def _L1_ffn_ref(h, gate_w, gate_b, w1, b1, w2, b2):
        import math
        import jax, jax.numpy as jnp
        import numpy as np
        CAPACITY_FACTOR = 1.25
        B, L, D = h.shape
        E = gate_w.shape[1]
        T = B * L
        C = max(1, math.ceil(CAPACITY_FACTOR * T / E))
        x = h.reshape(T, D)
        logits = x @ gate_w + gate_b
        probs = jax.nn.softmax(logits, axis=-1)
        idx = jnp.argmax(probs, axis=-1)
        prb = jnp.take_along_axis(probs, idx[:, None], axis=1)[:, 0]
        one_hot = jax.nn.one_hot(idx, E, dtype=jnp.float32)
        pos = (jnp.cumsum(one_hot, axis=0) * one_hot).sum(-1).astype(jnp.int32) - 1
        kept = pos < C
        pos_safe = jnp.where(kept, pos, C)
        buf = jnp.zeros((E, C, D), dtype=h.dtype).at[idx, pos_safe].set(x, mode='drop')
        hmid = jax.nn.relu(jnp.einsum('ecd,edf->ecf', buf, w1) + b1[:, None, :])
        ybuf = jnp.einsum('ecf,efd->ecd', hmid, w2) + b2[:, None, :]
        pos_g = jnp.minimum(pos, C - 1)
        y_tok = ybuf[idx, pos_g] * (prb * kept)[:, None]
        y = y_tok.reshape(B, L, D)
        y = jnp.nan_to_num(y, nan=0.0, posinf=10000.0, neginf=-10000.0)
        return y
    edge_index = jnp.stack([src, dst])
    x = x + _L0_gnn_ref(_layernorm(x, axis=-1), L0_gnn_W, L0_gnn_a_src, L0_gnn_a_dst, L0_gnn_edge_W, L0_gnn_edge_b, L0_gnn_bias, edge_attr_3, edge_index)
    x = x + _L0_ffn_ref(_layernorm(x, axis=-1)[None], L0_ffn_Wr, L0_ffn_br, L0_ffn_ln_g, L0_ffn_ln_b, L0_ffn_W1, L0_ffn_b1, L0_ffn_W2, L0_ffn_b2)[0]
    x = x + _L1_gnn_ref(_layernorm(x, axis=-1), edge_index, L1_gnn_W, L1_gnn_attn_l, L1_gnn_attn_r, L1_gnn_bias)
    x = x + _L1_ffn_ref(_layernorm(x, axis=-1)[None], L1_ffn_gate_w, L1_ffn_gate_b, L1_ffn_w1, L1_ffn_b1, L1_ffn_w2, L1_ffn_b2)[0]
    return x

_drawn_inputs = setup_inputs


def setup_inputs(seed=0):
    import zlib

    import numpy as np

    out = dict(_drawn_inputs(seed))
    spreads = {'L0_gnn_edge_b': (0.0, 0.1),
     'L0_gnn_bias': (0.0, 0.1),
     'L0_ffn_br': (0.0, 0.1),
     'L0_ffn_ln_g': (1.0, 0.2),
     'L0_ffn_ln_b': (0.0, 0.1),
     'L0_ffn_b1': (0.0, 0.1),
     'L0_ffn_b2': (0.0, 0.1),
     'L1_gnn_bias': (0.0, 0.1),
     'L1_ffn_gate_b': (0.0, 0.1),
     'L1_ffn_b1': (0.0, 0.8),
     'L1_ffn_b2': (0.0, 0.572)}
    factors = {}
    for name, (base, spread) in spreads.items():
        noise = np.random.default_rng([zlib.crc32(name.encode()), seed]).standard_normal(out[name].shape)
        drawn = base * np.exp(spread * noise) if base else spread * noise
        out[name] = jnp.asarray(drawn.astype(out[name].dtype))
    for name, factor in factors.items():
        out[name] = (out[name] * factor).astype(out[name].dtype)
    return out
```

```python
from contextlib import ExitStack

import numpy as np
import concourse.bass as bass
from concourse import mybir

F32 = mybir.dt.float32
BF16 = mybir.dt.bfloat16
I32 = mybir.dt.int32
ALU = mybir.AluOpType
ACT = mybir.ActivationFunctionType
AX_X = mybir.AxisListType.X

P = 128
N, D, E = 6250, 256, 206250
HEADS, DH = 8, 32
NT = -(-N // P)
NP = NT * P
EC = -(-E // P)
E_LAST = E - (P - 1) * EC
WIN = P // HEADS
NW = -(-N // WIN)
WT = -(-(NW + 1) // P)
CH = 5
BE = CH * P
HB = BE // 2
UN = 4
TAIL = BE * (UN + 6)
EP = P * EC + TAIL
MAXB = NW * (-(-E // BE)) + P * 2
MAXB = -(-MAXB // P) * P
PAD_DST = 100000
MASKED = -1.0e30
FLOOR = -1.0e20
EPS = 1e-5
ROW = D + HEADS
PAIRS = 9
K_ENC = PAIRS * 4


def semaphores(nc, ctx, prefix):
    taken = []

    def retire():
        nc.clear_and_free_semaphores(taken)
        nc.all_engine_barrier()

    def sem(name):
        taken.append(nc.alloc_semaphore(prefix + name))
        return taken[-1]

    ctx.callback(retire)
    return sem


def hold(eng, sem, value, passed):
    eng.wait_ge(sem, value)
    eng.sem_inc(passed, 1)


def plan_phase(nc, io, dr):
    with ExitStack() as ctx:
        sb = lambda n, s, d: ctx.enter_context(nc.sbuf_tensor("pl_" + n, s, d))
        ps = lambda n, s: ctx.enter_context(nc.psum_tensor("pl_" + n, s, F32))
        sem = semaphores(nc, ctx, "pl_")
        dst_i = sb("dst_i", [P, EC], I32)
        src_i = sb("src_i", [P, EC], I32)
        dst_f = sb("dst_f", [P, EC], F32)
        pmax = sb("pmax", [P, EC], F32)
        smin = sb("smin", [P, EC], F32)
        attr = sb("attr", [P, EC, 3], F32)
        rest = sb("rest", [P, 3, EC], F32)
        part = sb("part", [P, 3, 3, EC], BF16)
        ones = sb("ones", [P, 2, EC], BF16)
        tail_i = sb("tail_i", [2, TAIL], I32)
        tail_b = sb("tail_b", [12, TAIL], BF16)
        ident = sb("ident", [P, P], F32)
        upper = sb("upper", [P, P], F32)
        allone = sb("allone", [P, P], F32)
        ends = sb("ends", [P, 4], F32)
        erow = sb("erow", [1, 4, P + 1], F32)
        bnd = sb("bnd", [P, 2, P], F32)
        thr = sb("thr", [P, 2, WT], F32)
        cnt = sb("cnt", [P, 2, WT], F32)
        rix = sb("rix", [P, 2, WT], I32)
        rows = sb("rows", [P, 2, EC], F32)
        junk = sb("junk", [P, EC], F32)
        lohi = sb("lohi", [P, 2, WT], F32)
        nb = sb("nb", [P, 4, WT], F32)
        valid = sb("valid", [P, WT], F32)
        cum = sb("cum", [P, WT], F32)
        off = sb("off", [P, WT], F32)
        win = sb("win", [P, WT, 2], F32)
        cumrow = sb("cumrow", [P, WT * P], F32)
        bcol = sb("bcol", [P, 1], F32)
        bw = sb("bw", [P, 6], F32)
        bwi = sb("bwi", [P, 2], I32)
        wi = sb("wi", [P, 1], I32)
        winb = sb("winb", [P, 2], F32)
        nbf = sb("nbf", [1, 4], F32)
        nbi = sb("nbi", [1, 4], I32)
        pt = ps("pt", [P, 512])
        pb = ps("pb", [P, 512])
        pc = ps("pc", [P, 512])
        s_in, s_attr, s_pad, s_const, s_pe, s_tab = (sem(n) for n in ("in", "attr", "pad", "const", "pe", "tab"))
        s_out, s_row, s_wq, s_wg, s_bt = (sem(n) for n in ("out", "row", "wq", "wg", "bt"))
        s_pass = sem("pass")
        s_win, s_go, s_cp, s_step, s_chain, s_tile = (sem(n) for n in ("win", "go", "cp", "step", "chain", "tile"))
        s_ends, s_scan, s_final, s_parts, s_nb, s_cum, s_blk = (sem(n) for n in ("ends", "scan", "final", "parts", "nb", "cum", "blk"))

        block = ctx.enter_context(nc.Block())

        @block.gpsimd
        def _(pool):
            nc.gpsimd.memset(ident[:, :], 0.0).then_inc(s_const, 1)
            nc.gpsimd.memset(upper[:, :], 1.0).then_inc(s_const, 1)
            nc.gpsimd.memset(allone[:, :], 1.0).then_inc(s_const, 1)
            pool.wait_ge(s_const, 3)
            nc.gpsimd.affine_select(out=ident[:, :], in_=ident[:, :], compare_op=ALU.not_equal, fill=1.0, base=0,
                                    pattern=[[-1, P]], channel_multiplier=1).then_inc(s_const, 1)
            nc.gpsimd.affine_select(out=upper[:, :], in_=upper[:, :], compare_op=ALU.is_ge, fill=0.0, base=0,
                                    pattern=[[1, P]], channel_multiplier=-1).then_inc(s_const, 1)
            nc.gpsimd.iota(bcol[:, :], pattern=[[0, 1]], base=0, channel_multiplier=1,
                           allow_small_or_imprecise_dtypes=True).then_inc(s_const, 1)
            for s in range(2):
                nc.gpsimd.iota(thr[:, s, :], pattern=[[WIN * P, WT]], base=WIN * s, channel_multiplier=WIN,
                               allow_small_or_imprecise_dtypes=True).then_inc(s_const, 1)
            pool.wait_ge(s_row, 1)
            pool.wait_ge(s_out, 32)
            for s in range(2):
                for t in range(WT):
                    k = s * WT + t
                    if k:
                        pool.wait_ge(s_cp, k)
                    pool.indirect_dma_start(rows[:, 0, :], None, (dr["pmax"] if s == 0 else dr["smin"])[:, :],
                                            bass.IndirectOffsetOnAxis(rix[:, s, t:t + 1], 0)).then_inc(s_wg, 16)
                    pool.wait_ge(s_wg, 16 * (k + 1))
            pool.wait_ge(s_win, 16)
            pool.wait_ge(s_step, 1)
            tiles = pool.value_load(nbi[0:1, 1:2], min_val=1, max_val=MAXB // P)
            with pool.Fori(0, tiles) as u:
                hold(pool, s_bt, u * 2 + 1, s_go)
                pool.indirect_dma_start(winb[:, :], None, dr["win"][:, :],
                                        bass.IndirectOffsetOnAxis(wi[:, 0:1], 0)).then_inc(s_wq, 16)

        @block.sync
        def _(sp):
            for tile, name, pad in ((dst_i, "dst", s_pad), (src_i, "src", s_pad)):
                sp.wait_ge(s_pad, 3)
                v = io[name]
                sp.dma_start(tile[0:P - 1, :], v[0:(P - 1) * EC].rearrange("(p e) -> p e", p=P - 1)).then_inc(s_in, 16)
                sp.dma_start(tile[P - 1:P, 0:E_LAST], v[(P - 1) * EC:E].rearrange("(p e) -> p e", p=1)).then_inc(s_in, 16)
            v = io["edge_attr_3"]
            sp.dma_start(attr[0:P - 1, :, :], v[0:(P - 1) * EC, :].rearrange("(p e) c -> p e c", p=P - 1)).then_inc(s_attr, 16)
            sp.dma_start(attr[P - 1:P, 0:E_LAST, :], v[(P - 1) * EC:E, :].rearrange("(p e) c -> p e c", p=1)).then_inc(s_attr, 16)
            sp.wait_ge(s_in, 64)
            sp.wait_ge(s_pad, 6)
            for tile, name, r in ((dst_i, "dstp", 0), (src_i, "srcp", 1)):
                sp.dma_start(dr[name][0:P * EC].rearrange("(p e) -> p e", p=P), tile[:, :]).then_inc(s_tab, 16)
                sp.dma_start(dr[name][P * EC:EP].rearrange("(p e) -> p e", p=1), tail_i[0:1, :]).then_inc(s_tab, 16)
            sp.wait_ge(s_final, 1)
            sp.dma_start(dr["pmax"][:, :], pmax[:, :]).then_inc(s_out, 16)
            sp.dma_start(dr["smin"][:, :], smin[:, :]).then_inc(s_out, 16)
            sp.wait_ge(s_step, 1)
            sp.dma_start(dr["win"].rearrange("(t p) c -> p t c", p=P), win[:, :, :]).then_inc(s_win, 16)
            sp.dma_start(dr["nblk"][:, :], nbi[0:1, :]).then_inc(s_tab, 16)
            sp.wait_ge(s_parts, 1)
            for k in range(3):
                for i in range(3):
                    for c in range(3):
                        sp.dma_start(dr["attrp"][12 * k + 4 * i + c, 0:P * EC].rearrange("(p e) -> p e", p=P),
                                     part[:, i, c, :]).then_inc(s_tab, 16)
                    sp.dma_start(dr["attrp"][12 * k + 4 * i + 3, 0:P * EC].rearrange("(p e) -> p e", p=P),
                                 ones[:, 0 if i == 0 else 1, :]).then_inc(s_tab, 16)
                sp.dma_start(dr["attrp"][12 * k:12 * k + 12, P * EC:EP], tail_b[:, :]).then_inc(s_tab, 16)
            sp.wait_ge(s_tab, 16 * (5 + 39))
            tiles = sp.value_load(nbi[0:1, 1:2], min_val=1, max_val=MAXB // P)
            with sp.Fori(0, tiles) as u:
                hold(sp, s_bt, u * 2 + 2, s_pass)
                sp.dma_start(dr["blk"][bass.ds(u * P, P), :], bwi[:, :]).then_inc(s_row, 16)
                sp.dma_start(dr["blkf"][bass.ds(u * P, P), :], bw[:, 5:6]).then_inc(s_row, 16)
                sp.wait_ge(s_row, u * 32 + 33)
                sp.sem_inc(s_blk, 1)

        @block.tensor
        def _(pe):
            pe.wait_ge(s_const, 8)
            pe.wait_ge(s_ends, 1)
            nc.tensor.transpose(pt[0:1, 0:P], ends[:, 0:1], ident[:, :])
            nc.tensor.transpose(pt[0:1, P:2 * P], ends[:, 1:2], ident[:, :]).then_inc(s_pe, 1)
            pe.wait_ge(s_scan, 1)
            nc.tensor.matmul(pb[:, 0:1], erow[0:1, 2, 0:P], allone[0:1, 0:1], start=True, stop=True)
            nc.tensor.matmul(pb[:, 1:2], erow[0:1, 3, 0:P], allone[0:1, 0:1], start=True, stop=True).then_inc(s_pe, 1)
            pe.wait_ge(s_final, 1)
            nc.tensor.matmul(pc[:, 0:P], ends[:, 2:3].to_broadcast([P, P]), ident[:, :], start=True, stop=True)
            nc.tensor.matmul(pc[:, P:2 * P], ends[:, 3:4].to_broadcast([P, P]), ident[:, :], start=True, stop=True).then_inc(s_pe, 1)
            pe.wait_ge(s_nb, 1)
            nc.tensor.matmul(pt[:, 0:WT], upper[:, :], nb[:, 3, :], start=True, stop=True)
            nc.tensor.matmul(pt[:, 8:8 + WT], allone[:, :], nb[:, 3, :], start=True, stop=True).then_inc(s_pe, 1)
            pe.wait_ge(s_cum, 1)
            for t in range(WT):
                mm = nc.tensor.matmul(pb[:, t * P:(t + 1) * P], cum[:, t:t + 1].to_broadcast([P, P]), ident[:, :],
                                      start=True, stop=True)
            mm.then_inc(s_pe, 1)

        @block.vector
        def _(v):
            steps = [0]

            def done(ins):
                steps[0] += 1
                ins.then_inc(s_chain, 1)
                v.wait_ge(s_chain, steps[0])

            nc.vector.memset(dst_i[:, :], PAD_DST).then_inc(s_pad, 1)
            nc.vector.memset(src_i[:, :], 0).then_inc(s_pad, 1)
            nc.vector.memset(attr[:, :, :], 0.0).then_inc(s_pad, 1)
            nc.vector.memset(tail_i[:, :], 0).then_inc(s_pad, 1)
            nc.vector.memset(tail_b[:, :], 0.0).then_inc(s_pad, 1)
            nc.vector.memset(ones[:, 0, :], 1.0).then_inc(s_pad, 1)
            done(nc.vector.memset(ones[:, 1, :], 0.0))
            v.wait_ge(s_in, 64)
            done(nc.vector.tensor_copy(dst_f[:, :], dst_i[:, :]))
            done(nc.vector.tensor_tensor_scan(pmax[:, :], dst_f[:, :], dst_f[:, :], -1.0, ALU.max, ALU.max))
            done(nc.vector.tensor_tensor_scan(smin[:, ::-1], dst_f[:, ::-1], dst_f[:, ::-1], float(PAD_DST), ALU.min, ALU.min))
            done(nc.vector.tensor_copy(ends[:, 0:1], pmax[:, EC - 1:EC]))
            nc.vector.tensor_copy(ends[:, 1:2], smin[:, 0:1]).then_inc(s_ends, 1)
            v.wait_ge(s_pe, 1)
            done(nc.vector.memset(erow[:, :, :], -1.0))
            done(nc.vector.memset(erow[0:1, 3, :], float(PAD_DST)))
            done(nc.vector.tensor_copy(erow[0:1, 0, 0:P], pt[0:1, 0:P]))
            done(nc.vector.tensor_copy(erow[0:1, 1, 0:P], pt[0:1, P:2 * P]))
            done(nc.vector.tensor_tensor_scan(erow[0:1, 2, 1:P + 1], erow[0:1, 0, 0:P], erow[0:1, 0, 0:P], -1.0, ALU.max, ALU.max))
            nc.vector.tensor_tensor_scan(erow[0:1, 3, P - 2::-1], erow[0:1, 1, P - 1:0:-1], erow[0:1, 1, P - 1:0:-1],
                                         float(PAD_DST), ALU.min, ALU.min).then_inc(s_scan, 1)
            v.wait_ge(s_pe, 2)
            done(nc.vector.tensor_copy(bw[:, 0:2], pb[:, 0:2]))
            done(nc.vector.tensor_scalar(pmax[:, :], pmax[:, :], bw[:, 0:1], None, ALU.max))
            done(nc.vector.tensor_scalar(smin[:, :], smin[:, :], bw[:, 1:2], None, ALU.min))
            done(nc.vector.tensor_copy(ends[:, 2:3], pmax[:, EC - 1:EC]))
            nc.vector.tensor_copy(ends[:, 3:4], smin[:, EC - 1:EC]).then_inc(s_final, 1)
            v.wait_ge(s_pe, 3)
            v.wait_ge(s_const, 8)
            done(nc.vector.tensor_copy(bnd[:, 0, :], pc[:, 0:P]))
            done(nc.vector.tensor_copy(bnd[:, 1, :], pc[:, P:2 * P]))
            for s in range(2):
                for t in range(WT):
                    done(nc.vector.tensor_scalar(junk[:, 0:P], bnd[:, s, :], thr[:, s, t:t + 1], 0.0, ALU.is_lt, ALU.add,
                                                 accum_out=cnt[:, s, t:t + 1]))
            done(nc.vector.tensor_scalar(cnt[:, :, :], cnt[:, :, :], float(P - 1), None, ALU.min))
            nc.vector.tensor_copy(rix[:, :, :], cnt[:, :, :]).then_inc(s_row, 1)
            for s in range(2):
                for t in range(WT):
                    v.wait_ge(s_wg, 16 * (s * WT + t + 1))
                    nc.vector.tensor_scalar(junk[:, :], rows[:, 0, :], thr[:, s, t:t + 1], 0.0, ALU.is_lt, ALU.add,
                                            accum_out=lohi[:, s, t:t + 1]).then_inc(s_cp, 1)
            v.wait_ge(s_cp, 2 * WT)
            done(nc.vector.scalar_tensor_tensor(lohi[:, :, :], cnt[:, :, :], float(EC), lohi[:, :, :], ALU.mult, ALU.add))
            done(nc.vector.tensor_tensor(nb[:, 0, :], lohi[:, 1, :], lohi[:, 0, :], ALU.subtract))
            done(nc.vector.tensor_scalar(nb[:, 1, :], nb[:, 0, :], 1.0 / BE, 0.5 - 0.5 / BE, ALU.mult, ALU.add))
            done(nc.vector.tensor_scalar(nb[:, 2, :], nb[:, 1, :], 8388608.0, None, ALU.add))
            done(nc.vector.tensor_scalar(nb[:, 2, :], nb[:, 2, :], -8388608.0, 1.0, ALU.add, ALU.max))
            done(nc.vector.tensor_scalar(valid[:, :], thr[:, 0, :], float(WIN * NW), None, ALU.is_lt))
            nc.vector.tensor_tensor(nb[:, 3, :], nb[:, 2, :], valid[:, :], ALU.mult).then_inc(s_nb, 1)
            v.wait_ge(s_nb, 1)
            v.wait_ge(s_attr, 32)
            at = attr[:, :, :].rearrange("p e c -> p c e")
            done(nc.vector.tensor_copy(part[:, 0, :, :], at))
            done(nc.vector.tensor_tensor(rest[:, :, :], at, part[:, 0, :, :], ALU.subtract))
            done(nc.vector.tensor_copy(part[:, 1, :, :], rest[:, :, :]))
            done(nc.vector.tensor_tensor(rest[:, :, :], rest[:, :, :], part[:, 1, :, :], ALU.subtract))
            nc.vector.tensor_copy(part[:, 2, :, :], rest[:, :, :]).then_inc(s_parts, 1)
            v.wait_ge(s_pe, 4)
            done(nc.vector.memset(off[:, 0:1], 0.0))
            for t in range(1, WT):
                done(nc.vector.tensor_tensor(off[:, t:t + 1], off[:, t - 1:t], pt[:, 7 + t:8 + t], ALU.add))
            done(nc.vector.tensor_tensor(cum[:, :], off[:, :], pt[:, 0:WT], ALU.add))
            done(nc.vector.tensor_copy(win[:, :, 0], lohi[:, 0, :]))
            done(nc.vector.tensor_tensor(win[:, :, 1], cum[:, :], nb[:, 3, :], ALU.subtract))
            v.sem_inc(s_cum, 1)
            v.wait_ge(s_pe, 5)
            done(nc.vector.tensor_copy(cumrow[:, :], pb[:, 0:WT * P]))
            last = cumrow[0:1, WT * P - 1:WT * P]
            rnd = lambda o, i, m, a: (done(nc.vector.tensor_scalar(o, i, m, a, ALU.mult, ALU.add)),
                                      done(nc.vector.tensor_scalar(o, o, 8388608.0, None, ALU.add)),
                                      done(nc.vector.tensor_scalar(o, o, -8388608.0, None, ALU.add)))
            rnd(nbf[0:1, 0:1], last, 1.0 / UN, 0.5 - 0.5 / UN - 2.0 / UN)
            rnd(nbf[0:1, 1:2], last, 1.0 / P, 0.5 - 0.5 / P + (UN + 5.0) / P)
            done(nc.vector.tensor_copy(nbf[0:1, 2:3], last))
            done(nc.vector.tensor_copy(nbf[0:1, 3:4], last))
            done(nc.vector.tensor_copy(nbi[0:1, :], nbf[0:1, :]))
            v.sem_inc(s_step, 1)
            tiles = v.value_load(nbi[0:1, 1:2], min_val=1, max_val=MAXB // P)
            K = 8
            with v.Fori(0, tiles) as u:
                nc.vector.tensor_scalar(junk[:, 0:WT * P], cumrow[:, :], bcol[:, 0:1], 0.0, ALU.is_le, ALU.add,
                                        accum_out=bw[:, 2:3]).then_inc(s_tile, 1)
                v.wait_ge(s_tile, u * K + 1)
                nc.vector.tensor_scalar(bw[:, 2:3], bw[:, 2:3], float(NW), None, ALU.min).then_inc(s_tile, 1)
                v.wait_ge(s_tile, u * K + 2)
                nc.vector.tensor_copy(wi[:, :], bw[:, 2:3]).then_inc(s_bt, 1)
                v.wait_ge(s_wq, u * 16 + 16)
                nc.vector.tensor_tensor(bw[:, 3:4], bcol[:, 0:1], winb[:, 1:2], ALU.subtract).then_inc(s_tile, 1)
                v.wait_ge(s_tile, u * K + 3)
                nc.vector.scalar_tensor_tensor(bw[:, 4:5], bw[:, 3:4], float(BE), winb[:, 0:1], ALU.mult, ALU.add).then_inc(s_tile, 1)
                nc.vector.tensor_scalar(bw[:, 5:6], bw[:, 3:4], 0.0, MASKED, ALU.is_equal, ALU.mult).then_inc(s_tile, 1)
                nc.vector.tensor_copy(bwi[:, 0:1], bw[:, 2:3]).then_inc(s_tile, 1)
                v.wait_ge(s_tile, u * K + 6)
                nc.vector.tensor_copy(bwi[:, 1:2], bw[:, 4:5]).then_inc(s_tile, 1)
                nc.vector.tensor_scalar(bcol[:, 0:1], bcol[:, 0:1], float(P), None, ALU.add).then_inc(s_tile, 1)
                v.wait_ge(s_tile, u * K + 8)
                v.sem_inc(s_bt, 1)
                v.wait_ge(s_blk, u + 1)


def node_phase(nc, io, dr, layer):
    first = layer == 0
    with ExitStack() as ctx:
        sb = lambda n, s, d: ctx.enter_context(nc.sbuf_tensor(f"n{layer}_" + n, s, d))
        ps = lambda n, s: ctx.enter_context(nc.psum_tensor(f"n{layer}_" + n, s, F32))
        sem = semaphores(nc, ctx, f"n{layer}_")
        U = 7
        xs = sb("xs", [P, NT, D], F32)
        st = sb("st", [P, NT, 6], F32)
        mean = sb("mean", [P, NT], F32)
        var = sb("var", [P, NT], F32)
        dif = sb("dif", [P, NT], F32)
        std = sb("std", [P, NT], F32)
        rstd = sb("rstd", [P, NT], F32)
        w_in = sb("w_in", [P, 2, D], F32)
        w = sb("w", [P, 2, D], F32)
        avec = sb("avec", [P, 2, 2], F32)
        amask = sb("amask", [P, 2, HEADS], F32)
        amat = sb("amat", [P, 2, 2 * HEADS], F32)
        ident = sb("ident", [P, P], F32)
        ncol = sb("ncol", [P, HEADS], F32)
        eps = sb("eps", [P, 1], F32)
        xg = sb("xg", [P, U, D], F32)
        xt = sb("xt", [P, U, 2, P], F32)
        ht = sb("ht", [P, U, 2, P], F32)
        row = sb("row", [P, U, ROW], F32)
        wcol = sb("wcol", [P, U, HEADS, 2], F32)
        ps_x = ps("ps_x", [P, 2, 512])
        ps_h = ps("ps_h", [P, 2, 512])
        ps_t = ps("ps_t", [P, 2, 512])
        ps_a = ps("ps_a", [P, 2, 512])
        s_x = [sem(f"x{c}") for c in range(U)]
        s_w, s_const, s_zero, s_stat, s_var, s_std, s_xn, s_chain = (sem(n) for n in ("w", "const", "zero", "stat", "var", "std", "xn", "chain"))
        s_wt, s_wts, s_amat, s_xt, s_xts, s_h, s_hts, s_hrow, s_a, s_acp, s_pass, s_passp, s_xg, s_pa, s_nc = (
            sem(n) for n in ("wt", "wts", "amat", "xt", "xts", "h", "hts", "hrow", "a", "acp", "pass", "passp", "xg", "pa", "nc"))
        s_st = [sem(f"st{k}") for k in range(U)]
        a_names = ("L0_gnn_a_src", "L0_gnn_a_dst") if first else ("L1_gnn_attn_l", "L1_gnn_attn_r")
        n_st = 16 * (3 if first else 2)
        block = ctx.enter_context(nc.Block())

        @block.sync
        def _(sp):
            sp.dma_start(w_in[:, :, :], io["L0_gnn_W" if first else "L1_gnn_W"].rearrange("(k p) n -> p k n", p=P)).then_inc(s_w, 16)
            with nc.allow_non_contiguous_dma(reason="attention vectors as columns, once"):
                for i, name in enumerate(a_names):
                    v = io[name] if first else io[name][0]
                    sp.dma_start(avec[:, :, i], v.rearrange("(k g) d -> (g d) k", k=2)).then_inc(s_w, 16)
            for c in range(U):
                if first and c == U - 1:
                    sp.wait_ge(s_zero, 1)
                    full = (NT - 1) - c * U
                    sp.dma_start(xs[:, c * U:NT - 1, :], io["x"][c * U * P:(NT - 1) * P, :].rearrange("(t p) d -> p t d", p=P)).then_inc(s_x[c], 16)
                    sp.dma_start(xs[0:N - (NT - 1) * P, NT - 1, :], io["x"][(NT - 1) * P:N, :]).then_inc(s_x[c], 16)
                else:
                    src = io["x"] if first else dr["x2"]
                    sp.dma_start(xs[:, c * U:(c + 1) * U, :],
                                 src[c * U * P:(c + 1) * U * P, :].rearrange("(t p) d -> p t d", p=P)).then_inc(s_x[c], 16)
            for k in range(U):
                sp.sem_inc(s_st[k], 16)
            with sp.Fori(0, NT // U) as i:
                for k in range(U):
                    hold(sp, s_hrow, i * U + (k + 2), s_pass)
                    hold(sp, s_acp, i * U + (k + 2), s_pass)
                    n0 = i * (U * P) + k * P
                    sp.dma_start(dr["table"][bass.ds(n0, P), :], row[:, k, :]).then_inc(s_st[k], 16)
                    sp.dma_start(dr["wcol"][bass.ds(n0, P), :], wcol[:, k, :, :].rearrange("p h c -> p (h c)")).then_inc(s_st[k], 16)
                    if first:
                        hold(sp, s_hts, i * U + (k + 2), s_pass)
                        sp.dma_start(dr["hT"].rearrange("(c p) n -> p c n", p=P)[:, :, bass.ds(n0, P)], ht[:, k, :, :]).then_inc(s_st[k], 16)
            for k in range(U):
                sp.wait_ge(s_st[k], n_st * (NT // U) + 16)

        @block.gpsimd
        def _(pool):
            nc.gpsimd.memset(ident[:, :], 0.0).then_inc(s_const, 1)
            nc.gpsimd.memset(amask[:, :, :], 1.0).then_inc(s_const, 1)
            pool.wait_ge(s_const, 2)
            nc.gpsimd.affine_select(out=ident[:, :], in_=ident[:, :], compare_op=ALU.not_equal, fill=1.0, base=0,
                                    pattern=[[-1, P]], channel_multiplier=1).then_inc(s_const, 1)
            nc.gpsimd.affine_select(out=amask[:, :, :], in_=amask[:, :, :], compare_op=ALU.is_ge, fill=0.0, base=0,
                                    pattern=[[P, 2], [-DH, HEADS]], channel_multiplier=1).then_inc(s_const, 1)
            pool.wait_ge(s_const, 4)
            nc.gpsimd.affine_select(out=amask[:, :, :], in_=amask[:, :, :], compare_op=ALU.is_ge, fill=0.0, base=DH - 1,
                                    pattern=[[-P, 2], [DH, HEADS]], channel_multiplier=-1).then_inc(s_const, 1)
            nc.gpsimd.iota(ncol[:, :], pattern=[[0, HEADS]], base=0, channel_multiplier=1,
                           allow_small_or_imprecise_dtypes=True).then_inc(s_const, 1)

        @block.tensor
        def _(pe):
            pe.wait_ge(s_const, 6)
            pe.wait_ge(s_w, 48)
            if first:
                for o in range(2):
                    for i in range(2):
                        mm = nc.tensor.transpose(ps_x[:, i, o * P:(o + 1) * P], w_in[:, o, i * P:(i + 1) * P], ident[:, :])
                mm.then_inc(s_wt, 1)
            pe.wait_ge(s_wts, 1)
            pe.wait_ge(s_amat, 1)

            def turn(i, k):
                hold(pe, s_xg, i * U + (k + 1), s_passp)
                hold(pe, s_xts, i * U + (k + 1), s_passp)
                for c in range(2):
                    mm = nc.tensor.transpose(ps_x[:, k % 2, c * P:(c + 1) * P], xg[:, k, c * P:(c + 1) * P], ident[:, :])
                mm.then_inc(s_xt, 1)

            def project(i, k):
                hold(pe, s_xts, i * U + (k + 2), s_passp)
                hold(pe, s_hrow, i * U + (k + 1), s_passp)
                hold(pe, s_hts, i * U + (k + 1), s_passp)
                for c in range(2):
                    nc.tensor.matmul(ps_h[:, k % 2, 0:D], xt[:, k, c, :], w[:, c, :], start=(c == 0), stop=(c == 1))
                for o in range(2):
                    for c in range(2):
                        mm = nc.tensor.matmul(ps_t[:, k % 2, o * P:(o + 1) * P], w[:, c, o * P:(o + 1) * P], xt[:, k, c, :],
                                              start=(c == 0), stop=(c == 1))
                mm.then_inc(s_h, 1)

            def logits(i, k):
                hold(pe, s_hts, i * U + (k + 2), s_passp)
                hold(pe, s_acp, i * U + (k + 1), s_passp)
                for o in range(2):
                    mm = nc.tensor.matmul(ps_a[:, k % 2, 0:2 * HEADS], ht[:, k, o, :], amat[:, o, :], start=(o == 0), stop=(o == 1))
                mm.then_inc(s_a, 1)

            with pe.Fori(0, NT // U) as i:
                turn(i, 0)
                for k in range(U):
                    if k + 1 < U:
                        turn(i, k + 1)
                    project(i, k)
                    if k:
                        logits(i, k - 1)
                logits(i, U - 1)

        @block.scalar
        def _(act):
            if first:
                act.wait_ge(s_wt, 1)
                nc.scalar.copy(w[:, :, :], ps_x[:, :, 0:D]).then_inc(s_wts, 1)
            else:
                act.wait_ge(s_w, 48)
                nc.scalar.copy(w[:, :, :], w_in[:, :, :]).then_inc(s_wts, 1)
            act.wait_ge(s_var, 1)
            nc.scalar.activation(std[:, :], var[:, :], ACT.Sqrt, bias=eps[:, 0:1]).then_inc(s_std, 1)
            act.wait_ge(s_wts, 1)
            act.sem_inc(s_xts, 1)
            act.sem_inc(s_hrow, 1)

            def copy_x(i, k):
                hold(act, s_xt, i * U + (k + 1), s_pa)
                nc.scalar.copy(xt[:, k, :, :], ps_x[:, k % 2, 0:D].rearrange("p (c n) -> p c n", c=2)).then_inc(s_xts, 1)

            def copy_h(i, k):
                hold(act, s_h, i * U + (k + 1), s_pa)
                hold(act, s_st[k], i * n_st + 16, s_pa)
                nc.scalar.copy(row[:, k, 0:D], ps_h[:, k % 2, 0:D]).then_inc(s_hrow, 1)

            with act.Fori(0, NT // U) as i:
                copy_x(i, 0)
                for k in range(U):
                    if k + 1 < U:
                        copy_x(i, k + 1)
                    copy_h(i, k)

        @block.vector
        def _(v):
            steps = [0]

            def done(ins):
                steps[0] += 1
                ins.then_inc(s_chain, 1)
                v.wait_ge(s_chain, steps[0])

            done(nc.vector.memset(eps[:, :], EPS))
            if first:
                nc.vector.memset(xs[:, NT - 1, :], 0.0).then_inc(s_zero, 1)
            v.wait_ge(s_const, 6)
            v.wait_ge(s_w, 48)
            for k in range(2):
                for i in range(2):
                    done(nc.vector.tensor_scalar(amat[:, k, i * HEADS:(i + 1) * HEADS], amask[:, k, :], avec[:, k, i:i + 1], None, ALU.mult))
            v.sem_inc(s_amat, 1)
            for c in range(U):
                v.wait_ge(s_x[c], 32 if first and c == U - 1 else 16)
                with v.Fori(c * U, (c + 1) * U) as t:
                    nc.vector.bn_stats(st[:, bass.ds(t, 1), :], xs[:, bass.ds(t, 1), :]).then_inc(s_stat, 1)
            v.wait_ge(s_stat, NT)
            done(nc.vector.tensor_tensor(mean[:, :], st[:, :, 1], st[:, :, 4], ALU.add))
            done(nc.vector.tensor_scalar(mean[:, :], mean[:, :], 0.5, None, ALU.mult))
            done(nc.vector.tensor_tensor(dif[:, :], st[:, :, 1], st[:, :, 4], ALU.subtract))
            done(nc.vector.scalar_tensor_tensor(dif[:, :], dif[:, :], 0.25, dif[:, :], ALU.mult, ALU.mult))
            done(nc.vector.tensor_tensor(var[:, :], st[:, :, 2], st[:, :, 5], ALU.add))
            done(nc.vector.scalar_tensor_tensor(var[:, :], var[:, :], 1.0 / D, dif[:, :], ALU.mult, ALU.add))
            v.sem_inc(s_var, 1)
            v.wait_ge(s_std, 1)
            done(nc.vector.reciprocal(rstd[:, :], std[:, :]))
            v.sem_inc(s_hts, 1)
            v.sem_inc(s_acp, 1)

            def normalise(i, k):
                t = i * U + k
                nc.vector.tensor_scalar(xg[:, k, :], xs[:, bass.ds(t, 1), :], mean[:, bass.ds(t, 1)], rstd[:, bass.ds(t, 1)],
                                        ALU.subtract, ALU.mult).then_inc(s_xg, 1)

            def copy_ht(i, k):
                hold(v, s_h, i * U + (k + 1), s_pass)
                hold(v, s_st[k], i * n_st + 16, s_pass)
                nc.vector.tensor_copy(ht[:, k, :, :], ps_t[:, k % 2, 0:D].rearrange("p (c n) -> p c n", c=2)).then_inc(s_hts, 1)

            def copy_a(i, k):
                hold(v, s_a, i * U + (k + 1), s_pass)
                nc.vector.tensor_copy(wcol[:, k, :, 0], ncol[:, :])
                nc.vector.tensor_copy(wcol[:, k, :, 1], ps_a[:, k % 2, HEADS:2 * HEADS]).then_inc(s_nc, 1)
                nc.vector.tensor_copy(row[:, k, D:ROW], ps_a[:, k % 2, 0:HEADS]).then_inc(s_nc, 1)
                hold(v, s_nc, (i * U + (k + 1)) * 2, s_pass)
                nc.vector.tensor_scalar(ncol[:, :], ncol[:, :], float(P), None, ALU.add).then_inc(s_acp, 1)
                hold(v, s_acp, i * U + (k + 2), s_pass)

            with v.Fori(0, NT // U) as i:
                normalise(i, 0)
                for k in range(U):
                    if k + 1 < U:
                        normalise(i, k + 1)
                    copy_ht(i, k)
                    if k:
                        copy_a(i, k - 1)
                copy_a(i, U - 1)


def edge_phase(nc, io, dr, layer):
    first = layer == 0
    with ExitStack() as ctx:
        sb = lambda n, s, d: ctx.enter_context(nc.sbuf_tensor(f"e{layer}_" + n, s, d))
        ps = lambda n, s: ctx.enter_context(nc.psum_tensor(f"e{layer}_" + n, s, F32))
        sem = semaphores(nc, ctx, f"e{layer}_")
        ident = sb("ident", [P, P], F32)
        hmask = sb("hmask", [P, 2, HEADS], F32)
        own_i = sb("own_i", [P, HEADS], I32)
        prow_i = sb("prow_i", [P, 1], I32)
        own = sb("own", [P, HEADS], F32)
        prow = sb("prow", [P, 1], F32)
        dstb = sb("dstb", [P, UN, BE], I32)
        idx = sb("idx", [P, UN, CH], I32)
        wc = sb("wc", [P, UN, 2], F32)
        nf = sb("nf", [P, UN], F32)
        htw = sb("htw", [P, UN, 2, WIN], F32)
        at = sb("at", [K_ENC, UN, BE], BF16)
        rows = sb("rows", [P, UN, CH, ROW], F32)
        arep = sb("arep", [P, 2, CH, WIN, HEADS], F32)
        encr = sb("encr", [P, 2, 2, BE], F32)
        bd = sb("bd", [P, 2, 2, P], F32)
        mask = sb("mask", [P, 2, BE], F32)
        x = sb("x", [P, BE], F32)
        z = sb("z", [P, BE], F32)
        lk = sb("lk", [P, 2, BE], F32)
        prob = sb("prob", [P, 2, BE], F32)
        pt = sb("pt", [P, 2, BE], F32)
        mx = sb("mx", [P, 4], F32)
        nmo = sb("nmo", [P, UN], F32)
        negm = sb("negm", [P, UN], F32)
        corr = sb("corr", [P, UN], F32)
        denb = sb("denb", [P, UN], F32)
        den = sb("den", [P, 3], F32)
        dia = sb("dia", [P, HEADS, DH], F32)
        dg = sb("dg", [P, DH], F32)
        acc = sb("acc", [P, DH], F32)
        res = sb("res", [P, 2, DH], F32)
        nbi = sb("nbi", [1, 4], I32)
        w_st = sb("w_st", [4, D], F32)
        w_rest = sb("w_rest", [4, D], F32)
        w_part = sb("w_part", [4, 3, D], BF16)
        w_enc = sb("w_enc", [K_ENC, D], BF16)
        ps_e = ps("ps_e", [P, 1024])
        ps_s = ps("ps_s", [P, 1024])
        ps_t = ps("ps_t", [P, 1024])
        ps_o = ps("ps_o", [P, 2, 512])
        s_nb, s_const, s_w, s_wp, s_we, s_init = (sem(n) for n in ("nb", "const", "w", "wp", "we", "init"))
        s_load = [sem(f"load{k}") for k in range(UN)]
        s_rows = [sem(f"rows{k}") for k in range(UN)]
        s_enc, s_relu, s_bd, s_s, s_a, s_lk, s_exp, s_t, s_pt, s_o, s_fin, s_out = (
            sem(n) for n in ("enc", "relu", "bd", "s", "a", "lk", "exp", "t", "pt", "o", "fin", "out"))
        s_rep = sem("rep")
        s_v, s_pv, s_pp, s_pa, s_ps, s_pg = (sem(n) for n in ("v", "pv", "pp", "pa", "ps", "pg"))
        n_load = 16 * (6 if first else 4)
        MAXS = MAXB // UN - 2

        def steps_of(eng):
            eng.wait_ge(s_nb, 16)
            return eng.value_load(nbi[0:1, 0:1], min_val=1, max_val=MAXS)

        block = ctx.enter_context(nc.Block())

        @block.sync
        def _(sp):
            sp.dma_start(nbi[0:1, :], dr["nblk"][:, :]).then_inc(s_nb, 16)
            if first:
                with nc.allow_non_contiguous_dma(reason="a 256 x 3 matrix transposed, once"):
                    sp.dma_start(w_st[0:3, :], io["L0_gnn_edge_W"].rearrange("o c -> c o")).then_inc(s_w, 16)
                sp.dma_start(w_st[3:4, :], io["L0_gnn_edge_b"].rearrange("(a o) -> a o", a=1)).then_inc(s_w, 16)
                sp.wait_ge(s_wp, 1)
                for k in range(3):
                    for i in range(3):
                        sp.dma_start(w_enc[12 * k + 4 * i:12 * k + 4 * i + 4, :], w_part[:, k, :]).then_inc(s_we, 16)

            def load(b, k):
                w = sp.value_load(dr["blk"][bass.ds(b, 1), 0:1], min_val=0, max_val=NW)
                e = sp.value_load(dr["blk"][bass.ds(b, 1), 1:2], min_val=0, max_val=EP - BE)
                sp.dma_start(idx[:, k, :], dr["srcp"][bass.ds(e, BE)].rearrange("(p j) -> p j", j=CH)).then_inc(s_load[k], 16)
                sp.dma_start(dstb[:, k, :], dr["dstp"][bass.ds(e, BE)].partition_broadcast(P)).then_inc(s_load[k], 16)
                sp.dma_start(wc[:, k, :], dr["wcol"].rearrange("(w t) (h c) -> w (t h) c", t=WIN, c=2)[bass.ds(w, 1), :, :]
                             .rearrange("a p c -> (a p) c")).then_inc(s_load[k], 16)
                sp.dma_start(nf[:, k:k + 1], dr["blkf"][bass.ds(b, 1), 0:1].rearrange("a c -> (a c)").partition_broadcast(P)).then_inc(s_load[k], 16)
                if first:
                    sp.dma_start(at[:, k, :], dr["attrp"][:, bass.ds(e, BE)]).then_inc(s_load[k], 16)
                    sp.dma_start(htw[:, k, :, :], dr["hT"].rearrange("(c p) n -> p c n", p=P)[:, :, bass.ds(w * WIN, WIN)]).then_inc(s_load[k], 16)

            def store(b, p):
                w = sp.value_load(dr["blk"][bass.ds(b, 1), 0:1], min_val=0, max_val=NW)
                hold(sp, s_out, b * 16 + 32, s_ps)
                hold(sp, s_fin, b + 3, s_ps)
                sp.dma_start(dr["agg"].rearrange("(w t) (h c) -> w (t h) c", t=WIN, c=DH)[bass.ds(w, 1), :, :]
                             .rearrange("a p c -> (a p) c"), res[:, p, :]).then_inc(s_out, 16)

            for k in range(UN):
                load(k, k)
            sp.sem_inc(s_out, 32)
            steps = steps_of(sp)
            with sp.Fori(0, steps) as i:
                for k in range(UN):
                    hold(sp, s_lk, i * UN + (k + 1), s_ps)
                    load(i * UN + (UN + k), k)
                    store(i * UN + k, k % 2)
            for k in range(2):
                store(steps * UN + k, k)
            for k in range(UN):
                hold(sp, s_load[k], steps * n_load + n_load, s_ps)
            hold(sp, s_out, steps * (16 * UN) + 64, s_ps)

        @block.gpsimd
        def _(pool):
            nc.gpsimd.memset(ident[:, :], 0.0).then_inc(s_const, 1)
            nc.gpsimd.memset(hmask[:, :, :], 1.0).then_inc(s_const, 1)
            pool.wait_ge(s_const, 2)
            nc.gpsimd.affine_select(out=ident[:, :], in_=ident[:, :], compare_op=ALU.not_equal, fill=1.0, base=0,
                                    pattern=[[-1, P]], channel_multiplier=1).then_inc(s_const, 1)
            nc.gpsimd.affine_select(out=hmask[:, :, :], in_=hmask[:, :, :], compare_op=ALU.is_ge, fill=0.0, base=0,
                                    pattern=[[P, 2], [-DH, HEADS]], channel_multiplier=1).then_inc(s_const, 1)
            pool.wait_ge(s_const, 4)
            nc.gpsimd.affine_select(out=hmask[:, :, :], in_=hmask[:, :, :], compare_op=ALU.is_ge, fill=0.0, base=DH - 1,
                                    pattern=[[-P, 2], [DH, HEADS]], channel_multiplier=-1).then_inc(s_const, 1)
            nc.gpsimd.iota(prow_i[:, :], pattern=[[0, 1]], base=0, channel_multiplier=1).then_inc(s_const, 1)
            nc.gpsimd.iota(own_i[:, :], pattern=[[1, HEADS]], base=0, channel_multiplier=0).then_inc(s_const, 1)

            def gather(k, turns):
                hold(pool, s_load[k], turns * n_load + n_load, s_pg)
                for j in range(CH):
                    pool.indirect_dma_start(rows[:, k, j, :], None, dr["table"][:, :],
                                            bass.IndirectOffsetOnAxis(idx[:, k, j:j + 1], 0)).then_inc(s_rows[k], 16)

            for k in range(UN):
                pool.wait_ge(s_load[k], n_load)
                for j in range(CH):
                    pool.indirect_dma_start(rows[:, k, j, :], None, dr["table"][:, :],
                                            bass.IndirectOffsetOnAxis(idx[:, k, j:j + 1], 0)).then_inc(s_rows[k], 16)
            steps = steps_of(pool)
            with pool.Fori(0, steps) as i:
                for k in range(UN):
                    hold(pool, s_o, i * UN + (k + 1), s_pg)
                    gather(k, i + 1)
            for k in range(UN):
                hold(pool, s_rows[k], steps * (16 * CH) + 16 * CH, s_pg)

        @block.tensor
        def _(pe):
            pe.wait_ge(s_const, 7)
            if first:
                pe.wait_ge(s_we, 16 * 9)

            def enc(b, k, turns, half):
                if half == 0:
                    hold(pe, s_load[k], turns * n_load + n_load, s_pp)
                hold(pe, s_relu, b * 2 + (half + 1), s_pp)
                cols = at[:, k, :].rearrange("k (p j) -> k j p", j=CH)
                lhs = w_enc[:, half * P:(half + 1) * P]
                nc.tensor.matmul(ps_e[:, 0:4 * P], lhs, cols[:, 0:4, :], start=True, stop=True)
                nc.tensor.matmul(ps_e[:, 4 * P:BE], lhs, cols[:, 4, :], start=True, stop=True).then_inc(s_enc, 1)

            def score(b, p):
                hold(pe, s_a, b + 1, s_pp)
                if first:
                    hold(pe, s_bd, b + 1, s_pp)
                    hold(pe, s_relu, b * 2 + 3, s_pp)
                    for half in range(2):
                        for c0, c1 in ((0, 4 * P), (4 * P, BE)):
                            nc.tensor.matmul(ps_s[:, c0:c1], bd[:, p, half, :], encr[:, p, half, c0:c1],
                                             start=(half == 0), stop=False, skip_group_check=True)
                hold(pe, s_rep, b + 1, s_pp)
                for j in range(CH):
                    mm = nc.tensor.matmul(ps_s[:, j * P:(j + 1) * P], arep[:, p, j, :, :].rearrange("p t h -> p (t h)"),
                                          ident[:, :], start=not first, stop=True, skip_group_check=True)
                mm.then_inc(s_s, 1)

            def turn(b, p):
                hold(pe, s_exp, b + 1, s_pp)
                hold(pe, s_pt, b + 1, s_pp)
                for j in range(CH):
                    mm = nc.tensor.transpose(ps_t[:, j * P:(j + 1) * P], prob[:, p, j * P:(j + 1) * P], ident[:, :])
                mm.then_inc(s_t, 1)

            def total(b, k, p):
                hold(pe, s_pt, b + 2, s_pp)
                hold(pe, s_fin, b + 1, s_pp)
                for j in range(CH):
                    mm = nc.tensor.matmul(ps_o[:, p, 0:D], pt[:, p, j * P:(j + 1) * P], rows[:, k, j, 0:D],
                                          start=(j == 0), stop=(j == CH - 1))
                mm.then_inc(s_o, 1)

            def encs(b):
                for half in range(2):
                    if first:
                        enc(b, b, 0, half)

            encs(0)
            score(0, 0)
            encs(1)
            score(1, 1)
            encs(2)
            turn(0, 0)
            total(0, 0, 0)
            steps = steps_of(pe)
            with pe.Fori(0, steps) as i:
                for q in range(UN):
                    score(i * UN + (q + 2), q % 2)
                    if first:
                        enc(i * UN + (q + 3), (q + 3) % UN, i + (q + 3) // UN, 0)
                    turn(i * UN + (q + 1), (q + 1) % 2)
                    if first:
                        enc(i * UN + (q + 3), (q + 3) % UN, i + (q + 3) // UN, 1)
                    total(i * UN + (q + 1), (q + 1) % UN, (q + 1) % 2)
            turn(steps * UN + 1, 1)
            total(steps * UN + 1, 1, 1)

        @block.scalar
        def _(act):
            act.sem_inc(s_relu, 1)
            act.sem_inc(s_pt, 1)

            def relu(b, p, half):
                hold(act, s_enc, b * 2 + (half + 1), s_pa)
                if not isinstance(b, int) and half == 0:
                    hold(act, s_s, b - 1, s_pa)
                nc.scalar.activation(encr[:, p, half, :], ps_e[:, 0:BE], ACT.Relu).then_inc(s_relu, 1)

            def repeat(b, k, turns, p):
                hold(act, s_rows[k], turns * (16 * CH) + 16 * CH, s_pa)
                if not isinstance(b, int):
                    hold(act, s_s, b - 1, s_pa)
                nc.scalar.copy(arep[:, p, :, :, :], rows[:, k, :, D:ROW].unsqueeze(2).to_broadcast([P, CH, WIN, HEADS])).then_inc(s_rep, 1)

            def copy_t(b, p):
                hold(act, s_t, b + 1, s_pa)
                if not isinstance(b, int):
                    hold(act, s_o, b - 1, s_pa)
                nc.scalar.copy(pt[:, p, :], ps_t[:, 0:BE]).then_inc(s_pt, 1)

            def weights(b, p, k):
                hold(act, s_lk, b + 1, s_pa)
                nc.scalar.activation(corr[:, k:k + 1], nmo[:, k:k + 1], ACT.Exp, bias=negm[:, k:k + 1], scale=-1.0)
                nc.scalar.activation(prob[:, p, :], lk[:, p, :], ACT.Exp, bias=negm[:, k:k + 1],
                                     accum_out=denb[:, k:k + 1]).then_inc(s_exp, 1)

            def relus(b, p):
                for half in range(2):
                    if first:
                        relu(b, p, half)

            relus(0, 0)
            repeat(0, 0, 0, 0)
            relus(1, 1)
            repeat(1, 1, 0, 1)
            weights(0, 0, 0)
            act.wait_ge(s_s, 1)
            relus(2, 0)
            copy_t(0, 0)
            repeat(2, 2, 0, 0)
            weights(1, 1, 1)
            steps = steps_of(act)
            with act.Fori(0, steps) as i:
                for q in range(UN):
                    if first:
                        relu(i * UN + (q + 3), (q + 1) % 2, 0)
                    if q == 0:
                        hold(act, s_t, i * UN + 2, s_pa)
                        hold(act, s_o, i * UN + 1, s_pa)
                        nc.scalar.copy(pt[:, 1, :], ps_t[:, 0:BE]).then_inc(s_pt, 1)
                    else:
                        copy_t(i * UN + (q + 1), (q + 1) % 2)
                    if first:
                        relu(i * UN + (q + 3), (q + 1) % 2, 1)
                    repeat(i * UN + (q + 3), (q + 3) % UN, i + (q + 3) // UN, (q + 1) % 2)
                    weights(i * UN + (q + 2), q % 2, (q + 2) % UN)
            copy_t(steps * UN + 1, 1)

        @block.vector
        def _(v):
            nc.vector.memset(acc[:, :], 0.0).then_inc(s_init, 1)
            nc.vector.memset(den[:, :], 0.0).then_inc(s_init, 1)
            nc.vector.memset(negm[:, :], 0.0).then_inc(s_init, 1)
            v.wait_ge(s_const, 7)
            nc.vector.tensor_single_scalar(prow_i[:, :], prow_i[:, :], HEADS - 1, ALU.bitwise_and).then_inc(s_init, 1)
            v.wait_ge(s_init, 4)
            nc.vector.tensor_copy(prow[:, :], prow_i[:, :]).then_inc(s_init, 1)
            nc.vector.tensor_copy(own[:, :], own_i[:, :]).then_inc(s_init, 1)
            v.wait_ge(s_init, 6)
            nc.vector.tensor_scalar(own[:, :], own[:, :], prow[:, 0:1], None, ALU.is_equal).then_inc(s_init, 1)
            v.wait_ge(s_init, 7)
            if first:
                v.wait_ge(s_w, 32)
                nc.vector.tensor_copy(w_part[:, 0, :], w_st[:, :]).then_inc(s_init, 1)
                v.wait_ge(s_init, 8)
                nc.vector.tensor_tensor(w_rest[:, :], w_st[:, :], w_part[:, 0, :], ALU.subtract).then_inc(s_init, 1)
                v.wait_ge(s_init, 9)
                nc.vector.tensor_copy(w_part[:, 1, :], w_rest[:, :]).then_inc(s_init, 1)
                v.wait_ge(s_init, 10)
                nc.vector.tensor_tensor(w_rest[:, :], w_rest[:, :], w_part[:, 1, :], ALU.subtract).then_inc(s_init, 1)
                v.wait_ge(s_init, 11)
                nc.vector.tensor_copy(w_part[:, 2, :], w_rest[:, :]).then_inc(s_wp, 1)
            v.sem_inc(s_a, 1)
            v.sem_inc(s_fin, 2)

            def diagonal(k, turns, p):
                hold(v, s_load[k], turns * n_load + n_load, s_pv)
                for half in range(2):
                    ins = nc.vector.tensor_tensor(bd[:, p, half, :].rearrange("p (t h) -> p t h", h=HEADS),
                                                  htw[:, k, half, :].unsqueeze(2).to_broadcast([P, WIN, HEADS]),
                                                  hmask[:, half, :].unsqueeze(1).to_broadcast([P, WIN, HEADS]), ALU.mult)
                ins.then_inc(s_bd, 1)

            FIN, SCO = 6, 6

            def counted(base):
                n = [0]

                def did(ins):
                    ins.then_inc(s_v, 1)
                    n[0] += 1
                    return base + n[0]
                return n, did

            def need(count):
                hold(v, s_v, count, s_pv)

            def masks(k, turns, p):
                hold(v, s_load[k], turns * n_load + n_load, s_pv)
                return nc.vector.tensor_scalar(mask[:, p, :], dstb[:, k, :], wc[:, k, 0:1], MASKED, ALU.not_equal, ALU.mult)

            def by_chunk(row):
                return row.rearrange("p (e j) -> p j e", j=CH)

            def chunks(row):
                return row.rearrange("p (j e) -> p j e", j=CH)

            def step(b, k, turns, p, base, sums):
                n, did = counted(base)
                kn, kp, kf = (k + 1) % UN, (k - 1) % UN, (k - 2) % UN
                if sums:
                    hold(v, s_o, b - 1, s_pv)
                    c_dia = did(nc.vector.tensor_tensor(dia[:, :, :], ps_o[:, p, 0:D].rearrange("p (h c) -> p h c", h=HEADS),
                                                        own[:, :].unsqueeze(2).to_broadcast([P, HEADS, DH]), ALU.mult))
                    c_den = did(nc.vector.scalar_tensor_tensor(den[:, 0:1], den[:, 0:1], corr[:, kf:kf + 1], denb[:, kf:kf + 1], ALU.mult, ALU.add))
                did(masks(kn, turns if k + 1 < UN else turns + 1, 1 - p))
                if sums:
                    need(c_den)
                    c_dg = did(nc.vector.tensor_reduce(dg[:, :], dia[:, :, :].rearrange("p h c -> p c h"), AX_X, ALU.add))
                    c_pos = did(nc.vector.tensor_scalar(den[:, 1:2], den[:, 0:1], 1e-10, None, ALU.max))
                    if first:
                        diagonal(kn, turns if k + 1 < UN else turns + 1, 1 - p)
                else:
                    need(base)
                hold(v, s_s, b + 1, s_pv)
                nc.vector.tensor_tensor_reduce(
                    out=chunks(x[:, :]), in0=chunks(ps_s[:, 0:BE]), in1=by_chunk(mask[:, p, :]), scale=1.0, scalar=3.0 * MASKED,
                    op0=ALU.add, op1=ALU.max, accum_out=mx[:, 0:1]).then_inc(s_a, 1)
                if sums:
                    need(c_pos)
                    c_rec = did(nc.vector.reciprocal(den[:, 2:3], den[:, 1:2]))
                    c_acc = did(nc.vector.scalar_tensor_tensor(acc[:, :], acc[:, :], corr[:, kf:kf + 1], dg[:, :], ALU.mult, ALU.add))
                hold(v, s_a, b + 2, s_pv)
                c_mx = did(nc.vector.tensor_scalar(mx[:, 1:2], mx[:, 0:1], wc[:, k, 1:2], -1.0, ALU.add, ALU.mult))
                c_z = did(nc.vector.tensor_scalar(z[:, :], x[:, :], wc[:, k, 1:2], 0.2, ALU.add, ALU.mult))
                need(c_mx)
                c_mo = did(nc.vector.tensor_tensor(nmo[:, k:k + 1], negm[:, kp:kp + 1], nf[:, k:k + 1], ALU.subtract))
                c_lm = did(nc.vector.scalar_tensor_tensor(mx[:, 2:3], mx[:, 1:2], 0.2, mx[:, 1:2], ALU.mult, ALU.min))
                if sums:
                    need(c_acc)
                    hold(v, s_out, b * 16 - 16, s_pv)
                    nc.vector.tensor_scalar(res[:, p, :], acc[:, :], den[:, 2:3], None, ALU.mult).then_inc(s_fin, 1)
                need(c_z)
                did(nc.vector.scalar_tensor_tensor(lk[:, p, :], x[:, :], wc[:, k, 1:2], z[:, :], ALU.add, ALU.max))
                need(c_lm)
                nc.vector.scalar_tensor_tensor(negm[:, k:k + 1], mx[:, 2:3], -FLOOR, nmo[:, k:k + 1], ALU.min, ALU.min).then_inc(s_lk, 1)
                assert n[0] == SCO + (FIN if sums else 0), n

            def finish(b, p, k, base):
                n, did = counted(base)
                hold(v, s_o, b + 1, s_pv)
                hold(v, s_out, b * 16 + 16, s_pv)
                did(nc.vector.tensor_tensor(dia[:, :, :], ps_o[:, p, 0:D].rearrange("p (h c) -> p h c", h=HEADS),
                                            own[:, :].unsqueeze(2).to_broadcast([P, HEADS, DH]), ALU.mult))
                c_den = did(nc.vector.scalar_tensor_tensor(den[:, 0:1], den[:, 0:1], corr[:, k:k + 1], denb[:, k:k + 1], ALU.mult, ALU.add))
                need(c_den)
                did(nc.vector.tensor_reduce(dg[:, :], dia[:, :, :].rearrange("p h c -> p c h"), AX_X, ALU.add))
                c_pos = did(nc.vector.tensor_scalar(den[:, 1:2], den[:, 0:1], 1e-10, None, ALU.max))
                need(c_pos)
                did(nc.vector.reciprocal(den[:, 2:3], den[:, 1:2]))
                c_acc = did(nc.vector.scalar_tensor_tensor(acc[:, :], acc[:, :], corr[:, k:k + 1], dg[:, :], ALU.mult, ALU.add))
                need(c_acc)
                nc.vector.tensor_scalar(res[:, p, :], acc[:, :], den[:, 2:3], None, ALU.mult).then_inc(s_fin, 1)

            if first:
                diagonal(0, 0, 0)
                diagonal(1, 0, 1)
            masks(0, 0, 0).then_inc(s_v, 1)
            step(0, 0, 0, 0, 1, False)
            if first:
                diagonal(2, 0, 0)
            step(1, 1, 0, 1, 1 + SCO, False)
            steps = steps_of(v)
            before = 1 + 2 * SCO
            with v.Fori(0, steps) as i:
                for q in range(UN):
                    step(i * UN + (q + 2), (q + 2) % UN, i + (q + 2) // UN, q % 2,
                         i * (UN * (FIN + SCO)) + (q * (FIN + SCO) + before), True)
            for q in range(2):
                finish(steps * UN + q, q, q, steps * (UN * (FIN + SCO)) + (before + q * FIN))


TB = 256
SUB = TB // P
EXP, FF = 8, 1024
FC = FF // P
DC = D // P
CAP = -(-(5 * N) // (4 * EXP))
R = 7
FMAX = 3.4028234e38


def max_blocks(top):
    return (top * N + EXP * (TB - 1)) // TB


def ffn_phases(nc, io, dr, layer, src, out):
    first = layer == 0
    top = 2 if first else 1
    nblk_max = max_blocks(top)
    n_slot = (nblk_max + 4) * TB
    n_tab = nblk_max + 8
    xb, yb = dr["xb"], dr["yb"]
    names = dict(zip(("wr", "br", "w1", "b1", "w2", "b2"),
                     ("L0_ffn_Wr", "L0_ffn_br", "L0_ffn_W1", "L0_ffn_b1", "L0_ffn_W2", "L0_ffn_b2") if first else
                     ("L1_ffn_gate_w", "L1_ffn_gate_b", "L1_ffn_w1", "L1_ffn_b1", "L1_ffn_w2", "L1_ffn_b2")))
    with ExitStack() as outer:
        keep = lambda n, s, d: outer.enter_context(nc.sbuf_tensor(f"f{layer}_" + n, s, d))
        xs = keep("xs", [P, NT, D], F32)
        slot_i = keep("slot_i", [P, 2, NT], I32)
        wgt = keep("wgt", [P, 2, NT], F32)
        tab_i = keep("tab_i", [1, n_tab], I32)
        cnt_i = keep("cnt_i", [1, 4], I32)

        with ExitStack() as ctx:
            sb = lambda n, s, d: ctx.enter_context(nc.sbuf_tensor(f"r{layer}_" + n, s, d))
            ps = lambda n, s: ctx.enter_context(nc.psum_tensor(f"r{layer}_" + n, s, F32))
            sem = semaphores(nc, ctx, f"r{layer}_")
            ag = sb("ag", [P, 2, R, D], F32)
            bias = sb("bias", [P, D], F32)
            xt = sb("xt", [P, NT, D], F32)
            st = sb("st", [P, NT, 6], F32)
            lnv = sb("lnv", [P, 5, NT], F32)
            eps = sb("eps", [P, 1], F32)
            ident = sb("ident", [P, P], F32)
            upper = sb("upper", [P, P], F32)
            allone = sb("allone", [P, P], F32)
            wr = sb("wr", [P, DC, EXP], F32)
            br = sb("br", [P, EXP], F32)
            xg = sb("xg", [P, R, D], F32)
            xT = sb("xT", [P, R, DC, P], F32)
            zero = sb("zero", [P, 2048], F32)
            lg = sb("lg", [P, NT, EXP], F32)
            pr = sb("pr", [P, NT, EXP], F32)
            tmp = sb("tmp", [P, NT, EXP], F32)
            oh = sb("oh", [P, 2, NT, EXP], F32)
            pick = sb("pick", [P, NT, EXP], F32)
            tot = sb("tot", [P, NT, EXP], F32)
            pos = sb("pos", [P, NT, EXP], F32)
            iota8 = sb("iota8", [P, EXP], F32)
            iotan = sb("iotan", [P, NT], F32)
            valid = sb("valid", [P, NT], F32)
            c1 = sb("c1", [P, 10, NT], F32)
            e8 = sb("e8", [P, 5, EXP], F32)
            trow = sb("trow", [1, 2, n_tab], F32)
            blkrow = sb("blkrow", [1, n_tab], F32)
            cnt_f = sb("cnt_f", [1, 4], F32)
            ps_x = ps("ps_x", [P, 2, 512])
            ps_l = ps("ps_l", [P, 2, 512])
            ps_c = ps("ps_c", [P, 2, 512])
            s_x = [sem(f"x{c}") for c in range(R)]
            s_ag = [sem(f"ag{c}") for c in range(2)]
            s_w, s_const, s_zero, s_fill, s_sum, s_chain, s_stat, s_var, s_std, s_agu, s_xtn = (
                sem(n) for n in ("w", "const", "zero", "fill", "sum", "chain", "stat", "var", "std", "agu", "xtn"))
            s_xg, s_t, s_xT, s_l, s_lg, s_pick, s_cnt, s_slot, s_sc, s_pp, s_pa, s_pv, s_soft, s_exp, s_in = (
                sem(n) for n in ("xg", "t", "xT", "l", "lg", "pick", "cnt", "slot", "sc", "pp", "pa", "pv", "soft", "exp", "in"))

            block = ctx.enter_context(nc.Block())

            @block.sync
            def _(sp):
                sp.wait_ge(s_zero, 2)
                for c in range(R):
                    rest = N - (NT - 1) * P
                    if first and c == R - 1:
                        sp.dma_start(xs[:, c * R:NT - 1, :], src[c * R * P:(NT - 1) * P, :].rearrange("(t p) d -> p t d", p=P)).then_inc(s_x[c], 16)
                        sp.dma_start(xs[0:rest, NT - 1, :], src[(NT - 1) * P:N, :]).then_inc(s_x[c], 16)
                    else:
                        sp.dma_start(xs[:, c * R:(c + 1) * R, :],
                                     src[c * R * P:(c + 1) * R * P, :].rearrange("(t p) d -> p t d", p=P)).then_inc(s_x[c], 16)
                    if c >= 2:
                        sp.wait_ge(s_agu, c - 1)
                    sp.dma_start(ag[:, c % 2, :, :], dr["agg"][c * R * P:(c + 1) * R * P, :].rearrange("(t p) d -> p t d", p=P)).then_inc(s_ag[c % 2], 16)
                    if c == 0:
                        sp.dma_start(bias[:, :], io["L0_gnn_bias" if first else "L1_gnn_bias"].partition_broadcast(P)).then_inc(s_w, 16)
                        sp.dma_start(wr[:, :, :], io[names["wr"]].rearrange("(c p) e -> p c e", p=P)).then_inc(s_w, 16)
                        sp.dma_start(br[:, :], io[names["br"]].partition_broadcast(P)).then_inc(s_w, 16)
                for r0 in range(0, n_slot, 8 * P):
                    n = min(8, (n_slot - r0) // P)
                    sp.dma_start(xb[r0:r0 + n * P, :].rearrange("(p j) d -> p (j d)", p=P), zero[:, 0:n * D]).then_inc(s_fill, 16)
                least = -(-top * N // TB) * TB
                for r0 in range(least, n_slot + 2 * P, 8 * P):
                    n = min(8, (n_slot + 2 * P - r0) // P)
                    sp.dma_start(yb[r0:r0 + n * P, :].rearrange("(p j) d -> p (j d)", p=P), zero[:, 0:n * D]).then_inc(s_fill, 16)
                sp.wait_ge(s_fill, 16 * (-(-n_slot // (8 * P)) - (-(n_slot + 2 * P - least) // (8 * P))))
                sp.sem_inc(s_in, 1)

            @block.gpsimd
            def _(pool):
                nc.gpsimd.memset(ident[:, :], 0.0).then_inc(s_const, 1)
                nc.gpsimd.memset(upper[:, :], 1.0).then_inc(s_const, 1)
                nc.gpsimd.memset(allone[:, :], 1.0).then_inc(s_const, 1)
                pool.wait_ge(s_const, 3)
                nc.gpsimd.affine_select(out=ident[:, :], in_=ident[:, :], compare_op=ALU.not_equal, fill=1.0, base=0,
                                        pattern=[[-1, P]], channel_multiplier=1).then_inc(s_const, 1)
                nc.gpsimd.affine_select(out=upper[:, :], in_=upper[:, :], compare_op=ALU.is_ge, fill=0.0, base=-1,
                                        pattern=[[1, P]], channel_multiplier=-1).then_inc(s_const, 1)
                nc.gpsimd.iota(iota8[:, :], pattern=[[1, EXP]], base=0, channel_multiplier=0,
                               allow_small_or_imprecise_dtypes=True).then_inc(s_const, 1)
                nc.gpsimd.iota(iotan[:, :], pattern=[[P, NT]], base=0, channel_multiplier=1,
                               allow_small_or_imprecise_dtypes=True).then_inc(s_const, 1)
                nc.gpsimd.iota(blkrow[:, :], pattern=[[1, n_tab]], base=0, channel_multiplier=0,
                               allow_small_or_imprecise_dtypes=True).then_inc(s_const, 1)
                pool.wait_ge(s_in, 1)
                pool.wait_ge(s_slot, 1)
                for t in range(NT):
                    for c in range(top):
                        pool.indirect_dma_start(xb[:, :], bass.IndirectOffsetOnAxis(slot_i[:, c, t:t + 1], 0),
                                                xt[:, t, :], None).then_inc(s_sc, 16)
                pool.wait_ge(s_sc, 16 * NT * top)

            @block.tensor
            def _(pe):
                pe.wait_ge(s_const, 8)
                pe.wait_ge(s_w, 48)

                def turn(i, k):
                    hold(pe, s_xg, i * R + (k + 1), s_pp)
                    hold(pe, s_xT, i * R + (k + 1), s_pp)
                    for c in range(DC):
                        mm = nc.tensor.transpose(ps_x[:, k % 2, c * P:(c + 1) * P], xg[:, k, c * P:(c + 1) * P], ident[:, :])
                    mm.then_inc(s_t, 1)

                def logits(i, k):
                    hold(pe, s_xT, i * R + (k + 2), s_pp)
                    hold(pe, s_lg, i * R + (k + 1), s_pp)
                    for c in range(DC):
                        mm = nc.tensor.matmul(ps_l[:, k % 2, 0:EXP], xT[:, k, c, :], wr[:, c, :], start=(c == 0), stop=(c == DC - 1))
                    mm.then_inc(s_l, 1)

                with pe.Fori(0, NT // R) as i:
                    turn(i, 0)
                    for k in range(R):
                        if k + 1 < R:
                            turn(i, k + 1)
                        logits(i, k)
                pe.wait_ge(s_pick, 1)
                picks = pick[:, :, :].rearrange("p t e -> p (t e)")
                nc.tensor.matmul(ps_c[:, 0, 0:NT * EXP], upper[:, :], picks, start=True, stop=True)
                nc.tensor.matmul(ps_c[:, 1, 0:NT * EXP], allone[:, :], picks, start=True, stop=True).then_inc(s_cnt, 1)

            @block.scalar
            def _(act):
                act.wait_ge(s_var, 1)
                nc.scalar.activation(lnv[:, 3, :], lnv[:, 1, :], ACT.Sqrt, bias=eps[:, 0:1]).then_inc(s_std, 1)
                if first:
                    act.wait_ge(s_var, 2)
                    nc.scalar.activation(lnv[:, 3, :], lnv[:, 1, :], ACT.Sqrt, bias=eps[:, 0:1]).then_inc(s_std, 1)
                act.sem_inc(s_xT, 1)
                with act.Fori(0, NT // R) as i:
                    for k in range(R):
                        hold(act, s_t, i * R + (k + 1), s_pa)
                        nc.scalar.copy(xT[:, k, :, :], ps_x[:, k % 2, 0:D].rearrange("p (c n) -> p c n", c=DC)).then_inc(s_xT, 1)
                act.wait_ge(s_soft, 1)
                nc.scalar.activation(pr[:, :, :], tmp[:, :, :], ACT.Exp).then_inc(s_exp, 1)

            @block.vector
            def _(v):
                steps = [0]

                def done(ins):
                    steps[0] += 1
                    ins.then_inc(s_chain, 1)
                    v.wait_ge(s_chain, steps[0])

                def tt(o, a, b, op):
                    done(nc.vector.tensor_tensor(o, a, b, op))

                def ts(o, a, s1, s2, *ops):
                    done(nc.vector.tensor_scalar(o, a, s1, s2, *ops))

                nc.vector.memset(zero[:, :], 0.0).then_inc(s_zero, 1)
                nc.vector.memset(xs[:, NT - 1, :], 0.0).then_inc(s_zero, 1)
                done(nc.vector.memset(eps[:, :], EPS))
                v.wait_ge(s_const, 8)
                v.wait_ge(s_w, 48)
                v.wait_ge(s_zero, 2)
                for c in range(R):
                    v.wait_ge(s_x[c], 32 if first and c == R - 1 else 16)
                    v.wait_ge(s_ag[c % 2], 16 * (c // 2 + 1))
                    rows = xs[:, c * R:(c + 1) * R, :]
                    tt(ag[:, c % 2, :, :], ag[:, c % 2, :, :], bias[:, :].unsqueeze(1).to_broadcast([P, R, D]), ALU.add)
                    tt(rows, rows, ag[:, c % 2, :, :], ALU.add)
                    v.sem_inc(s_agu, 1)

                def stats(t0, count):
                    v.wait_ge(s_stat, count)
                    m, var, d = lnv[:, 0, :], lnv[:, 1, :], lnv[:, 2, :]
                    tt(m, st[:, :, 1], st[:, :, 4], ALU.add)
                    ts(m, m, 0.5, None, ALU.mult)
                    tt(d, st[:, :, 1], st[:, :, 4], ALU.subtract)
                    done(nc.vector.scalar_tensor_tensor(d, d, 0.25, d, ALU.mult, ALU.mult))
                    tt(var, st[:, :, 2], st[:, :, 5], ALU.add)
                    done(nc.vector.scalar_tensor_tensor(var, var, 1.0 / D, d, ALU.mult, ALU.add))
                    v.sem_inc(s_var, 1)
                    v.wait_ge(s_std, t0)
                    done(nc.vector.reciprocal(lnv[:, 4, :], lnv[:, 3, :]))

                with v.Fori(0, NT) as t:
                    nc.vector.bn_stats(st[:, bass.ds(t, 1), :], xs[:, bass.ds(t, 1), :]).then_inc(s_stat, 1)
                stats(1, NT)
                with v.Fori(0, NT) as t:
                    nc.vector.tensor_scalar(xt[:, bass.ds(t, 1), :], xs[:, bass.ds(t, 1), :], lnv[:, 0, bass.ds(t, 1)],
                                            lnv[:, 4, bass.ds(t, 1)], ALU.subtract, ALU.mult).then_inc(s_xtn, 1)
                v.wait_ge(s_xtn, NT)
                if first:
                    with v.Fori(0, NT) as t:
                        nc.vector.bn_stats(st[:, bass.ds(t, 1), :], xt[:, bass.ds(t, 1), :]).then_inc(s_stat, 1)
                    stats(2, 2 * NT)
                v.sem_inc(s_lg, 1)
                with v.Fori(0, NT // R) as i:
                    for k in range(R + 1):
                        if k < R:
                            if k == 0:
                                hold(v, s_lg, i * R + 1, s_pv)
                            nc.vector.tensor_copy(xg[:, k, :], xt[:, bass.ds(i * R + k, 1), :]).then_inc(s_xg, 1)
                            if first:
                                hold(v, s_xg, i * R + (k + 1), s_pv)
                                t = i * R + k
                                nc.vector.tensor_scalar(xt[:, bass.ds(t, 1), :], xt[:, bass.ds(t, 1), :], lnv[:, 0, bass.ds(t, 1)],
                                                        lnv[:, 4, bass.ds(t, 1)], ALU.subtract, ALU.mult).then_inc(s_xtn, 1)
                        if k:
                            hold(v, s_l, i * R + k, s_pv)
                            nc.vector.tensor_tensor(lg[:, bass.ds(i * R + (k - 1), 1), :], ps_l[:, (k - 1) % 2:(k - 1) % 2 + 1, 0:EXP],
                                                    br[:, :].unsqueeze(1), ALU.add).then_inc(s_lg, 1)
                v.wait_ge(s_lg, NT + 1)
                v.wait_ge(s_xtn, NT * (2 if first else 1))
                wide = lambda col: col.unsqueeze(2).to_broadcast([P, NT, EXP])
                each = lambda row: row.unsqueeze(1).to_broadcast([P, NT, EXP])

                def red(o, i, op):
                    done(nc.vector.tensor_reduce(o, i, AX_X, op))

                red(c1[:, 0, :], lg[:, :, :], ALU.max)
                tt(tmp[:, :, :], lg[:, :, :], wide(c1[:, 0, :]), ALU.subtract)
                v.sem_inc(s_soft, 1)
                v.wait_ge(s_exp, 1)
                red(c1[:, 1, :], pr[:, :, :], ALU.add)
                done(nc.vector.reciprocal(c1[:, 2, :], c1[:, 1, :]))
                tt(pr[:, :, :], pr[:, :, :], wide(c1[:, 2, :]), ALU.mult)
                ts(valid[:, :], iotan[:, :], float(N), None, ALU.is_lt)
                for c in range(top):
                    red(c1[:, 3 + c, :], pr[:, :, :], ALU.max)
                    tt(tmp[:, :, :], pr[:, :, :], wide(c1[:, 3 + c, :]), ALU.is_equal)
                    done(nc.vector.scalar_tensor_tensor(tmp[:, :, :], tmp[:, :, :], -float(EXP), each(iota8[:, :]), ALU.mult, ALU.add))
                    red(c1[:, 5, :], tmp[:, :, :], ALU.min)
                    tt(oh[:, c, :, :], tmp[:, :, :], wide(c1[:, 5, :]), ALU.is_equal)
                    if c + 1 < top:
                        done(nc.vector.scalar_tensor_tensor(pr[:, :, :], oh[:, c, :, :], -2.0, pr[:, :, :], ALU.mult, ALU.add))
                if first:
                    tt(c1[:, 5, :], c1[:, 3, :], c1[:, 4, :], ALU.add)
                    done(nc.vector.reciprocal(c1[:, 6, :], c1[:, 5, :]))
                    tt(wgt[:, 0, :], c1[:, 3, :], c1[:, 6, :], ALU.mult)
                    tt(wgt[:, 1, :], c1[:, 4, :], c1[:, 6, :], ALU.mult)
                    tt(pick[:, :, :], oh[:, 0, :, :], oh[:, 1, :, :], ALU.add)
                    tt(pick[:, :, :], pick[:, :, :], wide(valid[:, :]), ALU.mult)
                else:
                    tt(pick[:, :, :], oh[:, 0, :, :], wide(valid[:, :]), ALU.mult)
                v.sem_inc(s_pick, 1)
                v.wait_ge(s_cnt, 1)
                done(nc.vector.tensor_copy(tot[:, :, :], ps_c[:, 1, 0:NT * EXP].rearrange("p (t e) -> p t e", e=EXP)))
                for e in range(EXP):
                    done(nc.vector.tensor_tensor_scan(pos[:, :, e], tot[:, :, e], zero[:, 0:NT], 0.0, ALU.add, ALU.add))
                done(nc.vector.tensor_copy(e8[:, 0, :], pos[:, NT - 1, :]))
                ts(e8[:, 1, :], e8[:, 0, :], 1.0 / TB, 0.5 - 0.5 / TB, ALU.mult, ALU.add)
                ts(e8[:, 1, :], e8[:, 1, :], 8388608.0, None, ALU.add)
                ts(e8[:, 1, :], e8[:, 1, :], -8388608.0, None, ALU.add)
                done(nc.vector.tensor_tensor_scan(e8[:, 2, :], e8[:, 1, :], zero[:, 0:EXP], 0.0, ALU.add, ALU.add))
                tt(e8[:, 3, :], e8[:, 2, :], e8[:, 1, :], ALU.subtract)
                ts(e8[:, 3, :], e8[:, 3, :], float(TB), None, ALU.mult)
                tt(pos[:, :, :], pos[:, :, :], tot[:, :, :], ALU.subtract)
                tt(pos[:, :, :], pos[:, :, :], ps_c[:, 0, 0:NT * EXP].rearrange("p (t e) -> p t e", e=EXP), ALU.add)
                if not first:
                    tt(tmp[:, :, :], pos[:, :, :], oh[:, 0, :, :], ALU.mult)
                    red(c1[:, 5, :], tmp[:, :, :], ALU.add)
                    ts(c1[:, 6, :], c1[:, 5, :], float(CAP), None, ALU.is_lt)
                    tt(wgt[:, 0, :], c1[:, 3, :], c1[:, 6, :], ALU.mult)
                tt(pos[:, :, :], pos[:, :, :], each(e8[:, 3, :]), ALU.add)
                for c in range(top):
                    tt(tmp[:, :, :], pos[:, :, :], oh[:, c, :, :], ALU.mult)
                    red(c1[:, 5, :], tmp[:, :, :], ALU.add)
                    ts(c1[:, 7, :], c1[:, 5, :], -float(n_slot), None, ALU.add)
                    tt(c1[:, 7, :], c1[:, 7, :], valid[:, :], ALU.mult)
                    ts(c1[:, 7, :], c1[:, 7, :], float(n_slot), None, ALU.add)
                    ts(c1[:, 9, :], iotan[:, :], float(c * P), None, ALU.add)
                    ts(c1[:, 8, :], valid[:, :], -1.0, 1.0, ALU.mult, ALU.add)
                    done(nc.vector.scalar_tensor_tensor(c1[:, 8, :], c1[:, 8, :], c1[:, 9, 0:1], c1[:, 7, :], ALU.mult, ALU.add))
                    done(nc.vector.tensor_copy(slot_i[:, c, :], c1[:, 8, :]))
                v.sem_inc(s_slot, 1)
                done(nc.vector.memset(trow[:, 0, :], 0.0))
                for e in range(EXP - 1):
                    done(nc.vector.scalar_tensor_tensor(trow[:, 0, :], blkrow[:, :], e8[0:1, 2, e:e + 1], trow[:, 0, :], ALU.is_ge, ALU.add))
                done(nc.vector.tensor_copy(tab_i[:, :], trow[:, 0, :]))
                done(nc.vector.tensor_copy(cnt_f[:, :], e8[0:1, 2, EXP - 1:EXP].to_broadcast([1, 4])))
                ts(cnt_f[:, :], cnt_f[:, :], 0.5, 0.25, ALU.mult, ALU.add)
                ts(cnt_f[:, :], cnt_f[:, :], 8388608.0, None, ALU.add)
                ts(cnt_f[:, :], cnt_f[:, :], -8388608.0, None, ALU.add)
                done(nc.vector.tensor_copy(cnt_i[:, :], cnt_f[:, :]))

        with ExitStack() as ctx:
            sb = lambda n, s, d: ctx.enter_context(nc.sbuf_tensor(f"x{layer}_" + n, s, d))
            ps = lambda n, s: ctx.enter_context(nc.psum_tensor(f"x{layer}_" + n, s, F32))
            sem = semaphores(nc, ctx, f"x{layer}_")
            ident = sb("ident", [P, P], F32)
            xin = sb("xin", [P, 2, SUB, D], F32)
            w1 = sb("w1", [P, 2, DC, FF], F32)
            w2 = sb("w2", [P, 2, FC, D], F32)
            b1 = sb("b1", [P, 2, FC], F32)
            b2 = sb("b2", [P, 2, D], F32)
            lng = sb("lng", [P, 2, DC], F32)
            lnb = sb("lnb", [P, 2, DC], F32)
            xT = sb("xT", [P, 2, DC, TB], F32)
            hT = sb("hT", [P, 2, FC, TB], F32)
            y = sb("y", [P, 2, SUB, D], F32)
            ps_x = ps("ps_x", [P, DC, TB])
            ps_h = ps("ps_h", [P, 4, 512])
            ps_y = ps("ps_y", [P, SUB, 512])
            s_const, s_t, s_xT, s_h, s_act, s_y, s_yc, s_pp, s_pa, s_pv, s_ps = (
                sem(n) for n in ("const", "t", "xT", "h", "act", "y", "yc", "pp", "pa", "pv", "ps"))
            s_ldx = [sem(f"ldx{k}") for k in range(2)]
            s_ldw = [sem(f"ldw{k}") for k in range(2)]
            s_out = [sem(f"out{k}") for k in range(2)]
            n_ldx = 16 * (3 if first else 1)
            n_ldw = 16 * 4

            block = ctx.enter_context(nc.Block())

            @block.sync
            def _(sp):
                def load(b, k):
                    e = sp.value_load(tab_i[0:1, bass.ds(b, 1)], min_val=0, max_val=EXP - 1)
                    one = lambda name: io[name][bass.ds(e, 1)]
                    sp.dma_start(xin[:, k, :, :], xb[bass.ds(b * TB, TB), :].rearrange("(s p) d -> p s d", p=P)).then_inc(s_ldx[k], 16)
                    if first:
                        sp.dma_start(lng[:, k, :], one("L0_ffn_ln_g").rearrange("a (p c) -> (a p) c", c=DC)).then_inc(s_ldx[k], 16)
                        sp.dma_start(lnb[:, k, :], one("L0_ffn_ln_b").rearrange("a (p c) -> (a p) c", c=DC)).then_inc(s_ldx[k], 16)
                    sp.dma_start(w1[:, k, :, :], one(names["w1"]).rearrange("a (p c) f -> (a p) c f", c=DC)).then_inc(s_ldw[k], 16)
                    sp.dma_start(w2[:, k, :, :], one(names["w2"]).rearrange("a (p j) d -> (a p) j d", j=FC)).then_inc(s_ldw[k], 16)
                    sp.dma_start(b1[:, k, :], one(names["b1"]).rearrange("a (p j) -> (a p) j", j=FC)).then_inc(s_ldw[k], 16)
                    sp.dma_start(b2[:, k, :], one(names["b2"]).rearrange("a d -> (a d)").partition_broadcast(P)).then_inc(s_ldw[k], 16)

                for k in range(2):
                    load(k, k)
                    sp.sem_inc(s_out[k], 16)
                pairs = sp.value_load(cnt_i[0:1, 0:1], min_val=1, max_val=(nblk_max + 1) // 2)
                with sp.Fori(0, pairs) as i:
                    for k in range(2):
                        hold(sp, s_yc, i * 2 + (k + 2), s_ps)
                        load(i * 2 + (k + 2), k)
                        sp.dma_start(yb[bass.ds(i * (2 * TB) + k * TB, TB), :].rearrange("(s p) d -> p s d", p=P),
                                     y[:, k, :, :]).then_inc(s_out[k], 16)
                for k in range(2):
                    hold(sp, s_out[k], pairs * 16 + 16, s_ps)
                    hold(sp, s_ldx[k], pairs * n_ldx + n_ldx, s_ps)
                    hold(sp, s_ldw[k], pairs * n_ldw + n_ldw, s_ps)

            @block.gpsimd
            def _(pool):
                nc.gpsimd.memset(ident[:, :], 0.0).then_inc(s_const, 1)
                pool.wait_ge(s_const, 1)
                nc.gpsimd.affine_select(out=ident[:, :], in_=ident[:, :], compare_op=ALU.not_equal, fill=1.0, base=0,
                                        pattern=[[-1, P]], channel_multiplier=1).then_inc(s_const, 1)

            @block.tensor
            def _(pe):
                pe.wait_ge(s_const, 2)

                def turn(k):
                    for c in range(DC):
                        for s in range(SUB):
                            mm = nc.tensor.transpose(ps_x[:, c, s * P:(s + 1) * P],
                                                     xin[:, k, s, :].rearrange("p (m c) -> p c m", c=DC)[:, c, :], ident[:, :])
                    mm.then_inc(s_t, 1)

                pe.wait_ge(s_ldx[0], n_ldx)
                turn(0)
                pairs = pe.value_load(cnt_i[0:1, 0:1], min_val=1, max_val=(nblk_max + 1) // 2)
                with pe.Fori(0, pairs) as i:
                    for k in range(2):
                        hold(pe, s_ldw[k], i * n_ldw + n_ldw, s_pp)
                        hold(pe, s_xT, i * 2 + (k + 1), s_pp)
                        for j in range(FC):
                            hold(pe, s_act, i * (2 * FC) + (k * FC + j + 1), s_pp)
                            for c in range(DC):
                                mm = nc.tensor.matmul(ps_h[:, j % 4, 0:TB],
                                                      w1[:, k, c, :].rearrange("p (m j) -> p j m", j=FC)[:, j, :],
                                                      xT[:, k, c, :], start=(c == 0), stop=(c == DC - 1))
                            mm.then_inc(s_h, 1)
                        hold(pe, s_ldx[1 - k], (i + k) * n_ldx + n_ldx, s_pp)
                        turn(1 - k)
                        hold(pe, s_yc, i * 2 + (k + 1), s_pp)
                        for j in range(FC):
                            hold(pe, s_act, i * (2 * FC) + (k * FC + j + 5), s_pp)
                            for s in range(SUB):
                                mm = nc.tensor.matmul(ps_y[:, s, 0:D], hT[:, k, j, s * P:(s + 1) * P], w2[:, k, j, :],
                                                      start=(j == 0), stop=(j == FC - 1))
                        mm.then_inc(s_y, 1)

            @block.scalar
            def _(act):
                act.sem_inc(s_act, 4)
                pairs = act.value_load(cnt_i[0:1, 0:1], min_val=1, max_val=(nblk_max + 1) // 2)
                with act.Fori(0, pairs) as i:
                    for k in range(2):
                        for j in range(FC):
                            hold(act, s_h, i * (2 * FC) + (k * FC + j + 1), s_pa)
                            nc.scalar.activation(hT[:, k, j, :], ps_h[:, j % 4, 0:TB], ACT.Gelu if first else ACT.Relu,
                                                 bias=b1[:, k, j:j + 1]).then_inc(s_act, 1)

            @block.vector
            def _(v):
                def affine(k):
                    for c in range(DC):
                        if first:
                            ins = nc.vector.tensor_scalar(xT[:, k, c, :], ps_x[:, c, :], lng[:, k, c:c + 1], lnb[:, k, c:c + 1],
                                                          ALU.mult, ALU.add)
                        else:
                            ins = nc.vector.tensor_copy(xT[:, k, c, :], ps_x[:, c, :])
                    ins.then_inc(s_xT, 1)

                v.sem_inc(s_yc, 1)
                v.wait_ge(s_t, 1)
                affine(0)
                pairs = v.value_load(cnt_i[0:1, 0:1], min_val=1, max_val=(nblk_max + 1) // 2)
                with v.Fori(0, pairs) as i:
                    for k in range(2):
                        hold(v, s_t, i * 2 + (k + 2), s_pv)
                        affine(1 - k)
                        hold(v, s_y, i * 2 + (k + 1), s_pv)
                        hold(v, s_out[k], i * 16 + 16, s_pv)
                        for s in range(SUB):
                            ins = nc.vector.tensor_tensor(y[:, k, s, :], ps_y[:, s, 0:D], b2[:, k, :], ALU.add)
                        ins.then_inc(s_yc, 1)

        with ExitStack() as ctx:
            sb = lambda n, s, d: ctx.enter_context(nc.sbuf_tensor(f"c{layer}_" + n, s, d))
            sem = semaphores(nc, ctx, f"c{layer}_")
            g = sb("g", [P, R, 2, D], F32)
            zero = sb("zero", [P, 3, D], F32)
            flag = sb("flag", [P, R, 3, D], I32)
            s_g = [sem(f"g{k}") for k in range(R)]
            s_use, s_one, s_res, s_out, s_pv, s_ps, s_z, s_fl = (sem(n) for n in ("use", "one", "res", "out", "pv", "ps", "z", "fl"))

            block = ctx.enter_context(nc.Block())

            @block.gpsimd
            def _(pool):
                for t in range(NT):
                    if t >= R:
                        pool.wait_ge(s_use, t - R + 1)
                    for c in range(top):
                        pool.indirect_dma_start(g[:, t % R, c, :], None, yb[0:n_slot + 2 * P, :],
                                                bass.IndirectOffsetOnAxis(slot_i[:, c, t:t + 1], 0)).then_inc(s_g[t % R], 16)

            @block.vector
            def _(v):
                for n, value in enumerate((0.0, 10000.0, -10000.0)):
                    nc.vector.memset(zero[:, n, :], value).then_inc(s_z, 1)
                v.wait_ge(s_z, 3)
                with v.Fori(0, NT // R) as i:
                    for k in range(R):
                        t = i * R + k
                        row = xs[:, bass.ds(t, 1), :]
                        hold(v, s_g[k], i * (16 * top) + 16 * top, s_pv)
                        if first:
                            nc.vector.scalar_tensor_tensor(g[:, k, 0:1, :], g[:, k, 0:1, :], wgt[:, 0, bass.ds(t, 1)], row,
                                                           ALU.mult, ALU.add).then_inc(s_one, 1)
                            hold(v, s_one, t + 1, s_pv)
                            nc.vector.scalar_tensor_tensor(row, g[:, k, 1:2, :], wgt[:, 1, bass.ds(t, 1)], g[:, k, 0:1, :],
                                                           ALU.mult, ALU.add).then_inc(s_res, 1)
                            hold(v, s_res, t + 1, s_pv)
                        else:
                            nc.vector.tensor_scalar(g[:, k, 1, :], g[:, k, 0, :], wgt[:, 0, bass.ds(t, 1)], None,
                                                    ALU.mult).then_inc(s_one, 1)
                            hold(v, s_one, t + 1, s_pv)
                            nc.vector.tensor_tensor(flag[:, k, 0, :], g[:, k, 1, :], g[:, k, 1, :], ALU.not_equal)
                            nc.vector.tensor_scalar(flag[:, k, 1, :], g[:, k, 1, :], FMAX, None, ALU.is_gt)
                            nc.vector.tensor_scalar(flag[:, k, 2, :], g[:, k, 1, :], -FMAX, None, ALU.is_lt).then_inc(s_fl, 1)
                            for n in range(3):
                                hold(v, s_fl, t * 4 + (n + 1), s_pv)
                                nc.vector.copy_predicated(g[:, k, 1, :], flag[:, k, n, :], zero[:, n, :]).then_inc(s_fl, 1)
                            hold(v, s_fl, t * 4 + 4, s_pv)
                            nc.vector.tensor_tensor(row, row, g[:, k, 1:2, :], ALU.add).then_inc(s_res, 1)
                            hold(v, s_res, t + 1, s_pv)
                        v.sem_inc(s_use, 1)

            @block.sync
            def _(sp):
                rest = N - (NT - 1) * P
                for c in range(R):
                    sp.wait_ge(s_res, (c + 1) * R)
                    n = R if first or c < R - 1 else R - 1
                    sp.dma_start(out[c * R * P:(c * R + n) * P, :].rearrange("(t p) d -> p t d", p=P),
                                 xs[:, c * R:c * R + n, :]).then_inc(s_out, 16)
                if not first:
                    sp.dma_start(out[(NT - 1) * P:N, :], xs[0:rest, NT - 1, :]).then_inc(s_out, 16)
                sp.wait_ge(s_out, 16 * R + (0 if first else 16))


def scratch(nc):
    dr = {}
    for name, shape, dt in (("pmax", [P, EC], F32), ("smin", [P, EC], F32), ("win", [WT * P, 2], F32), ("nblk", [1, 4], I32),
                            ("dstp", [EP], I32), ("srcp", [EP], I32), ("attrp", [K_ENC, EP], BF16),
                            ("blk", [MAXB, 2], I32), ("blkf", [MAXB, 1], F32),
                            ("table", [NP, ROW], F32), ("wcol", [NP, 2 * HEADS], F32), ("hT", [D, NP], F32),
                            ("agg", [NP, D], F32), ("x2", [NP, D], F32),
                            ("xb", [(max_blocks(2) + 4) * TB + 2 * P, D], F32), ("yb", [(max_blocks(2) + 4) * TB + 2 * P, D], F32)):
        dr[name] = nc.dram_tensor("sc_" + name, shape, dt).ap()
    return dr


def build(nc, io, out):
    dr = scratch(nc)
    plan_phase(nc, io, dr)
    node_phase(nc, io, dr, 0)
    edge_phase(nc, io, dr, 0)
    ffn_phases(nc, io, dr, 0, io["x"], dr["x2"])
    node_phase(nc, io, dr, 1)
    edge_phase(nc, io, dr, 1)
    ffn_phases(nc, io, dr, 1, dr["x2"], out)


_INS = ["x", "src", "dst", "edge_attr_3", "L0_gnn_W", "L0_gnn_a_src", "L0_gnn_a_dst", "L0_gnn_edge_W", "L0_gnn_edge_b",
        "L0_gnn_bias", "L0_ffn_Wr", "L0_ffn_br", "L0_ffn_ln_g", "L0_ffn_ln_b", "L0_ffn_W1", "L0_ffn_b1", "L0_ffn_W2",
        "L0_ffn_b2", "L1_gnn_W", "L1_gnn_attn_l", "L1_gnn_attn_r", "L1_gnn_bias", "L1_ffn_gate_w", "L1_ffn_gate_b",
        "L1_ffn_w1", "L1_ffn_b1", "L1_ffn_w2", "L1_ffn_b2"]


def kernel(**inputs):
    import concourse.bacc as _bacc
    from concourse.bass_utils import run_bass_kernel_spmd as _run

    nc = _bacc.Bacc("TRN2", target_bir_lowering=False, num_devices=1)
    arrays, io = {}, {}
    for name in _INS:
        a = np.ascontiguousarray(inputs[name])
        arrays[f"in_{name}_dram"] = a
        io[name] = nc.dram_tensor(f"in_{name}_dram", a.shape, mybir.dt.from_np(a.dtype), kind="ExternalInput").ap()
    out = nc.dram_tensor("out_0_dram", (N, D), F32, kind="ExternalOutput").ap()
    build(nc, io, out)
    r = _run(nc, [arrays], core_ids=[0])
    return r.results[0]["out_0_dram"]
```

```python
from contextlib import ExitStack

import numpy as np
import concourse.bass as bass
from concourse import mybir

F32 = mybir.dt.float32
BF16 = mybir.dt.bfloat16
I32 = mybir.dt.int32
ALU = mybir.AluOpType
ACT = mybir.ActivationFunctionType
AX_X = mybir.AxisListType.X

P = 128
N, D, E = 6250, 256, 206250
HEADS, DH = 8, 32
NT = -(-N // P)
NP = NT * P
EC = -(-E // P)
E_LAST = E - (P - 1) * EC
WIN = P // HEADS
NW = -(-N // WIN)
WT = -(-(NW + 1) // P)
MEAN = -(-E * WIN // N)
CH = -(-(MEAN + 2 * int(MEAN ** 0.5)) // P)
CK = -(-(MEAN + 9 * int(MEAN ** 0.5) // 4) // CH)
BE = CH * CK
UN = 6
TAIL = BE * (UN + 6)
EP = P * EC + TAIL
MAXB = NW * (-(-E // BE)) + P * 2
MAXB = -(-MAXB // P) * P
PAD_DST = 100000
MASKED = -1.0e30
FLOOR = -1.0e20
EPS = 1e-5
ROW = D + HEADS
PAIRS = 9
K_ENC = PAIRS * 4


def semaphores(nc, ctx, prefix):
    taken = []

    def retire():
        nc.clear_and_free_semaphores(taken)
        nc.all_engine_barrier()

    def sem(name):
        taken.append(nc.alloc_semaphore(prefix + name))
        return taken[-1]

    ctx.callback(retire)
    return sem


def hold(eng, sem, value, passed):
    eng.wait_ge(sem, value)
    eng.sem_inc(passed, 1)


def plan_phase(nc, io, dr):
    with ExitStack() as ctx:
        sb = lambda n, s, d: ctx.enter_context(nc.sbuf_tensor("pl_" + n, s, d))
        ps = lambda n, s: ctx.enter_context(nc.psum_tensor("pl_" + n, s, F32))
        sem = semaphores(nc, ctx, "pl_")
        dst_i = sb("dst_i", [P, EC], I32)
        src_i = sb("src_i", [P, EC], I32)
        dst_f = sb("dst_f", [P, EC], F32)
        pmax = sb("pmax", [P, EC], F32)
        smin = sb("smin", [P, EC], F32)
        attr = sb("attr", [P, EC, 3], F32)
        rest = sb("rest", [P, 3, EC], F32)
        part = sb("part", [P, 3, 3, EC], BF16)
        ones = sb("ones", [P, 2, EC], BF16)
        tail_i = sb("tail_i", [2, TAIL], I32)
        tail_b = sb("tail_b", [12, TAIL], BF16)
        ident = sb("ident", [P, P], F32)
        upper = sb("upper", [P, P], F32)
        allone = sb("allone", [P, P], F32)
        ends = sb("ends", [P, 4], F32)
        erow = sb("erow", [1, 4, P + 1], F32)
        bnd = sb("bnd", [P, 2, P], F32)
        thr = sb("thr", [P, 2, WT], F32)
        cnt = sb("cnt", [P, 2, WT], F32)
        rix = sb("rix", [P, 2, WT], I32)
        rows = sb("rows", [P, 2, EC], F32)
        junk = sb("junk", [P, EC], F32)
        lohi = sb("lohi", [P, 2, WT], F32)
        nb = sb("nb", [P, 4, WT], F32)
        valid = sb("valid", [P, WT], F32)
        cum = sb("cum", [P, WT], F32)
        off = sb("off", [P, WT], F32)
        win = sb("win", [P, WT, 2], F32)
        cumrow = sb("cumrow", [P, WT * P], F32)
        bcol = sb("bcol", [P, 1], F32)
        bw = sb("bw", [P, 6], F32)
        bwi = sb("bwi", [P, 2], I32)
        wi = sb("wi", [P, 1], I32)
        winb = sb("winb", [P, 2], F32)
        nbf = sb("nbf", [1, 4], F32)
        nbi = sb("nbi", [1, 4], I32)
        pt = ps("pt", [P, 512])
        pb = ps("pb", [P, 512])
        pc = ps("pc", [P, 512])
        s_in, s_attr, s_pad, s_const, s_pe, s_tab = (sem(n) for n in ("in", "attr", "pad", "const", "pe", "tab"))
        s_out, s_row, s_wq, s_wg, s_bt = (sem(n) for n in ("out", "row", "wq", "wg", "bt"))
        s_pass, s_split = sem("pass"), sem("split")
        s_win, s_go, s_cp, s_step, s_chain, s_tile = (sem(n) for n in ("win", "go", "cp", "step", "chain", "tile"))
        s_ends, s_scan, s_final, s_parts, s_nb, s_cum, s_blk = (sem(n) for n in ("ends", "scan", "final", "parts", "nb", "cum", "blk"))

        block = ctx.enter_context(nc.Block())

        @block.gpsimd
        def _(pool):
            nc.gpsimd.memset(ident[:, :], 0.0).then_inc(s_const, 1)
            nc.gpsimd.memset(upper[:, :], 1.0).then_inc(s_const, 1)
            nc.gpsimd.memset(allone[:, :], 1.0).then_inc(s_const, 1)
            pool.wait_ge(s_const, 3)
            nc.gpsimd.affine_select(out=ident[:, :], in_=ident[:, :], compare_op=ALU.not_equal, fill=1.0, base=0,
                                    pattern=[[-1, P]], channel_multiplier=1).then_inc(s_const, 1)
            nc.gpsimd.affine_select(out=upper[:, :], in_=upper[:, :], compare_op=ALU.is_ge, fill=0.0, base=0,
                                    pattern=[[1, P]], channel_multiplier=-1).then_inc(s_const, 1)
            nc.gpsimd.iota(bcol[:, :], pattern=[[0, 1]], base=0, channel_multiplier=1,
                           allow_small_or_imprecise_dtypes=True).then_inc(s_const, 1)
            for s in range(2):
                nc.gpsimd.iota(thr[:, s, :], pattern=[[WIN * P, WT]], base=WIN * s, channel_multiplier=WIN,
                               allow_small_or_imprecise_dtypes=True).then_inc(s_const, 1)
            pool.wait_ge(s_row, 1)
            pool.wait_ge(s_out, 32)
            for s in range(2):
                for t in range(WT):
                    k = s * WT + t
                    if k:
                        pool.wait_ge(s_cp, k)
                    pool.indirect_dma_start(rows[:, 0, :], None, (dr["pmax"] if s == 0 else dr["smin"])[:, :],
                                            bass.IndirectOffsetOnAxis(rix[:, s, t:t + 1], 0)).then_inc(s_wg, 16)
                    pool.wait_ge(s_wg, 16 * (k + 1))
            pool.wait_ge(s_win, 16)
            pool.wait_ge(s_step, 1)
            tiles = pool.value_load(nbi[0:1, 1:2], min_val=1, max_val=MAXB // P)
            with pool.Fori(0, tiles) as u:
                hold(pool, s_bt, u * 2 + 1, s_go)
                pool.indirect_dma_start(winb[:, :], None, dr["win"][:, :],
                                        bass.IndirectOffsetOnAxis(wi[:, 0:1], 0)).then_inc(s_wq, 16)

        @block.sync
        def _(sp):
            for tile, name, pad in ((dst_i, "dst", s_pad), (src_i, "src", s_pad)):
                sp.wait_ge(s_pad, 3)
                v = io[name]
                sp.dma_start(tile[0:P - 1, :], v[0:(P - 1) * EC].rearrange("(p e) -> p e", p=P - 1)).then_inc(s_in, 16)
                sp.dma_start(tile[P - 1:P, 0:E_LAST], v[(P - 1) * EC:E].rearrange("(p e) -> p e", p=1)).then_inc(s_in, 16)
            v = io["edge_attr_3"]
            sp.dma_start(attr[0:P - 1, :, :], v[0:(P - 1) * EC, :].rearrange("(p e) c -> p e c", p=P - 1)).then_inc(s_attr, 16)
            sp.dma_start(attr[P - 1:P, 0:E_LAST, :], v[(P - 1) * EC:E, :].rearrange("(p e) c -> p e c", p=1)).then_inc(s_attr, 16)
            sp.wait_ge(s_in, 64)
            sp.wait_ge(s_pad, 6)
            for tile, name, r in ((dst_i, "dstp", 0), (src_i, "srcp", 1)):
                sp.dma_start(dr[name][0:P * EC].rearrange("(p e) -> p e", p=P), tile[:, :]).then_inc(s_tab, 16)
                sp.dma_start(dr[name][P * EC:EP].rearrange("(p e) -> p e", p=1), tail_i[0:1, :]).then_inc(s_tab, 16)
            sp.wait_ge(s_final, 1)
            sp.dma_start(dr["pmax"][:, :], pmax[:, :]).then_inc(s_out, 16)
            sp.dma_start(dr["smin"][:, :], smin[:, :]).then_inc(s_out, 16)
            sp.wait_ge(s_step, 1)
            sp.dma_start(dr["win"].rearrange("(t p) c -> p t c", p=P), win[:, :, :]).then_inc(s_win, 16)
            sp.dma_start(dr["nblk"][:, :], nbi[0:1, :]).then_inc(s_tab, 16)
            tiles = sp.value_load(nbi[0:1, 1:2], min_val=1, max_val=MAXB // P)
            with sp.Fori(0, tiles) as u:
                hold(sp, s_bt, u * 2 + 2, s_pass)
                sp.dma_start(dr["blk"][bass.ds(u * P, P), :], bwi[:, :]).then_inc(s_row, 16)
                sp.dma_start(dr["blkf"][bass.ds(u * P, P), :], bw[:, 5:6]).then_inc(s_row, 16)
                sp.wait_ge(s_row, u * 32 + 33)
                sp.sem_inc(s_blk, 1)
            sp.wait_ge(s_tab, 16 * (5 + 39))

        @block.scalar
        def _(act):
            act.wait_ge(s_parts, 1)
            act.wait_ge(s_cp, 2 * WT)
            for k in range(3):
                for i in range(3):
                    for c in range(3):
                        act.dma_start(dr["attrp"][12 * k + 4 * i + c, 0:P * EC].rearrange("(p e) -> p e", p=P),
                                     part[:, i, c, :]).then_inc(s_tab, 16)
                    act.dma_start(dr["attrp"][12 * k + 4 * i + 3, 0:P * EC].rearrange("(p e) -> p e", p=P),
                                 ones[:, 0 if i == 0 else 1, :]).then_inc(s_tab, 16)
                act.dma_start(dr["attrp"][12 * k:12 * k + 12, P * EC:EP], tail_b[:, :]).then_inc(s_tab, 16)

        @block.tensor
        def _(pe):
            pe.wait_ge(s_const, 8)
            pe.wait_ge(s_ends, 1)
            nc.tensor.transpose(pt[0:1, 0:P], ends[:, 0:1], ident[:, :])
            nc.tensor.transpose(pt[0:1, P:2 * P], ends[:, 1:2], ident[:, :]).then_inc(s_pe, 1)
            pe.wait_ge(s_scan, 1)
            nc.tensor.matmul(pb[:, 0:1], erow[0:1, 2, 0:P], allone[0:1, 0:1], start=True, stop=True)
            nc.tensor.matmul(pb[:, 1:2], erow[0:1, 3, 0:P], allone[0:1, 0:1], start=True, stop=True).then_inc(s_pe, 1)
            pe.wait_ge(s_final, 1)
            nc.tensor.matmul(pc[:, 0:P], ends[:, 2:3].to_broadcast([P, P]), ident[:, :], start=True, stop=True)
            nc.tensor.matmul(pc[:, P:2 * P], ends[:, 3:4].to_broadcast([P, P]), ident[:, :], start=True, stop=True).then_inc(s_pe, 1)
            pe.wait_ge(s_nb, 1)
            nc.tensor.matmul(pt[:, 0:WT], upper[:, :], nb[:, 3, :], start=True, stop=True)
            nc.tensor.matmul(pt[:, 8:8 + WT], allone[:, :], nb[:, 3, :], start=True, stop=True).then_inc(s_pe, 1)
            pe.wait_ge(s_cum, 1)
            for t in range(WT):
                mm = nc.tensor.matmul(pb[:, t * P:(t + 1) * P], cum[:, t:t + 1].to_broadcast([P, P]), ident[:, :],
                                      start=True, stop=True)
            mm.then_inc(s_pe, 1)

        @block.vector
        def _(v):
            steps = [0]

            def done(ins):
                steps[0] += 1
                ins.then_inc(s_chain, 1)
                v.wait_ge(s_chain, steps[0])

            nc.vector.memset(dst_i[:, :], PAD_DST).then_inc(s_pad, 1)
            nc.vector.memset(src_i[:, :], 0).then_inc(s_pad, 1)
            nc.vector.memset(attr[:, :, :], 0.0).then_inc(s_pad, 1)
            nc.vector.memset(tail_i[:, :], 0).then_inc(s_pad, 1)
            nc.vector.memset(tail_b[:, :], 0.0).then_inc(s_pad, 1)
            nc.vector.memset(ones[:, 0, :], 1.0).then_inc(s_pad, 1)
            done(nc.vector.memset(ones[:, 1, :], 0.0))
            v.wait_ge(s_in, 64)
            done(nc.vector.tensor_copy(dst_f[:, :], dst_i[:, :]))
            done(nc.vector.tensor_tensor_scan(pmax[:, :], dst_f[:, :], dst_f[:, :], -1.0, ALU.max, ALU.max))
            done(nc.vector.tensor_tensor_scan(smin[:, ::-1], dst_f[:, ::-1], dst_f[:, ::-1], float(PAD_DST), ALU.min, ALU.min))
            done(nc.vector.tensor_copy(ends[:, 0:1], pmax[:, EC - 1:EC]))
            nc.vector.tensor_copy(ends[:, 1:2], smin[:, 0:1]).then_inc(s_ends, 1)
            v.wait_ge(s_pe, 1)
            done(nc.vector.memset(erow[:, :, :], -1.0))
            done(nc.vector.memset(erow[0:1, 3, :], float(PAD_DST)))
            done(nc.vector.tensor_copy(erow[0:1, 0, 0:P], pt[0:1, 0:P]))
            done(nc.vector.tensor_copy(erow[0:1, 1, 0:P], pt[0:1, P:2 * P]))
            done(nc.vector.tensor_tensor_scan(erow[0:1, 2, 1:P + 1], erow[0:1, 0, 0:P], erow[0:1, 0, 0:P], -1.0, ALU.max, ALU.max))
            nc.vector.tensor_tensor_scan(erow[0:1, 3, P - 2::-1], erow[0:1, 1, P - 1:0:-1], erow[0:1, 1, P - 1:0:-1],
                                         float(PAD_DST), ALU.min, ALU.min).then_inc(s_scan, 1)
            v.wait_ge(s_pe, 2)
            done(nc.vector.tensor_copy(bw[:, 0:2], pb[:, 0:2]))
            done(nc.vector.tensor_scalar(pmax[:, :], pmax[:, :], bw[:, 0:1], None, ALU.max))
            done(nc.vector.tensor_scalar(smin[:, :], smin[:, :], bw[:, 1:2], None, ALU.min))
            done(nc.vector.tensor_copy(ends[:, 2:3], pmax[:, EC - 1:EC]))
            nc.vector.tensor_copy(ends[:, 3:4], smin[:, EC - 1:EC]).then_inc(s_final, 1)
            v.wait_ge(s_pe, 3)
            v.wait_ge(s_const, 8)
            done(nc.vector.tensor_copy(bnd[:, 0, :], pc[:, 0:P]))
            done(nc.vector.tensor_copy(bnd[:, 1, :], pc[:, P:2 * P]))
            for s in range(2):
                for t in range(WT):
                    done(nc.vector.tensor_scalar(junk[:, 0:P], bnd[:, s, :], thr[:, s, t:t + 1], 0.0, ALU.is_lt, ALU.add,
                                                 accum_out=cnt[:, s, t:t + 1]))
            done(nc.vector.tensor_scalar(cnt[:, :, :], cnt[:, :, :], float(P - 1), None, ALU.min))
            nc.vector.tensor_copy(rix[:, :, :], cnt[:, :, :]).then_inc(s_row, 1)
            at = attr[:, :, :].rearrange("p e c -> p c e")
            v.wait_ge(s_attr, 32)

            def split(n):
                if n < 5:
                    if n:
                        v.wait_ge(s_split, n)
                    if n % 2 == 0:
                        ins = nc.vector.tensor_copy(part[:, n // 2, :, :], at if n == 0 else rest[:, :, :])
                    else:
                        ins = nc.vector.tensor_tensor(rest[:, :, :], at if n == 1 else rest[:, :, :], part[:, n // 2, :, :], ALU.subtract)
                    ins.then_inc(s_split if n < 4 else s_parts, 1)

            assert 2 * WT >= 5
            for s in range(2):
                for t in range(WT):
                    split(s * WT + t)
                    v.wait_ge(s_wg, 16 * (s * WT + t + 1))
                    nc.vector.tensor_scalar(junk[:, :], rows[:, 0, :], thr[:, s, t:t + 1], 0.0, ALU.is_lt, ALU.add,
                                            accum_out=lohi[:, s, t:t + 1]).then_inc(s_cp, 1)
            v.wait_ge(s_cp, 2 * WT)
            done(nc.vector.scalar_tensor_tensor(lohi[:, :, :], cnt[:, :, :], float(EC), lohi[:, :, :], ALU.mult, ALU.add))
            done(nc.vector.tensor_tensor(nb[:, 0, :], lohi[:, 1, :], lohi[:, 0, :], ALU.subtract))
            done(nc.vector.tensor_scalar(nb[:, 1, :], nb[:, 0, :], 1.0 / BE, 0.5 - 0.5 / BE, ALU.mult, ALU.add))
            done(nc.vector.tensor_scalar(nb[:, 2, :], nb[:, 1, :], 8388608.0, None, ALU.add))
            done(nc.vector.tensor_scalar(nb[:, 2, :], nb[:, 2, :], -8388608.0, 1.0, ALU.add, ALU.max))
            done(nc.vector.tensor_scalar(valid[:, :], thr[:, 0, :], float(WIN * NW), None, ALU.is_lt))
            nc.vector.tensor_tensor(nb[:, 3, :], nb[:, 2, :], valid[:, :], ALU.mult).then_inc(s_nb, 1)
            v.wait_ge(s_nb, 1)
            v.wait_ge(s_pe, 4)
            done(nc.vector.memset(off[:, 0:1], 0.0))
            for t in range(1, WT):
                done(nc.vector.tensor_tensor(off[:, t:t + 1], off[:, t - 1:t], pt[:, 7 + t:8 + t], ALU.add))
            done(nc.vector.tensor_tensor(cum[:, :], off[:, :], pt[:, 0:WT], ALU.add))
            done(nc.vector.tensor_copy(win[:, :, 0], lohi[:, 0, :]))
            done(nc.vector.tensor_tensor(win[:, :, 1], cum[:, :], nb[:, 3, :], ALU.subtract))
            v.sem_inc(s_cum, 1)
            v.wait_ge(s_pe, 5)
            done(nc.vector.tensor_copy(cumrow[:, :], pb[:, 0:WT * P]))
            last = cumrow[0:1, WT * P - 1:WT * P]
            rnd = lambda o, i, m, a: (done(nc.vector.tensor_scalar(o, i, m, a, ALU.mult, ALU.add)),
                                      done(nc.vector.tensor_scalar(o, o, 8388608.0, None, ALU.add)),
                                      done(nc.vector.tensor_scalar(o, o, -8388608.0, None, ALU.add)))
            rnd(nbf[0:1, 0:1], last, 1.0 / UN, 0.5 - 0.5 / UN - 2.0 / UN)
            rnd(nbf[0:1, 1:2], last, 1.0 / P, 0.5 - 0.5 / P + (UN + 5.0) / P)
            done(nc.vector.tensor_copy(nbf[0:1, 2:3], last))
            done(nc.vector.tensor_copy(nbf[0:1, 3:4], last))
            done(nc.vector.tensor_copy(nbi[0:1, :], nbf[0:1, :]))
            v.sem_inc(s_step, 1)
            tiles = v.value_load(nbi[0:1, 1:2], min_val=1, max_val=MAXB // P)
            K = 8
            with v.Fori(0, tiles) as u:
                nc.vector.tensor_scalar(junk[:, 0:WT * P], cumrow[:, :], bcol[:, 0:1], 0.0, ALU.is_le, ALU.add,
                                        accum_out=bw[:, 2:3]).then_inc(s_tile, 1)
                v.wait_ge(s_tile, u * K + 1)
                nc.vector.tensor_scalar(bw[:, 2:3], bw[:, 2:3], float(NW), None, ALU.min).then_inc(s_tile, 1)
                v.wait_ge(s_tile, u * K + 2)
                nc.vector.tensor_copy(wi[:, :], bw[:, 2:3]).then_inc(s_bt, 1)
                v.wait_ge(s_wq, u * 16 + 16)
                nc.vector.tensor_tensor(bw[:, 3:4], bcol[:, 0:1], winb[:, 1:2], ALU.subtract).then_inc(s_tile, 1)
                v.wait_ge(s_tile, u * K + 3)
                nc.vector.scalar_tensor_tensor(bw[:, 4:5], bw[:, 3:4], float(BE), winb[:, 0:1], ALU.mult, ALU.add).then_inc(s_tile, 1)
                nc.vector.tensor_scalar(bw[:, 5:6], bw[:, 3:4], 0.0, MASKED, ALU.is_equal, ALU.mult).then_inc(s_tile, 1)
                nc.vector.tensor_copy(bwi[:, 0:1], bw[:, 2:3]).then_inc(s_tile, 1)
                v.wait_ge(s_tile, u * K + 6)
                nc.vector.tensor_copy(bwi[:, 1:2], bw[:, 4:5]).then_inc(s_tile, 1)
                nc.vector.tensor_scalar(bcol[:, 0:1], bcol[:, 0:1], float(P), None, ALU.add).then_inc(s_tile, 1)
                v.wait_ge(s_tile, u * K + 8)
                v.sem_inc(s_bt, 1)
                v.wait_ge(s_blk, u + 1)


def node_phase(nc, io, dr, layer):
    first = layer == 0
    with ExitStack() as ctx:
        sb = lambda n, s, d: ctx.enter_context(nc.sbuf_tensor(f"n{layer}_" + n, s, d))
        ps = lambda n, s: ctx.enter_context(nc.psum_tensor(f"n{layer}_" + n, s, F32))
        sem = semaphores(nc, ctx, f"n{layer}_")
        U = 7
        xs = sb("xs", [P, NT, D], F32)
        st = sb("st", [P, NT, 6], F32)
        mean = sb("mean", [P, NT], F32)
        var = sb("var", [P, NT], F32)
        dif = sb("dif", [P, NT], F32)
        std = sb("std", [P, NT], F32)
        rstd = sb("rstd", [P, NT], F32)
        w_in = sb("w_in", [P, 2, D], F32)
        w = sb("w", [P, 2, D], F32)
        avec = sb("avec", [P, 2, 2], F32)
        amask = sb("amask", [P, 2, HEADS], F32)
        amat = sb("amat", [P, 2, 2 * HEADS], F32)
        ident = sb("ident", [P, P], F32)
        ncol = sb("ncol", [P, NT], F32)
        eps = sb("eps", [P, 1], F32)
        xg = sb("xg", [P, U, D], F32)
        xt = sb("xt", [P, U, 2, P], F32)
        ht = sb("ht", [P, U, 2, P], F32)
        row = sb("row", [P, U, ROW], F32)
        wcol = sb("wcol", [P, U, HEADS, 2], F32)
        ps_x = ps("ps_x", [P, 2, 512])
        ps_h = ps("ps_h", [P, 2, 512])
        ps_t = ps("ps_t", [P, 2, 512])
        ps_a = ps("ps_a", [P, 2, 512])
        s_x = [sem(f"x{c}") for c in range(U)]
        s_w, s_const, s_zero, s_stat, s_var, s_std, s_xn, s_chain = (sem(n) for n in ("w", "const", "zero", "stat", "var", "std", "xn", "chain"))
        s_wt, s_wts, s_amat, s_xt, s_xts, s_h, s_hts, s_hrow, s_a, s_acp, s_pass, s_passp, s_xg, s_pa = (
            sem(n) for n in ("wt", "wts", "amat", "xt", "xts", "h", "hts", "hrow", "a", "acp", "pass", "passp", "xg", "pa"))
        s_st = [sem(f"st{k}") for k in range(U)]
        a_names = ("L0_gnn_a_src", "L0_gnn_a_dst") if first else ("L1_gnn_attn_l", "L1_gnn_attn_r")
        n_st = 16 * (3 if first else 2)
        slot = lambda k: k % 2
        left = lambda i, k: i * U + (k + 1 if k else 2)
        block = ctx.enter_context(nc.Block())

        @block.sync
        def _(sp):
            sp.dma_start(w_in[:, :, :], io["L0_gnn_W" if first else "L1_gnn_W"].rearrange("(k p) n -> p k n", p=P)).then_inc(s_w, 16)
            with nc.allow_non_contiguous_dma(reason="attention vectors as columns, once"):
                for i, name in enumerate(a_names):
                    v = io[name] if first else io[name][0]
                    sp.dma_start(avec[:, :, i], v.rearrange("(k g) d -> (g d) k", k=2)).then_inc(s_w, 16)
            for c in range(U):
                if first and c == U - 1:
                    sp.wait_ge(s_zero, 1)
                    full = (NT - 1) - c * U
                    sp.dma_start(xs[:, c * U:NT - 1, :], io["x"][c * U * P:(NT - 1) * P, :].rearrange("(t p) d -> p t d", p=P)).then_inc(s_x[c], 16)
                    sp.dma_start(xs[0:N - (NT - 1) * P, NT - 1, :], io["x"][(NT - 1) * P:N, :]).then_inc(s_x[c], 16)
                else:
                    src = io["x"] if first else dr["x2"]
                    sp.dma_start(xs[:, c * U:(c + 1) * U, :],
                                 src[c * U * P:(c + 1) * U * P, :].rearrange("(t p) d -> p t d", p=P)).then_inc(s_x[c], 16)
            for k in range(U):
                sp.sem_inc(s_st[k], 16)
            with sp.Fori(0, NT // U) as i:
                for k in range(U):
                    hold(sp, s_hrow, i * U + (k + 3), s_pass)
                    hold(sp, s_acp, i * U + (k + 3), s_pass)
                    n0 = i * (U * P) + k * P
                    sp.dma_start(dr["table"][bass.ds(n0, P), :], row[:, k, :]).then_inc(s_st[k], 16)
                    sp.dma_start(dr["wcol"][bass.ds(n0, P), :], wcol[:, k, :, :].rearrange("p h c -> p (h c)")).then_inc(s_st[k], 16)
                    if first:
                        hold(sp, s_hts, i * U + (k + 3), s_pass)
                        sp.dma_start(dr["hT"].rearrange("(c p) n -> p c n", p=P)[:, :, bass.ds(n0, P)], ht[:, k, :, :]).then_inc(s_st[k], 16)
            for k in range(U):
                sp.wait_ge(s_st[k], n_st * (NT // U) + 16)

        @block.gpsimd
        def _(pool):
            nc.gpsimd.memset(ident[:, :], 0.0).then_inc(s_const, 1)
            nc.gpsimd.memset(amask[:, :, :], 1.0).then_inc(s_const, 1)
            pool.wait_ge(s_const, 2)
            nc.gpsimd.affine_select(out=ident[:, :], in_=ident[:, :], compare_op=ALU.not_equal, fill=1.0, base=0,
                                    pattern=[[-1, P]], channel_multiplier=1).then_inc(s_const, 1)
            nc.gpsimd.affine_select(out=amask[:, :, :], in_=amask[:, :, :], compare_op=ALU.is_ge, fill=0.0, base=0,
                                    pattern=[[P, 2], [-DH, HEADS]], channel_multiplier=1).then_inc(s_const, 1)
            pool.wait_ge(s_const, 4)
            nc.gpsimd.affine_select(out=amask[:, :, :], in_=amask[:, :, :], compare_op=ALU.is_ge, fill=0.0, base=DH - 1,
                                    pattern=[[-P, 2], [DH, HEADS]], channel_multiplier=-1).then_inc(s_const, 1)
            nc.gpsimd.iota(ncol[:, :], pattern=[[P, NT]], base=0, channel_multiplier=1,
                           allow_small_or_imprecise_dtypes=True).then_inc(s_const, 1)

        @block.tensor
        def _(pe):
            pe.wait_ge(s_const, 6)
            pe.wait_ge(s_w, 48)
            if first:
                for o in range(2):
                    for i in range(2):
                        mm = nc.tensor.transpose(ps_x[:, i, o * P:(o + 1) * P], w_in[:, o, i * P:(i + 1) * P], ident[:, :])
                mm.then_inc(s_wt, 1)
            pe.wait_ge(s_wts, 1)
            pe.wait_ge(s_amat, 1)

            def turn(i, k):
                hold(pe, s_xg, i * U + (k + 1), s_passp)
                hold(pe, s_xts, left(i, k), s_passp)
                for c in range(2):
                    mm = nc.tensor.transpose(ps_x[:, slot(k), c * P:(c + 1) * P], xg[:, k, c * P:(c + 1) * P], ident[:, :])
                mm.then_inc(s_xt, 1)

            def project(i, k):
                hold(pe, s_xts, i * U + (k + 3), s_passp)
                hold(pe, s_hrow, left(i, k), s_passp)
                hold(pe, s_hts, left(i, k), s_passp)
                for c in range(2):
                    nc.tensor.matmul(ps_h[:, slot(k), 0:D], xt[:, k, c, :], w[:, c, :], start=(c == 0), stop=(c == 1))
                for o in range(2):
                    for c in range(2):
                        mm = nc.tensor.matmul(ps_t[:, slot(k), o * P:(o + 1) * P], w[:, c, o * P:(o + 1) * P], xt[:, k, c, :],
                                              start=(c == 0), stop=(c == 1))
                mm.then_inc(s_h, 1)

            def logits(i, k):
                hold(pe, s_hts, i * U + (k + 3), s_passp)
                hold(pe, s_acp, left(i, k), s_passp)
                for o in range(2):
                    mm = nc.tensor.matmul(ps_a[:, slot(k), 0:2 * HEADS], ht[:, k, o, :], amat[:, o, :], start=(o == 0), stop=(o == 1))
                mm.then_inc(s_a, 1)

            with pe.Fori(0, NT // U) as i:
                turn(i, 0)
                turn(i, 1)
                for k in range(U):
                    project(i, k)
                    if k + 2 < U:
                        turn(i, k + 2)
                    if k:
                        logits(i, k - 1)
                logits(i, U - 1)

        @block.scalar
        def _(act):
            if first:
                act.wait_ge(s_wt, 1)
                nc.scalar.copy(w[:, :, :], ps_x[:, 0:2, 0:D]).then_inc(s_wts, 1)
            else:
                act.wait_ge(s_w, 48)
                nc.scalar.copy(w[:, :, :], w_in[:, :, :]).then_inc(s_wts, 1)
            act.wait_ge(s_var, 1)
            nc.scalar.activation(std[:, :], var[:, :], ACT.Sqrt, bias=eps[:, 0:1]).then_inc(s_std, 1)
            act.wait_ge(s_wts, 1)
            act.sem_inc(s_xts, 2)
            act.sem_inc(s_hrow, 2)

            def copy_x(i, k):
                hold(act, s_xt, i * U + (k + 1), s_pa)
                nc.scalar.copy(xt[:, k, :, :], ps_x[:, slot(k), 0:D].rearrange("p (c n) -> p c n", c=2)).then_inc(s_xts, 1)

            def copy_h(i, k):
                hold(act, s_h, i * U + (k + 1), s_pa)
                hold(act, s_st[k], i * n_st + 16, s_pa)
                nc.scalar.copy(row[:, k, 0:D], ps_h[:, slot(k), 0:D]).then_inc(s_hrow, 1)

            with act.Fori(0, NT // U) as i:
                copy_x(i, 0)
                copy_x(i, 1)
                for k in range(U):
                    if k + 2 < U:
                        copy_x(i, k + 2)
                    copy_h(i, k)

        @block.vector
        def _(v):
            steps = [0]

            def done(ins):
                steps[0] += 1
                ins.then_inc(s_chain, 1)
                v.wait_ge(s_chain, steps[0])

            done(nc.vector.memset(eps[:, :], EPS))
            if first:
                nc.vector.memset(xs[:, NT - 1, :], 0.0).then_inc(s_zero, 1)
            v.wait_ge(s_const, 6)
            v.wait_ge(s_w, 48)
            for k in range(2):
                for i in range(2):
                    done(nc.vector.tensor_scalar(amat[:, k, i * HEADS:(i + 1) * HEADS], amask[:, k, :], avec[:, k, i:i + 1], None, ALU.mult))
            v.sem_inc(s_amat, 1)
            for c in range(U):
                v.wait_ge(s_x[c], 32 if first and c == U - 1 else 16)
                for t in range(c * U, (c + 1) * U):
                    nc.vector.bn_stats(st[:, t, :], xs[:, t, :]).then_inc(s_stat, 1)
            v.wait_ge(s_stat, NT)
            done(nc.vector.tensor_tensor(mean[:, :], st[:, :, 1], st[:, :, 4], ALU.add))
            done(nc.vector.tensor_scalar(mean[:, :], mean[:, :], 0.5, None, ALU.mult))
            done(nc.vector.tensor_tensor(dif[:, :], st[:, :, 1], st[:, :, 4], ALU.subtract))
            done(nc.vector.scalar_tensor_tensor(dif[:, :], dif[:, :], 0.25, dif[:, :], ALU.mult, ALU.mult))
            done(nc.vector.tensor_tensor(var[:, :], st[:, :, 2], st[:, :, 5], ALU.add))
            done(nc.vector.scalar_tensor_tensor(var[:, :], var[:, :], 1.0 / D, dif[:, :], ALU.mult, ALU.add))
            v.sem_inc(s_var, 1)
            v.wait_ge(s_std, 1)
            done(nc.vector.reciprocal(rstd[:, :], std[:, :]))
            v.sem_inc(s_hts, 2)
            v.sem_inc(s_acp, 2)

            def normalise(i, k):
                t = i * U + k
                nc.vector.tensor_scalar(xg[:, k, :], xs[:, bass.ds(t, 1), :], mean[:, bass.ds(t, 1)], rstd[:, bass.ds(t, 1)],
                                        ALU.subtract, ALU.mult).then_inc(s_xg, 1)

            def copy_ht(i, k):
                hold(v, s_h, i * U + (k + 1), s_pass)
                hold(v, s_st[k], i * n_st + 16, s_pass)
                nc.vector.tensor_copy(ht[:, k, :, :], ps_t[:, slot(k), 0:D].rearrange("p (c n) -> p c n", c=2)).then_inc(s_hts, 1)

            def copy_a(i, k):
                hold(v, s_a, i * U + (k + 1), s_pass)
                nc.vector.tensor_copy(wcol[:, k, :, 0], ncol[:, bass.ds(i * U + k, 1)].to_broadcast([P, HEADS]))
                nc.vector.tensor_copy(wcol[:, k, :, 1], ps_a[:, slot(k), HEADS:2 * HEADS])
                nc.vector.tensor_copy(row[:, k, D:ROW], ps_a[:, slot(k), 0:HEADS]).then_inc(s_acp, 1)

            with v.Fori(0, NT // U) as i:
                for k in range(U):
                    normalise(i, k)
                for k in range(U):
                    copy_ht(i, k)
                    if k:
                        copy_a(i, k - 1)
                copy_a(i, U - 1)


def edge_phase(nc, io, dr, layer):
    first = layer == 0
    with ExitStack() as ctx:
        sb = lambda n, s, d: ctx.enter_context(nc.sbuf_tensor(f"e{layer}_" + n, s, d))
        ps = lambda n, s: ctx.enter_context(nc.psum_tensor(f"e{layer}_" + n, s, F32))
        sem = semaphores(nc, ctx, f"e{layer}_")
        ident = sb("ident", [P, P], F32)
        hmask = sb("hmask", [P, 2, HEADS], F32)
        own_i = sb("own_i", [P, HEADS], I32)
        prow_i = sb("prow_i", [P, 1], I32)
        own = sb("own", [P, HEADS], F32)
        prow = sb("prow", [P, 1], F32)
        dstb = sb("dstb", [P, UN, BE], I32)
        idx = sb("idx", [P, UN, CH], I32)
        wc = sb("wc", [P, UN, 2], F32)
        nf = sb("nf", [P, UN], F32)
        htw = sb("htw", [P, UN, 2, WIN], F32)
        at = sb("at", [K_ENC, UN, BE], BF16)
        rows = sb("rows", [P, UN, CH, ROW], F32)
        arep = sb("arep", [P, 2, CH, WIN, HEADS], F32)
        encr = sb("encr", [P, 2, 2, BE], F32)
        bd = sb("bd", [P, 2, 2, P], F32)
        mask = sb("mask", [P, 2, BE], F32)
        x = sb("x", [P, BE], F32)
        z = sb("z", [P, BE], F32)
        lk = sb("lk", [P, 2, BE], F32)
        prob = sb("prob", [P, 2, BE], F32)
        pt = sb("pt", [P, 2, CH * P], F32)
        mx = sb("mx", [P, 4], F32)
        nmo = sb("nmo", [P, UN], F32)
        negm = sb("negm", [P, UN], F32)
        corr = sb("corr", [P, UN], F32)
        denb = sb("denb", [P, UN], F32)
        den = sb("den", [P, 3], F32)
        dia = sb("dia", [P, HEADS, DH], F32)
        dg = sb("dg", [P, DH], F32)
        acc = sb("acc", [P, DH], F32)
        res = sb("res", [P, UN, DH], F32)
        nbi = sb("nbi", [1, 4], I32)
        tab = sb("tab", [1, 2 * UN, 2], I32)
        w_st = sb("w_st", [4, D], F32)
        w_rest = sb("w_rest", [4, D], F32)
        w_part = sb("w_part", [4, 3, D], BF16)
        w_enc = sb("w_enc", [K_ENC, D], BF16)
        ps_e = ps("ps_e", [P, 1024])
        ps_s = ps("ps_s", [P, 1024])
        ps_t = ps("ps_t", [P, 1024])
        ps_o = ps("ps_o", [P, 2, 512])
        s_nb, s_const, s_w, s_wp, s_we, s_init = (sem(n) for n in ("nb", "const", "w", "wp", "we", "init"))
        s_load = [sem(f"load{k}") for k in range(UN)]
        s_rows = [sem(f"rows{k}") for k in range(UN)]
        s_enc, s_relu, s_bd, s_s, s_a, s_lk, s_exp, s_t, s_pt, s_o, s_fin, s_out = (
            sem(n) for n in ("enc", "relu", "bd", "s", "a", "lk", "exp", "t", "pt", "o", "fin", "out"))
        s_rep, s_tab = sem("rep"), sem("tab")
        s_v, s_pv, s_pp, s_pa, s_ps, s_pg = (sem(n) for n in ("v", "pv", "pp", "pa", "ps", "pg"))
        n_load = 16 * (6 if first else 4)
        MAXS = MAXB // UN - 2

        def chunks(row):
            return row.rearrange("p (j e) -> p j e", j=CH)

        def banked(t):
            return t[:, 0:CH * P].rearrange("p (j e) -> p j e", j=CH)[:, :, 0:CK]

        def steps_of(eng):
            eng.wait_ge(s_nb, 16)
            return eng.value_load(nbi[0:1, 0:1], min_val=1, max_val=MAXS)

        block = ctx.enter_context(nc.Block())

        @block.sync
        def _(sp):
            sp.dma_start(nbi[0:1, :], dr["nblk"][:, :]).then_inc(s_nb, 16)
            if first:
                with nc.allow_non_contiguous_dma(reason="a 256 x 3 matrix transposed, once"):
                    sp.dma_start(w_st[0:3, :], io["L0_gnn_edge_W"].rearrange("o c -> c o")).then_inc(s_w, 16)
                sp.dma_start(w_st[3:4, :], io["L0_gnn_edge_b"].rearrange("(a o) -> a o", a=1)).then_inc(s_w, 16)
                sp.wait_ge(s_wp, 1)
                for k in range(3):
                    for i in range(3):
                        sp.dma_start(w_enc[12 * k + 4 * i:12 * k + 4 * i + 4, :], w_part[:, k, :]).then_inc(s_we, 16)

            def fetch(step):
                sp.dma_start(tab[0:1, :, :].rearrange("a r c -> a (r c)"),
                             dr["blk"][bass.ds(step * UN, 2 * UN), :].rearrange("(a r) c -> a (r c)", a=1)).then_inc(s_tab, 16)
                hold(sp, s_tab, step * 16 + 16, s_ps)

            def load(b, k, r):
                w = sp.value_load(tab[0:1, r, 0:1], min_val=0, max_val=NW)
                e = sp.value_load(tab[0:1, r, 1:2], min_val=0, max_val=EP - BE)
                sp.dma_start(idx[0:CK, k, :], dr["srcp"][bass.ds(e, BE)].rearrange("(p j) -> p j", j=CH)).then_inc(s_load[k], 16)
                sp.dma_start(dstb[:, k, :], dr["dstp"][bass.ds(e, BE)].partition_broadcast(P)).then_inc(s_load[k], 16)
                sp.dma_start(wc[:, k, :], dr["wcol"].rearrange("(w t) (h c) -> w (t h) c", t=WIN, c=2)[bass.ds(w, 1), :, :]
                             .rearrange("a p c -> (a p) c")).then_inc(s_load[k], 16)
                sp.dma_start(nf[:, k:k + 1], dr["blkf"][bass.ds(b, 1), 0:1].rearrange("a c -> (a c)").partition_broadcast(P)).then_inc(s_load[k], 16)
                if first:
                    sp.dma_start(at[:, k, :], dr["attrp"][:, bass.ds(e, BE)]).then_inc(s_load[k], 16)
                    sp.dma_start(htw[:, k, :, :], dr["hT"].rearrange("(c p) n -> p c n", p=P)[:, :, bass.ds(w * WIN, WIN)]).then_inc(s_load[k], 16)

            def store(b, k):
                w = sp.value_load(tab[0:1, k, 0:1], min_val=0, max_val=NW)
                hold(sp, s_out, b * 16 + 16 * UN, s_ps)
                hold(sp, s_fin, b + 3, s_ps)
                sp.dma_start(dr["agg"].rearrange("(w t) (h c) -> w (t h) c", t=WIN, c=DH)[bass.ds(w, 1), :, :]
                             .rearrange("a p c -> (a p) c"), res[:, k, :]).then_inc(s_out, 16)

            fetch(0)
            for k in range(UN):
                load(k, k, k)
            sp.sem_inc(s_out, 16 * UN)
            steps = steps_of(sp)
            with sp.Fori(0, steps) as i:
                for k in range(UN):
                    hold(sp, s_lk, i * UN + (k + 1), s_ps)
                    load(i * UN + (UN + k), k, UN + k)
                    store(i * UN + k, k)
                fetch(i + 1)
            for k in range(2):
                store(steps * UN + k, k)
            for k in range(UN):
                hold(sp, s_load[k], steps * n_load + n_load, s_ps)
            hold(sp, s_out, steps * (16 * UN) + 16 * (UN + 2), s_ps)

        @block.gpsimd
        def _(pool):
            nc.gpsimd.memset(ident[:, :], 0.0).then_inc(s_const, 1)
            nc.gpsimd.memset(hmask[:, :, :], 1.0).then_inc(s_const, 1)
            pool.wait_ge(s_const, 2)
            nc.gpsimd.affine_select(out=ident[:, :], in_=ident[:, :], compare_op=ALU.not_equal, fill=1.0, base=0,
                                    pattern=[[-1, P]], channel_multiplier=1).then_inc(s_const, 1)
            nc.gpsimd.affine_select(out=hmask[:, :, :], in_=hmask[:, :, :], compare_op=ALU.is_ge, fill=0.0, base=0,
                                    pattern=[[P, 2], [-DH, HEADS]], channel_multiplier=1).then_inc(s_const, 1)
            pool.wait_ge(s_const, 4)
            nc.gpsimd.affine_select(out=hmask[:, :, :], in_=hmask[:, :, :], compare_op=ALU.is_ge, fill=0.0, base=DH - 1,
                                    pattern=[[-P, 2], [DH, HEADS]], channel_multiplier=-1).then_inc(s_const, 1)
            nc.gpsimd.iota(prow_i[:, :], pattern=[[0, 1]], base=0, channel_multiplier=1).then_inc(s_const, 1)
            nc.gpsimd.iota(own_i[:, :], pattern=[[1, HEADS]], base=0, channel_multiplier=0).then_inc(s_const, 1)

            def gather(k, turns):
                hold(pool, s_load[k], turns * n_load + n_load, s_pg)
                for j in range(CH):
                    pool.indirect_dma_start(rows[0:CK, k, j, :], None, dr["table"][:, :],
                                            bass.IndirectOffsetOnAxis(idx[0:CK, k, j:j + 1], 0)).then_inc(s_rows[k], 16)

            for k in range(UN):
                pool.wait_ge(s_load[k], n_load)
                for j in range(CH):
                    pool.indirect_dma_start(rows[0:CK, k, j, :], None, dr["table"][:, :],
                                            bass.IndirectOffsetOnAxis(idx[0:CK, k, j:j + 1], 0)).then_inc(s_rows[k], 16)
            steps = steps_of(pool)
            with pool.Fori(0, steps) as i:
                for k in range(UN):
                    hold(pool, s_o, i * UN + (k + 2), s_pg)
                    gather(k, i + 1)
            for k in range(UN):
                hold(pool, s_rows[k], steps * (16 * CH) + 16 * CH, s_pg)

        @block.tensor
        def _(pe):
            pe.wait_ge(s_const, 7)
            if first:
                pe.wait_ge(s_we, 16 * 9)
            pe.sem_inc(s_o, 1)

            def enc(b, k, turns, half):
                if half == 0:
                    hold(pe, s_load[k], turns * n_load + n_load, s_pp)
                hold(pe, s_relu, b * 2 + (half + 1), s_pp)
                cols = at[:, k, :].rearrange("k (p j) -> k j p", j=CH)
                lhs = w_enc[:, half * P:(half + 1) * P]
                nc.tensor.matmul(banked(ps_e)[:, 0:4, :], lhs, cols[:, 0:4, :], start=True, stop=True)
                nc.tensor.matmul(banked(ps_e)[:, 4, :], lhs, cols[:, 4, :], start=True, stop=True).then_inc(s_enc, 1)

            def score(b, p):
                hold(pe, s_a, b + 1, s_pp)
                if first:
                    hold(pe, s_bd, b + 1, s_pp)
                    for half in range(2):
                        hold(pe, s_relu, b * 2 + (half + 2), s_pp)
                        for c0, c1 in ((0, 4), (4, CH)):
                            nc.tensor.matmul(banked(ps_s)[:, c0:c1, :], bd[:, p, half, :], chunks(encr[:, p, half, :])[:, c0:c1, :],
                                             start=(half == 0), stop=False, skip_group_check=True)
                hold(pe, s_rep, b + 1, s_pp)
                for j in range(CH):
                    mm = nc.tensor.matmul(banked(ps_s)[:, j, :], arep[0:CK, p, j, :, :].rearrange("p t h -> p (t h)"),
                                          ident[0:CK, 0:CK], start=not first, stop=True, skip_group_check=True)
                mm.then_inc(s_s, 1)

            def turn(b, p):
                hold(pe, s_exp, b + 1, s_pp)
                hold(pe, s_pt, b + 1, s_pp)
                for j in range(CH):
                    mm = nc.tensor.transpose(ps_t[0:CK, j * P:(j + 1) * P], prob[:, p, j * CK:(j + 1) * CK], ident[:, :])
                mm.then_inc(s_t, 1)

            def total(b, k, p):
                hold(pe, s_pt, b + 2, s_pp)
                hold(pe, s_fin, b + 1, s_pp)
                for j in range(CH):
                    mm = nc.tensor.matmul(ps_o[:, p, 0:D], pt[0:CK, p, j * P:(j + 1) * P], rows[0:CK, k, j, 0:D],
                                          start=(j == 0), stop=(j == CH - 1))
                mm.then_inc(s_o, 1)

            def encs(b):
                for half in range(2):
                    if first:
                        enc(b, b, 0, half)

            encs(0)
            score(0, 0)
            encs(1)
            score(1, 1)
            encs(2)
            turn(0, 0)
            if not first:
                total(0, 0, 0)
            steps = steps_of(pe)
            with pe.Fori(0, steps) as i:
                for q in range(UN):
                    score(i * UN + (q + 2), q % 2)
                    if first:
                        enc(i * UN + (q + 3), (q + 3) % UN, i + (q + 3) // UN, 0)
                    turn(i * UN + (q + 1), (q + 1) % 2)
                    if first:
                        total(i * UN + q, q, q % 2)
                        enc(i * UN + (q + 3), (q + 3) % UN, i + (q + 3) // UN, 1)
                    else:
                        total(i * UN + (q + 1), (q + 1) % UN, (q + 1) % 2)
            if first:
                total(steps * UN, 0, 0)
            turn(steps * UN + 1, 1)
            total(steps * UN + 1, 1, 1)

        @block.scalar
        def _(act):
            act.sem_inc(s_relu, 1)
            act.sem_inc(s_pt, 1)

            def relu(b, p, half):
                hold(act, s_enc, b * 2 + (half + 1), s_pa)
                if not isinstance(b, int) and half == 0:
                    hold(act, s_s, b - 1, s_pa)
                nc.scalar.activation(chunks(encr[:, p, half, :]), banked(ps_e), ACT.Relu).then_inc(s_relu, 1)

            def repeat(b, k, turns, p):
                hold(act, s_rows[k], turns * (16 * CH) + 16 * CH, s_pa)
                if not isinstance(b, int):
                    hold(act, s_s, b - 1, s_pa)
                nc.scalar.copy(arep[0:CK, p, :, :, :], rows[0:CK, k, :, D:ROW].unsqueeze(2).to_broadcast([CK, CH, WIN, HEADS])).then_inc(s_rep, 1)

            def copy_t(b, p):
                hold(act, s_t, b + 1, s_pa)
                if not isinstance(b, int):
                    hold(act, s_o, b, s_pa)
                nc.scalar.copy(pt[0:CK, p, :], ps_t[0:CK, 0:CH * P]).then_inc(s_pt, 1)

            def weights(b, p, k):
                hold(act, s_lk, b + 1, s_pa)
                nc.scalar.activation(corr[:, k:k + 1], nmo[:, k:k + 1], ACT.Exp, bias=negm[:, k:k + 1], scale=-1.0)
                nc.scalar.activation(prob[:, p, :], lk[:, p, :], ACT.Exp, bias=negm[:, k:k + 1],
                                     accum_out=denb[:, k:k + 1]).then_inc(s_exp, 1)

            def relus(b, p):
                for half in range(2):
                    if first:
                        relu(b, p, half)

            relus(0, 0)
            repeat(0, 0, 0, 0)
            relus(1, 1)
            repeat(1, 1, 0, 1)
            weights(0, 0, 0)
            act.wait_ge(s_s, 1)
            relus(2, 0)
            copy_t(0, 0)
            repeat(2, 2, 0, 0)
            weights(1, 1, 1)
            steps = steps_of(act)
            with act.Fori(0, steps) as i:
                for q in range(UN):
                    if first:
                        relu(i * UN + (q + 3), (q + 1) % 2, 0)
                    copy_t(i * UN + (q + 1), (q + 1) % 2)
                    repeat(i * UN + (q + 3), (q + 3) % UN, i + (q + 3) // UN, (q + 1) % 2)
                    if first:
                        relu(i * UN + (q + 3), (q + 1) % 2, 1)
                    weights(i * UN + (q + 2), q % 2, (q + 2) % UN)
            copy_t(steps * UN + 1, 1)

        @block.vector
        def _(v):
            nc.vector.memset(acc[:, :], 0.0).then_inc(s_init, 1)
            nc.vector.memset(den[:, :], 0.0).then_inc(s_init, 1)
            nc.vector.memset(negm[:, :], 0.0).then_inc(s_init, 1)
            v.wait_ge(s_const, 7)
            nc.vector.tensor_single_scalar(prow_i[:, :], prow_i[:, :], HEADS - 1, ALU.bitwise_and).then_inc(s_init, 1)
            v.wait_ge(s_init, 4)
            nc.vector.tensor_copy(prow[:, :], prow_i[:, :]).then_inc(s_init, 1)
            nc.vector.tensor_copy(own[:, :], own_i[:, :]).then_inc(s_init, 1)
            v.wait_ge(s_init, 6)
            nc.vector.tensor_scalar(own[:, :], own[:, :], prow[:, 0:1], None, ALU.is_equal).then_inc(s_init, 1)
            v.wait_ge(s_init, 7)
            if first:
                v.wait_ge(s_w, 32)
                nc.vector.tensor_copy(w_part[:, 0, :], w_st[:, :]).then_inc(s_init, 1)
                v.wait_ge(s_init, 8)
                nc.vector.tensor_tensor(w_rest[:, :], w_st[:, :], w_part[:, 0, :], ALU.subtract).then_inc(s_init, 1)
                v.wait_ge(s_init, 9)
                nc.vector.tensor_copy(w_part[:, 1, :], w_rest[:, :]).then_inc(s_init, 1)
                v.wait_ge(s_init, 10)
                nc.vector.tensor_tensor(w_rest[:, :], w_rest[:, :], w_part[:, 1, :], ALU.subtract).then_inc(s_init, 1)
                v.wait_ge(s_init, 11)
                nc.vector.tensor_copy(w_part[:, 2, :], w_rest[:, :]).then_inc(s_wp, 1)
            v.sem_inc(s_a, 1)
            v.sem_inc(s_fin, 2)

            def diagonal(k, turns, p):
                hold(v, s_load[k], turns * n_load + n_load, s_pv)
                for half in range(2):
                    ins = nc.vector.tensor_tensor(bd[:, p, half, :].rearrange("p (t h) -> p t h", h=HEADS),
                                                  htw[:, k, half, :].unsqueeze(2).to_broadcast([P, WIN, HEADS]),
                                                  hmask[:, half, :].unsqueeze(1).to_broadcast([P, WIN, HEADS]), ALU.mult)
                ins.then_inc(s_bd, 1)

            FIN, SCO = 6, 6

            def counted(base):
                n = [0]

                def did(ins):
                    ins.then_inc(s_v, 1)
                    n[0] += 1
                    return base + n[0]
                return n, did

            def need(count):
                hold(v, s_v, count, s_pv)

            def masks(k, turns, p):
                hold(v, s_load[k], turns * n_load + n_load, s_pv)
                return nc.vector.tensor_scalar(mask[:, p, :], dstb[:, k, :], wc[:, k, 0:1], MASKED, ALU.not_equal, ALU.mult)

            def by_chunk(row):
                return row.rearrange("p (e j) -> p j e", j=CH)

            def sums_a(b, p, k, did):
                hold(v, s_o, b + 2, s_pv)
                did(nc.vector.tensor_tensor(dia[:, :, :], ps_o[:, p, 0:D].rearrange("p (h c) -> p h c", h=HEADS),
                                            own[:, :].unsqueeze(2).to_broadcast([P, HEADS, DH]), ALU.mult))
                return did(nc.vector.scalar_tensor_tensor(den[:, 0:1], den[:, 0:1], corr[:, k:k + 1], denb[:, k:k + 1], ALU.mult, ALU.add))

            def sums_b(c_den, did):
                need(c_den)
                did(nc.vector.tensor_reduce(dg[:, :], dia[:, :, :].rearrange("p h c -> p c h"), AX_X, ALU.add))
                return did(nc.vector.tensor_scalar(den[:, 1:2], den[:, 0:1], 1e-10, None, ALU.max))

            def sums_c(c_pos, k, did):
                need(c_pos)
                did(nc.vector.reciprocal(den[:, 2:3], den[:, 1:2]))
                return did(nc.vector.scalar_tensor_tensor(acc[:, :], acc[:, :], corr[:, k:k + 1], dg[:, :], ALU.mult, ALU.add))

            def sums_d(b, c_acc, k):
                need(c_acc)
                hold(v, s_out, b * 16 + 16, s_pv)
                nc.vector.tensor_scalar(res[:, k, :], acc[:, :], den[:, 2:3], None, ALU.mult).then_inc(s_fin, 1)

            def finish(b, p, k, base):
                _, did = counted(base)
                sums_d(b, sums_c(sums_b(sums_a(b, p, k, did), did), k, did), k)

            def step(b, k, turns, p, base, sums):
                n, did = counted(base)
                kn, kp, kf = (k + 1) % UN, (k - 1) % UN, (k - 2) % UN
                inside, behind = sums and not first, sums and first
                if inside:
                    c_den = sums_a(b - 2, p, kf, did)
                did(masks(kn, turns if k + 1 < UN else turns + 1, 1 - p))
                if inside:
                    c_pos = sums_b(c_den, did)
                else:
                    need(base)
                hold(v, s_s, b + 1, s_pv)
                nc.vector.tensor_tensor_reduce(
                    out=chunks(x[:, :]), in0=banked(ps_s), in1=by_chunk(mask[:, p, :]), scale=1.0, scalar=3.0 * MASKED,
                    op0=ALU.add, op1=ALU.max, accum_out=mx[:, 0:1]).then_inc(s_a, 1)
                if inside:
                    c_acc = sums_c(c_pos, kf, did)
                if behind:
                    diagonal(kn, turns if k + 1 < UN else turns + 1, 1 - p)
                hold(v, s_a, b + 2, s_pv)
                c_mx = did(nc.vector.tensor_scalar(mx[:, 1:2], mx[:, 0:1], wc[:, k, 1:2], -1.0, ALU.add, ALU.mult))
                c_z = did(nc.vector.tensor_scalar(z[:, :], x[:, :], wc[:, k, 1:2], 0.2, ALU.add, ALU.mult))
                need(c_mx)
                did(nc.vector.tensor_tensor(nmo[:, k:k + 1], negm[:, kp:kp + 1], nf[:, k:k + 1], ALU.subtract))
                c_lm = did(nc.vector.scalar_tensor_tensor(mx[:, 2:3], mx[:, 1:2], 0.2, mx[:, 1:2], ALU.mult, ALU.min))
                if inside:
                    sums_d(b - 2, c_acc, kf)
                need(c_z)
                did(nc.vector.scalar_tensor_tensor(lk[:, p, :], x[:, :], wc[:, k, 1:2], z[:, :], ALU.add, ALU.max))
                need(c_lm)
                nc.vector.scalar_tensor_tensor(negm[:, k:k + 1], mx[:, 2:3], -FLOOR, nmo[:, k:k + 1], ALU.min, ALU.min).then_inc(s_lk, 1)
                assert n[0] == SCO + (FIN if inside else 0), n
                if behind:
                    finish(b - 2, p, kf, base + SCO)

            if first:
                diagonal(0, 0, 0)
                diagonal(1, 0, 1)
            masks(0, 0, 0).then_inc(s_v, 1)
            step(0, 0, 0, 0, 1, False)
            if first:
                diagonal(2, 0, 0)
            step(1, 1, 0, 1, 1 + SCO, False)
            steps = steps_of(v)
            before = 1 + 2 * SCO
            with v.Fori(0, steps) as i:
                for q in range(UN):
                    step(i * UN + (q + 2), (q + 2) % UN, i + (q + 2) // UN, q % 2,
                         i * (UN * (FIN + SCO)) + (q * (FIN + SCO) + before), True)
            for q in range(2):
                finish(steps * UN + q, q, q, steps * (UN * (FIN + SCO)) + (before + q * FIN))


TB = 256
SUB = TB // P
EXP, FF = 8, 1024
FC = FF // P
DC = D // P
CAP = -(-(5 * N) // (4 * EXP))
R = 7
FMAX = 3.4028234e38


def max_blocks(top):
    return (top * N + EXP * (TB - 1)) // TB


def ffn_phases(nc, io, dr, layer, src, out):
    first = layer == 0
    top = 2 if first else 1
    nblk_max = max_blocks(top)
    n_slot = (nblk_max + 4) * TB
    n_tab = nblk_max + 8
    xb, yb = dr["xb"], dr["yb"]
    names = dict(zip(("wr", "br", "w1", "b1", "w2", "b2"),
                     ("L0_ffn_Wr", "L0_ffn_br", "L0_ffn_W1", "L0_ffn_b1", "L0_ffn_W2", "L0_ffn_b2") if first else
                     ("L1_ffn_gate_w", "L1_ffn_gate_b", "L1_ffn_w1", "L1_ffn_b1", "L1_ffn_w2", "L1_ffn_b2")))
    with ExitStack() as outer:
        keep = lambda n, s, d: outer.enter_context(nc.sbuf_tensor(f"f{layer}_" + n, s, d))
        xs = keep("xs", [P, NT, D], F32)
        slot_i = keep("slot_i", [P, 2, NT], I32)
        wgt = keep("wgt", [P, 2, NT], F32)
        tab_i = keep("tab_i", [1, n_tab], I32)
        cnt_i = keep("cnt_i", [1, 4], I32)

        with ExitStack() as ctx:
            sb = lambda n, s, d: ctx.enter_context(nc.sbuf_tensor(f"r{layer}_" + n, s, d))
            ps = lambda n, s: ctx.enter_context(nc.psum_tensor(f"r{layer}_" + n, s, F32))
            sem = semaphores(nc, ctx, f"r{layer}_")
            ag = sb("ag", [P, 2, R, D], F32)
            bias = sb("bias", [P, D], F32)
            xt = sb("xt", [P, NT, D], F32)
            st = sb("st", [P, NT, 6], F32)
            lnv = sb("lnv", [P, 5, NT], F32)
            eps = sb("eps", [P, 1], F32)
            ident = sb("ident", [P, P], F32)
            upper = sb("upper", [P, P], F32)
            allone = sb("allone", [P, P], F32)
            wr = sb("wr", [P, DC, EXP], F32)
            br = sb("br", [P, EXP], F32)
            xg = sb("xg", [P, R, D], F32)
            xT = sb("xT", [P, R, DC, P], F32)
            zero = sb("zero", [P, 2048], F32)
            lg = sb("lg", [P, NT, EXP], F32)
            pr = sb("pr", [P, NT, EXP], F32)
            tmp = sb("tmp", [P, NT, EXP], F32)
            oh = sb("oh", [P, 2, NT, EXP], F32)
            pick = sb("pick", [P, NT, EXP], F32)
            tot = sb("tot", [P, NT, EXP], F32)
            pos = sb("pos", [P, NT, EXP], F32)
            iota8 = sb("iota8", [P, EXP], F32)
            iotan = sb("iotan", [P, NT], F32)
            valid = sb("valid", [P, NT], F32)
            c1 = sb("c1", [P, 10, NT], F32)
            e8 = sb("e8", [P, 5, EXP], F32)
            trow = sb("trow", [1, 2, n_tab], F32)
            blkrow = sb("blkrow", [1, n_tab], F32)
            cnt_f = sb("cnt_f", [1, 4], F32)
            ps_x = ps("ps_x", [P, 3, 512])
            ps_l = ps("ps_l", [P, 512 // EXP, EXP])
            ps_c = ps("ps_c", [P, 2, 512])
            s_x = [sem(f"x{c}") for c in range(R)]
            s_ag = [sem(f"ag{c}") for c in range(2)]
            s_w, s_const, s_zero, s_fill, s_sum, s_chain, s_stat, s_var, s_std, s_agu, s_xtn = (
                sem(n) for n in ("w", "const", "zero", "fill", "sum", "chain", "stat", "var", "std", "agu", "xtn"))
            s_xg, s_t, s_xT, s_l, s_lg, s_pick, s_cnt, s_slot, s_sc, s_pp, s_pa, s_pv, s_soft, s_exp, s_in = (
                sem(n) for n in ("xg", "t", "xT", "l", "lg", "pick", "cnt", "slot", "sc", "pp", "pa", "pv", "soft", "exp", "in"))

            pslot = lambda k: k % 2 if k < R - 1 else 2
            block = ctx.enter_context(nc.Block())

            @block.sync
            def _(sp):
                sp.wait_ge(s_zero, 2)
                for c in range(R):
                    rest = N - (NT - 1) * P
                    if first and c == R - 1:
                        sp.dma_start(xs[:, c * R:NT - 1, :], src[c * R * P:(NT - 1) * P, :].rearrange("(t p) d -> p t d", p=P)).then_inc(s_x[c], 16)
                        sp.dma_start(xs[0:rest, NT - 1, :], src[(NT - 1) * P:N, :]).then_inc(s_x[c], 16)
                    else:
                        sp.dma_start(xs[:, c * R:(c + 1) * R, :],
                                     src[c * R * P:(c + 1) * R * P, :].rearrange("(t p) d -> p t d", p=P)).then_inc(s_x[c], 16)
                    if c >= 2:
                        sp.wait_ge(s_agu, c - 1)
                    sp.dma_start(ag[:, c % 2, :, :], dr["agg"][c * R * P:(c + 1) * R * P, :].rearrange("(t p) d -> p t d", p=P)).then_inc(s_ag[c % 2], 16)
                    if c == 0:
                        sp.dma_start(bias[:, :], io["L0_gnn_bias" if first else "L1_gnn_bias"].partition_broadcast(P)).then_inc(s_w, 16)
                        sp.dma_start(wr[:, :, :], io[names["wr"]].rearrange("(c p) e -> p c e", p=P)).then_inc(s_w, 16)
                        sp.dma_start(br[:, :], io[names["br"]].partition_broadcast(P)).then_inc(s_w, 16)
                for r0 in range(0, n_slot, 8 * P):
                    n = min(8, (n_slot - r0) // P)
                    sp.dma_start(xb[r0:r0 + n * P, :].rearrange("(p j) d -> p (j d)", p=P), zero[:, 0:n * D]).then_inc(s_fill, 16)
                least = -(-top * N // TB) * TB
                for r0 in range(least, n_slot + 2 * P, 8 * P):
                    n = min(8, (n_slot + 2 * P - r0) // P)
                    sp.dma_start(yb[r0:r0 + n * P, :].rearrange("(p j) d -> p (j d)", p=P), zero[:, 0:n * D]).then_inc(s_fill, 16)
                sp.wait_ge(s_fill, 16 * (-(-n_slot // (8 * P)) - (-(n_slot + 2 * P - least) // (8 * P))))
                sp.sem_inc(s_in, 1)

            @block.gpsimd
            def _(pool):
                nc.gpsimd.memset(ident[:, :], 0.0).then_inc(s_const, 1)
                nc.gpsimd.memset(upper[:, :], 1.0).then_inc(s_const, 1)
                nc.gpsimd.memset(allone[:, :], 1.0).then_inc(s_const, 1)
                pool.wait_ge(s_const, 3)
                nc.gpsimd.affine_select(out=ident[:, :], in_=ident[:, :], compare_op=ALU.not_equal, fill=1.0, base=0,
                                        pattern=[[-1, P]], channel_multiplier=1).then_inc(s_const, 1)
                nc.gpsimd.affine_select(out=upper[:, :], in_=upper[:, :], compare_op=ALU.is_ge, fill=0.0, base=-1,
                                        pattern=[[1, P]], channel_multiplier=-1).then_inc(s_const, 1)
                nc.gpsimd.iota(iota8[:, :], pattern=[[1, EXP]], base=0, channel_multiplier=0,
                               allow_small_or_imprecise_dtypes=True).then_inc(s_const, 1)
                nc.gpsimd.iota(iotan[:, :], pattern=[[P, NT]], base=0, channel_multiplier=1,
                               allow_small_or_imprecise_dtypes=True).then_inc(s_const, 1)
                nc.gpsimd.iota(blkrow[:, :], pattern=[[1, n_tab]], base=0, channel_multiplier=0,
                               allow_small_or_imprecise_dtypes=True).then_inc(s_const, 1)
                pool.wait_ge(s_in, 1)
                pool.wait_ge(s_slot, 1)
                for t in range(NT):
                    for c in range(top):
                        pool.indirect_dma_start(xb[:, :], bass.IndirectOffsetOnAxis(slot_i[:, c, t:t + 1], 0),
                                                xt[:, t, :], None).then_inc(s_sc, 16)
                pool.wait_ge(s_sc, 16 * NT * top)

            @block.tensor
            def _(pe):
                pe.wait_ge(s_const, 8)
                pe.wait_ge(s_w, 48)

                def turn(i, k):
                    hold(pe, s_xg, i * R + (k + 1), s_pp)
                    hold(pe, s_xT, i * R + (k + 1), s_pp)
                    for c in range(DC):
                        mm = nc.tensor.transpose(ps_x[:, pslot(k), c * P:(c + 1) * P], xg[:, k, c * P:(c + 1) * P], ident[:, :])
                    mm.then_inc(s_t, 1)

                def logits(i, k):
                    hold(pe, s_xT, i * R + (k + 3), s_pp)
                    for c in range(DC):
                        mm = nc.tensor.matmul(ps_l[:, bass.ds(i * R + k, 1), :], xT[:, k, c, :], wr[:, c, :], start=(c == 0), stop=(c == DC - 1))
                    mm.then_inc(s_l, 1)

                with pe.Fori(0, NT // R) as i:
                    turn(i, 0)
                    turn(i, 1)
                    for k in range(R):
                        if k + 2 < R:
                            turn(i, k + 2)
                        logits(i, k)
                pe.wait_ge(s_pick, 1)
                picks = pick[:, :, :].rearrange("p t e -> p (t e)")
                nc.tensor.matmul(ps_c[:, 0, 0:NT * EXP], upper[:, :], picks, start=True, stop=True)
                nc.tensor.matmul(ps_c[:, 1, 0:NT * EXP], allone[:, :], picks, start=True, stop=True).then_inc(s_cnt, 1)

            @block.scalar
            def _(act):
                act.wait_ge(s_var, 1)
                nc.scalar.activation(lnv[:, 3, :], lnv[:, 1, :], ACT.Sqrt, bias=eps[:, 0:1]).then_inc(s_std, 1)
                if first:
                    act.wait_ge(s_var, 2)
                    nc.scalar.activation(lnv[:, 3, :], lnv[:, 1, :], ACT.Sqrt, bias=eps[:, 0:1]).then_inc(s_std, 1)
                act.sem_inc(s_xT, 2)
                with act.Fori(0, NT // R) as i:
                    for k in range(R):
                        hold(act, s_t, i * R + (k + R + 1), s_pa)
                        nc.scalar.copy(xT[:, k, :, :], ps_x[:, pslot(k), 0:D].rearrange("p (c n) -> p c n", c=DC)).then_inc(s_xT, 1)
                act.wait_ge(s_soft, 1)
                nc.scalar.activation(pr[:, :, :], tmp[:, :, :], ACT.Exp).then_inc(s_exp, 1)

            @block.vector
            def _(v):
                steps = [0]

                def done(ins):
                    steps[0] += 1
                    ins.then_inc(s_chain, 1)
                    v.wait_ge(s_chain, steps[0])

                def tt(o, a, b, op):
                    done(nc.vector.tensor_tensor(o, a, b, op))

                def ts(o, a, s1, s2, *ops):
                    done(nc.vector.tensor_scalar(o, a, s1, s2, *ops))

                nc.vector.memset(zero[:, :], 0.0).then_inc(s_zero, 1)
                nc.vector.memset(xs[:, NT - 1, :], 0.0).then_inc(s_zero, 1)
                done(nc.vector.memset(eps[:, :], EPS))
                v.wait_ge(s_const, 8)
                v.wait_ge(s_w, 48)
                v.wait_ge(s_zero, 2)
                for c in range(R):
                    v.wait_ge(s_x[c], 32 if first and c == R - 1 else 16)
                    v.wait_ge(s_ag[c % 2], 16 * (c // 2 + 1))
                    rows = xs[:, c * R:(c + 1) * R, :]
                    tt(ag[:, c % 2, :, :], ag[:, c % 2, :, :], bias[:, :].unsqueeze(1).to_broadcast([P, R, D]), ALU.add)
                    tt(rows, rows, ag[:, c % 2, :, :], ALU.add)
                    v.sem_inc(s_agu, 1)
                    for t in range(c * R, (c + 1) * R):
                        nc.vector.bn_stats(st[:, t, :], xs[:, t, :]).then_inc(s_stat, 1)

                def stats(t0, count):
                    v.wait_ge(s_stat, count)
                    m, var, d = lnv[:, 0, :], lnv[:, 1, :], lnv[:, 2, :]
                    tt(m, st[:, :, 1], st[:, :, 4], ALU.add)
                    ts(m, m, 0.5, None, ALU.mult)
                    tt(d, st[:, :, 1], st[:, :, 4], ALU.subtract)
                    done(nc.vector.scalar_tensor_tensor(d, d, 0.25, d, ALU.mult, ALU.mult))
                    tt(var, st[:, :, 2], st[:, :, 5], ALU.add)
                    done(nc.vector.scalar_tensor_tensor(var, var, 1.0 / D, d, ALU.mult, ALU.add))
                    v.sem_inc(s_var, 1)
                    v.wait_ge(s_std, t0)
                    done(nc.vector.reciprocal(lnv[:, 4, :], lnv[:, 3, :]))

                stats(1, NT)
                with v.Fori(0, NT // R) as i:
                    for k in range(R):
                        t = i * R + k
                        nc.vector.tensor_scalar(xt[:, bass.ds(t, 1), :], xs[:, bass.ds(t, 1), :], lnv[:, 0, bass.ds(t, 1)],
                                                lnv[:, 4, bass.ds(t, 1)], ALU.subtract, ALU.mult).then_inc(s_xtn, 1)
                v.wait_ge(s_xtn, NT)
                if first:
                    with v.Fori(0, NT // R) as i:
                        for k in range(R):
                            t = i * R + k
                            nc.vector.bn_stats(st[:, bass.ds(t, 1), :], xt[:, bass.ds(t, 1), :]).then_inc(s_stat, 1)
                    stats(2, 2 * NT)
                v.sem_inc(s_t, R)
                with v.Fori(0, NT // R) as i:
                    for k in range(R):
                        hold(v, s_t, i * R + (k + 1), s_pv)
                        nc.vector.tensor_copy(xg[:, k, :], xt[:, bass.ds(i * R + k, 1), :]).then_inc(s_xg, 1)
                    if first:
                        hold(v, s_xg, i * R + R, s_pv)
                        for k in range(R):
                            t = i * R + k
                            nc.vector.tensor_scalar(xt[:, bass.ds(t, 1), :], xt[:, bass.ds(t, 1), :], lnv[:, 0, bass.ds(t, 1)],
                                                    lnv[:, 4, bass.ds(t, 1)], ALU.subtract, ALU.mult).then_inc(s_xtn, 1)
                v.wait_ge(s_l, NT)
                tt(lg[:, :, :], ps_l[:, 0:NT, :], br[:, :].unsqueeze(1).to_broadcast([P, NT, EXP]), ALU.add)
                v.wait_ge(s_xtn, NT * (2 if first else 1))
                wide = lambda col: col.unsqueeze(2).to_broadcast([P, NT, EXP])
                each = lambda row: row.unsqueeze(1).to_broadcast([P, NT, EXP])

                def red(o, i, op):
                    done(nc.vector.tensor_reduce(o, i, AX_X, op))

                red(c1[:, 0, :], lg[:, :, :], ALU.max)
                tt(tmp[:, :, :], lg[:, :, :], wide(c1[:, 0, :]), ALU.subtract)
                v.sem_inc(s_soft, 1)
                v.wait_ge(s_exp, 1)
                red(c1[:, 1, :], pr[:, :, :], ALU.add)
                done(nc.vector.reciprocal(c1[:, 2, :], c1[:, 1, :]))
                tt(pr[:, :, :], pr[:, :, :], wide(c1[:, 2, :]), ALU.mult)
                ts(valid[:, :], iotan[:, :], float(N), None, ALU.is_lt)
                for c in range(top):
                    red(c1[:, 3 + c, :], pr[:, :, :], ALU.max)
                    tt(tmp[:, :, :], pr[:, :, :], wide(c1[:, 3 + c, :]), ALU.is_equal)
                    done(nc.vector.scalar_tensor_tensor(tmp[:, :, :], tmp[:, :, :], -float(EXP), each(iota8[:, :]), ALU.mult, ALU.add))
                    red(c1[:, 5, :], tmp[:, :, :], ALU.min)
                    tt(oh[:, c, :, :], tmp[:, :, :], wide(c1[:, 5, :]), ALU.is_equal)
                    if c + 1 < top:
                        done(nc.vector.scalar_tensor_tensor(pr[:, :, :], oh[:, c, :, :], -2.0, pr[:, :, :], ALU.mult, ALU.add))
                if first:
                    tt(c1[:, 5, :], c1[:, 3, :], c1[:, 4, :], ALU.add)
                    done(nc.vector.reciprocal(c1[:, 6, :], c1[:, 5, :]))
                    tt(wgt[:, 0, :], c1[:, 3, :], c1[:, 6, :], ALU.mult)
                    tt(wgt[:, 1, :], c1[:, 4, :], c1[:, 6, :], ALU.mult)
                    tt(pick[:, :, :], oh[:, 0, :, :], oh[:, 1, :, :], ALU.add)
                    tt(pick[:, :, :], pick[:, :, :], wide(valid[:, :]), ALU.mult)
                else:
                    tt(pick[:, :, :], oh[:, 0, :, :], wide(valid[:, :]), ALU.mult)
                v.sem_inc(s_pick, 1)
                v.wait_ge(s_cnt, 1)
                done(nc.vector.tensor_copy(tot[:, :, :], ps_c[:, 1, 0:NT * EXP].rearrange("p (t e) -> p t e", e=EXP)))
                for e in range(EXP):
                    done(nc.vector.tensor_tensor_scan(pos[:, :, e], tot[:, :, e], zero[:, 0:NT], 0.0, ALU.add, ALU.add))
                done(nc.vector.tensor_copy(e8[:, 0, :], pos[:, NT - 1, :]))
                ts(e8[:, 1, :], e8[:, 0, :], 1.0 / TB, 0.5 - 0.5 / TB, ALU.mult, ALU.add)
                ts(e8[:, 1, :], e8[:, 1, :], 8388608.0, None, ALU.add)
                ts(e8[:, 1, :], e8[:, 1, :], -8388608.0, None, ALU.add)
                done(nc.vector.tensor_tensor_scan(e8[:, 2, :], e8[:, 1, :], zero[:, 0:EXP], 0.0, ALU.add, ALU.add))
                tt(e8[:, 3, :], e8[:, 2, :], e8[:, 1, :], ALU.subtract)
                ts(e8[:, 3, :], e8[:, 3, :], float(TB), None, ALU.mult)
                tt(pos[:, :, :], pos[:, :, :], tot[:, :, :], ALU.subtract)
                tt(pos[:, :, :], pos[:, :, :], ps_c[:, 0, 0:NT * EXP].rearrange("p (t e) -> p t e", e=EXP), ALU.add)
                if not first:
                    tt(tmp[:, :, :], pos[:, :, :], oh[:, 0, :, :], ALU.mult)
                    red(c1[:, 5, :], tmp[:, :, :], ALU.add)
                    ts(c1[:, 6, :], c1[:, 5, :], float(CAP), None, ALU.is_lt)
                    tt(wgt[:, 0, :], c1[:, 3, :], c1[:, 6, :], ALU.mult)
                tt(pos[:, :, :], pos[:, :, :], each(e8[:, 3, :]), ALU.add)
                for c in range(top):
                    tt(tmp[:, :, :], pos[:, :, :], oh[:, c, :, :], ALU.mult)
                    red(c1[:, 5, :], tmp[:, :, :], ALU.add)
                    ts(c1[:, 7, :], c1[:, 5, :], -float(n_slot), None, ALU.add)
                    tt(c1[:, 7, :], c1[:, 7, :], valid[:, :], ALU.mult)
                    ts(c1[:, 7, :], c1[:, 7, :], float(n_slot), None, ALU.add)
                    ts(c1[:, 9, :], iotan[:, :], float(c * P), None, ALU.add)
                    ts(c1[:, 8, :], valid[:, :], -1.0, 1.0, ALU.mult, ALU.add)
                    done(nc.vector.scalar_tensor_tensor(c1[:, 8, :], c1[:, 8, :], c1[:, 9, 0:1], c1[:, 7, :], ALU.mult, ALU.add))
                    done(nc.vector.tensor_copy(slot_i[:, c, :], c1[:, 8, :]))
                v.sem_inc(s_slot, 1)
                done(nc.vector.memset(trow[:, 0, :], 0.0))
                for e in range(EXP - 1):
                    done(nc.vector.scalar_tensor_tensor(trow[:, 0, :], blkrow[:, :], e8[0:1, 2, e:e + 1], trow[:, 0, :], ALU.is_ge, ALU.add))
                done(nc.vector.tensor_copy(tab_i[:, :], trow[:, 0, :]))
                done(nc.vector.tensor_copy(cnt_f[:, :], e8[0:1, 2, EXP - 1:EXP].to_broadcast([1, 4])))
                ts(cnt_f[:, :], cnt_f[:, :], 0.5, 0.25, ALU.mult, ALU.add)
                ts(cnt_f[:, :], cnt_f[:, :], 8388608.0, None, ALU.add)
                ts(cnt_f[:, :], cnt_f[:, :], -8388608.0, None, ALU.add)
                done(nc.vector.tensor_copy(cnt_i[:, :], cnt_f[:, :]))

        with ExitStack() as ctx:
            sb = lambda n, s, d: ctx.enter_context(nc.sbuf_tensor(f"x{layer}_" + n, s, d))
            ps = lambda n, s: ctx.enter_context(nc.psum_tensor(f"x{layer}_" + n, s, F32))
            sem = semaphores(nc, ctx, f"x{layer}_")
            ident = sb("ident", [P, P], F32)
            xin = sb("xin", [P, 2, SUB, D], F32)
            w1 = sb("w1", [P, 2, DC, FF], F32)
            w2 = sb("w2", [P, 2, FC, D], F32)
            b1 = sb("b1", [P, 2, FC], F32)
            b2 = sb("b2", [P, 2, D], F32)
            lng = sb("lng", [P, 2, DC], F32)
            lnb = sb("lnb", [P, 2, DC], F32)
            xT = sb("xT", [P, 2, DC, TB], F32)
            hT = sb("hT", [P, 2, FC, TB], F32)
            y = sb("y", [P, 2, SUB, D], F32)
            ps_x = ps("ps_x", [P, DC, TB])
            ps_h = ps("ps_h", [P, 4, 512])
            ps_y = ps("ps_y", [P, SUB, 512])
            s_const, s_t, s_xT, s_h, s_act, s_y, s_yc, s_pp, s_pa, s_pv, s_ps = (
                sem(n) for n in ("const", "t", "xT", "h", "act", "y", "yc", "pp", "pa", "pv", "ps"))
            s_ldx = [sem(f"ldx{k}") for k in range(2)]
            s_ldw = [sem(f"ldw{k}") for k in range(2)]
            s_out = [sem(f"out{k}") for k in range(2)]
            n_ldx = 16 * (3 if first else 1)
            n_ldw = 16 * 4

            block = ctx.enter_context(nc.Block())

            @block.sync
            def _(sp):
                def load(b, k):
                    e = sp.value_load(tab_i[0:1, bass.ds(b, 1)], min_val=0, max_val=EXP - 1)
                    one = lambda name: io[name][bass.ds(e, 1)]
                    sp.dma_start(xin[:, k, :, :], xb[bass.ds(b * TB, TB), :].rearrange("(s p) d -> p s d", p=P)).then_inc(s_ldx[k], 16)
                    if first:
                        sp.dma_start(lng[:, k, :], one("L0_ffn_ln_g").rearrange("a (p c) -> (a p) c", c=DC)).then_inc(s_ldx[k], 16)
                        sp.dma_start(lnb[:, k, :], one("L0_ffn_ln_b").rearrange("a (p c) -> (a p) c", c=DC)).then_inc(s_ldx[k], 16)
                    sp.dma_start(w1[:, k, :, :], one(names["w1"]).rearrange("a (p c) f -> (a p) c f", c=DC)).then_inc(s_ldw[k], 16)
                    sp.dma_start(w2[:, k, :, :], one(names["w2"]).rearrange("a (p j) d -> (a p) j d", j=FC)).then_inc(s_ldw[k], 16)
                    sp.dma_start(b1[:, k, :], one(names["b1"]).rearrange("a (p j) -> (a p) j", j=FC)).then_inc(s_ldw[k], 16)
                    sp.dma_start(b2[:, k, :], one(names["b2"]).rearrange("a d -> (a d)").partition_broadcast(P)).then_inc(s_ldw[k], 16)

                for k in range(2):
                    load(k, k)
                    sp.sem_inc(s_out[k], 16)
                pairs = sp.value_load(cnt_i[0:1, 0:1], min_val=1, max_val=(nblk_max + 1) // 2)
                with sp.Fori(0, pairs) as i:
                    for k in range(2):
                        hold(sp, s_yc, i * 2 + (k + 2), s_ps)
                        load(i * 2 + (k + 2), k)
                        sp.dma_start(yb[bass.ds(i * (2 * TB) + k * TB, TB), :].rearrange("(s p) d -> p s d", p=P),
                                     y[:, k, :, :]).then_inc(s_out[k], 16)
                for k in range(2):
                    hold(sp, s_out[k], pairs * 16 + 16, s_ps)
                    hold(sp, s_ldx[k], pairs * n_ldx + n_ldx, s_ps)
                    hold(sp, s_ldw[k], pairs * n_ldw + n_ldw, s_ps)

            @block.gpsimd
            def _(pool):
                nc.gpsimd.memset(ident[:, :], 0.0).then_inc(s_const, 1)
                pool.wait_ge(s_const, 1)
                nc.gpsimd.affine_select(out=ident[:, :], in_=ident[:, :], compare_op=ALU.not_equal, fill=1.0, base=0,
                                        pattern=[[-1, P]], channel_multiplier=1).then_inc(s_const, 1)

            @block.tensor
            def _(pe):
                pe.wait_ge(s_const, 2)

                def turn(k):
                    for c in range(DC):
                        for s in range(SUB):
                            mm = nc.tensor.transpose(ps_x[:, c, s * P:(s + 1) * P],
                                                     xin[:, k, s, :].rearrange("p (m c) -> p c m", c=DC)[:, c, :], ident[:, :])
                    mm.then_inc(s_t, 1)

                pe.wait_ge(s_ldx[0], n_ldx)
                turn(0)
                pairs = pe.value_load(cnt_i[0:1, 0:1], min_val=1, max_val=(nblk_max + 1) // 2)
                with pe.Fori(0, pairs) as i:
                    for k in range(2):
                        hold(pe, s_ldw[k], i * n_ldw + n_ldw, s_pp)
                        hold(pe, s_xT, i * 2 + (k + 1), s_pp)
                        for j in range(FC):
                            hold(pe, s_act, i * (2 * FC) + (k * FC + j + 1), s_pp)
                            for c in range(DC):
                                mm = nc.tensor.matmul(ps_h[:, j % 4, 0:TB],
                                                      w1[:, k, c, :].rearrange("p (m j) -> p j m", j=FC)[:, j, :],
                                                      xT[:, k, c, :], start=(c == 0), stop=(c == DC - 1))
                            mm.then_inc(s_h, 1)
                        hold(pe, s_ldx[1 - k], (i + k) * n_ldx + n_ldx, s_pp)
                        turn(1 - k)
                        hold(pe, s_yc, i * 2 + (k + 1), s_pp)
                        for j in range(FC):
                            hold(pe, s_act, i * (2 * FC) + (k * FC + j + 5), s_pp)
                            for s in range(SUB):
                                mm = nc.tensor.matmul(ps_y[:, s, 0:D], hT[:, k, j, s * P:(s + 1) * P], w2[:, k, j, :],
                                                      start=(j == 0), stop=(j == FC - 1))
                        mm.then_inc(s_y, 1)

            @block.scalar
            def _(act):
                act.sem_inc(s_act, 4)
                pairs = act.value_load(cnt_i[0:1, 0:1], min_val=1, max_val=(nblk_max + 1) // 2)
                with act.Fori(0, pairs) as i:
                    for k in range(2):
                        for j in range(FC):
                            hold(act, s_h, i * (2 * FC) + (k * FC + j + 1), s_pa)
                            nc.scalar.activation(hT[:, k, j, :], ps_h[:, j % 4, 0:TB], ACT.Gelu if first else ACT.Relu,
                                                 bias=b1[:, k, j:j + 1]).then_inc(s_act, 1)

            @block.vector
            def _(v):
                def affine(k):
                    for c in range(DC):
                        if first:
                            ins = nc.vector.tensor_scalar(xT[:, k, c, :], ps_x[:, c, :], lng[:, k, c:c + 1], lnb[:, k, c:c + 1],
                                                          ALU.mult, ALU.add)
                        else:
                            ins = nc.vector.tensor_copy(xT[:, k, c, :], ps_x[:, c, :])
                    ins.then_inc(s_xT, 1)

                v.sem_inc(s_yc, 1)
                v.wait_ge(s_t, 1)
                affine(0)
                pairs = v.value_load(cnt_i[0:1, 0:1], min_val=1, max_val=(nblk_max + 1) // 2)
                with v.Fori(0, pairs) as i:
                    for k in range(2):
                        hold(v, s_t, i * 2 + (k + 2), s_pv)
                        affine(1 - k)
                        hold(v, s_y, i * 2 + (k + 1), s_pv)
                        hold(v, s_out[k], i * 16 + 16, s_pv)
                        for s in range(SUB):
                            ins = nc.vector.tensor_tensor(y[:, k, s, :], ps_y[:, s, 0:D], b2[:, k, :], ALU.add)
                        ins.then_inc(s_yc, 1)

        with ExitStack() as ctx:
            sb = lambda n, s, d: ctx.enter_context(nc.sbuf_tensor(f"c{layer}_" + n, s, d))
            sem = semaphores(nc, ctx, f"c{layer}_")
            g = sb("g", [P, R, 2, D], F32)
            zero = sb("zero", [P, 3, D], F32)
            flag = sb("flag", [P, 3, R, D], I32)
            part = sb("part", [P, R, D], F32)
            s_g = [sem(f"g{k}") for k in range(R)]
            s_one, s_res, s_out, s_pv, s_ps, s_z, s_fl = (sem(n) for n in ("one", "res", "out", "pv", "ps", "z", "fl"))

            block = ctx.enter_context(nc.Block())

            @block.gpsimd
            def _(pool):
                for t in range(NT):
                    if t >= R:
                        pool.wait_ge(s_res if first else s_one, t - R + 1)
                    for c in range(top):
                        pool.indirect_dma_start(g[:, t % R, c, :], None, yb[0:n_slot + 2 * P, :],
                                                bass.IndirectOffsetOnAxis(slot_i[:, c, t:t + 1], 0)).then_inc(s_g[t % R], 16)

            @block.vector
            def _(v):
                for n, value in enumerate((0.0, 10000.0, -10000.0)):
                    nc.vector.memset(zero[:, n, :], value).then_inc(s_z, 1)
                v.wait_ge(s_z, 3)
                with v.Fori(0, NT // R) as i:
                    for k in range(R):
                        t = i * R + k
                        row = xs[:, bass.ds(t, 1), :]
                        hold(v, s_g[k], i * (16 * top) + 16 * top, s_pv)
                        if first:
                            nc.vector.scalar_tensor_tensor(g[:, k, 0:1, :], g[:, k, 0:1, :], wgt[:, 0, bass.ds(t, 1)], row,
                                                           ALU.mult, ALU.add).then_inc(s_one, 1)
                            hold(v, s_one, t + 1, s_pv)
                            nc.vector.scalar_tensor_tensor(row, g[:, k, 1:2, :], wgt[:, 1, bass.ds(t, 1)], g[:, k, 0:1, :],
                                                           ALU.mult, ALU.add).then_inc(s_res, 1)
                        else:
                            nc.vector.tensor_scalar(part[:, k, :], g[:, k, 0, :], wgt[:, 0, bass.ds(t, 1)], None,
                                                    ALU.mult).then_inc(s_one, 1)
                    if not first:
                        hold(v, s_one, i * R + R, s_pv)
                        nc.vector.tensor_tensor(flag[:, 0, :, :], part[:, :, :], part[:, :, :], ALU.not_equal)
                        nc.vector.tensor_scalar(flag[:, 1, :, :], part[:, :, :], FMAX, None, ALU.is_gt)
                        nc.vector.tensor_scalar(flag[:, 2, :, :], part[:, :, :], -FMAX, None, ALU.is_lt).then_inc(s_fl, 1)
                        for n in range(3):
                            hold(v, s_fl, i * 4 + (n + 1), s_pv)
                            nc.vector.copy_predicated(part[:, :, :], flag[:, n, :, :],
                                                      zero[:, n, :].unsqueeze(1).to_broadcast([P, R, D])).then_inc(s_fl, 1)
                        hold(v, s_fl, i * 4 + 4, s_pv)
                        rows = xs[:, bass.ds(i * R, R), :]
                        nc.vector.tensor_tensor(rows, rows, part[:, :, :], ALU.add).then_inc(s_res, R)
                        hold(v, s_res, i * R + R, s_pv)

            @block.sync
            def _(sp):
                rest = N - (NT - 1) * P
                for c in range(R):
                    sp.wait_ge(s_res, (c + 1) * R)
                    n = R if first or c < R - 1 else R - 1
                    sp.dma_start(out[c * R * P:(c * R + n) * P, :].rearrange("(t p) d -> p t d", p=P),
                                 xs[:, c * R:c * R + n, :]).then_inc(s_out, 16)
                if not first:
                    sp.dma_start(out[(NT - 1) * P:N, :], xs[0:rest, NT - 1, :]).then_inc(s_out, 16)
                sp.wait_ge(s_out, 16 * R + (0 if first else 16))


def scratch(nc):
    dr = {}
    for name, shape, dt in (("pmax", [P, EC], F32), ("smin", [P, EC], F32), ("win", [WT * P, 2], F32), ("nblk", [1, 4], I32),
                            ("dstp", [EP], I32), ("srcp", [EP], I32), ("attrp", [K_ENC, EP], BF16),
                            ("blk", [MAXB, 2], I32), ("blkf", [MAXB, 1], F32),
                            ("table", [NP, ROW], F32), ("wcol", [NP, 2 * HEADS], F32), ("hT", [D, NP], F32),
                            ("agg", [NP, D], F32), ("x2", [NP, D], F32),
                            ("xb", [(max_blocks(2) + 4) * TB + 2 * P, D], F32), ("yb", [(max_blocks(2) + 4) * TB + 2 * P, D], F32)):
        dr[name] = nc.dram_tensor("sc_" + name, shape, dt).ap()
    return dr


def build(nc, io, out):
    dr = scratch(nc)
    plan_phase(nc, io, dr)
    node_phase(nc, io, dr, 0)
    edge_phase(nc, io, dr, 0)
    ffn_phases(nc, io, dr, 0, io["x"], dr["x2"])
    node_phase(nc, io, dr, 1)
    edge_phase(nc, io, dr, 1)
    ffn_phases(nc, io, dr, 1, dr["x2"], out)


_INS = ["x", "src", "dst", "edge_attr_3", "L0_gnn_W", "L0_gnn_a_src", "L0_gnn_a_dst", "L0_gnn_edge_W", "L0_gnn_edge_b",
        "L0_gnn_bias", "L0_ffn_Wr", "L0_ffn_br", "L0_ffn_ln_g", "L0_ffn_ln_b", "L0_ffn_W1", "L0_ffn_b1", "L0_ffn_W2",
        "L0_ffn_b2", "L1_gnn_W", "L1_gnn_attn_l", "L1_gnn_attn_r", "L1_gnn_bias", "L1_ffn_gate_w", "L1_ffn_gate_b",
        "L1_ffn_w1", "L1_ffn_b1", "L1_ffn_w2", "L1_ffn_b2"]


def kernel(**inputs):
    import concourse.bacc as _bacc
    from concourse.bass_utils import run_bass_kernel_spmd as _run

    nc = _bacc.Bacc("TRN2", target_bir_lowering=False, num_devices=1)
    arrays, io = {}, {}
    for name in _INS:
        a = np.ascontiguousarray(inputs[name])
        arrays[f"in_{name}_dram"] = a
        io[name] = nc.dram_tensor(f"in_{name}_dram", a.shape, mybir.dt.from_np(a.dtype), kind="ExternalInput").ap()
    out = nc.dram_tensor("out_0_dram", (N, D), F32, kind="ExternalOutput").ap()
    build(nc, io, out)
    r = _run(nc, [arrays], core_ids=[0])
    return r.results[0]["out_0_dram"]
```
